# Optimizing a Trainium2 kernel written in Bass

```python
import numpy as np
import jax
import jax.numpy as jnp

def _softmax(x, axis=-1):
    return jax.nn.softmax(x, axis=axis)

def _gelu(x):
    return jax.nn.gelu(x, approximate=True)

def _silu(x):
    return jax.nn.silu(x)

def _sigmoid(x):
    return jax.nn.sigmoid(x)

def _layernorm(x, axis=-1, eps=1e-05):
    m = jnp.mean(x, axis=axis, keepdims=True)
    v = jnp.var(x, axis=axis, keepdims=True)
    return (x - m) / jnp.sqrt(v + eps)

def _scatter_add(tgt, idx, src, axis=0):
    return tgt.at[idx].add(src)

def _segment_sum(src, seg, n):
    return jax.ops.segment_sum(src, seg, n)
kernel_name = 'mk_gnn_ffn_d2_gnn_r16_f707b8'

def setup_inputs(seed: int=0):
    np.random.seed(seed)
    _w = jnp.asarray

    def _rec_inputs():
        import jax
        import jax.numpy as jnp
        _gk = jax.random.key(seed)
        x = -0.0003713 + 1 * jax.random.normal(jax.random.fold_in(_gk, 1), (3125, 256), jnp.float32)
        src = jax.random.randint(jax.random.fold_in(_gk, 2), (100000,), 0, 3125, jnp.int32)
        dst = jnp.minimum((3125 * jax.random.uniform(jax.random.fold_in(_gk, 3), (100000,)) ** 2.0).astype(jnp.int32), 49999)
        _o = jnp.argsort(dst, stable=True)
        src = src[_o]
        dst = dst[_o]
        edge_attr_64 = 0.000189758 + 1.00013 * jax.random.normal(jax.random.fold_in(_gk, 11), (100000, 64), jnp.float32)
        return (x, src, dst, edge_attr_64)
    x, src, dst, edge_attr_64 = _rec_inputs()

    def _L0_gnn_setup():
        import jax, jax.numpy as jnp
        import numpy as np
        N_NODES = 3125
        N_EDGES = 50000
        NODE_DIM = 256
        EDGE_DIM = 64
        HIDDEN = 512
        OUT_DIM = 256
        key = jax.random.key(seed)
        ks = jax.random.split(key, 6)
        node_features = jax.random.normal(ks[0], (N_NODES, NODE_DIM), dtype=jnp.float32)
        edge_index = jax.random.randint(ks[1], (2, N_EDGES), 0, N_NODES, dtype=jnp.int64)
        edge_features = jax.random.normal(ks[2], (N_EDGES, EDGE_DIM), dtype=jnp.float32)
        in_dim = EDGE_DIM + NODE_DIM
        W1 = jax.random.normal(ks[3], (in_dim, HIDDEN), dtype=jnp.float32) * (1.0 / np.sqrt(in_dim))
        b1 = jnp.zeros((HIDDEN,), dtype=jnp.float32)
        W2 = jax.random.normal(ks[4], (HIDDEN, OUT_DIM), dtype=jnp.float32) * (1.0 / np.sqrt(HIDDEN))
        b2 = jnp.zeros((OUT_DIM,), dtype=jnp.float32)
        return {'node_features': node_features, 'edge_index': edge_index, 'edge_features': edge_features, 'W1': W1, 'b1': b1, 'W2': W2, 'b2': b2}
    _L0_gnn_all = _L0_gnn_setup()
    _L0_gnn_in = {k: v for k, v in _L0_gnn_all.items() if k in ('W1', 'b1', 'W2', 'b2')}
    del _L0_gnn_all

    def _L0_ffn_setup():
        import jax, jax.numpy as jnp
        import numpy as np
        D_MODEL = 256
        N_EXPERTS = 16
        HIDDEN = 512
        SCALE = 0.02
        key = jax.random.key(seed)
        ks = jax.random.split(key, 5)
        x = jax.random.normal(ks[0], (4, 512, D_MODEL), dtype=jnp.float32)
        gate_w = jax.random.normal(ks[1], (D_MODEL, N_EXPERTS), dtype=jnp.float32) * SCALE
        gate_b = jnp.zeros((N_EXPERTS,), dtype=jnp.float32)
        w1 = jax.random.normal(ks[2], (N_EXPERTS, D_MODEL, HIDDEN), dtype=jnp.float32) * SCALE
        w2 = jax.random.normal(ks[3], (N_EXPERTS, D_MODEL, HIDDEN), dtype=jnp.float32) * SCALE
        w3 = jax.random.normal(ks[4], (N_EXPERTS, HIDDEN, D_MODEL), dtype=jnp.float32) * SCALE
        return {'x': x, 'gate_w': gate_w, 'gate_b': gate_b, 'w1': w1, 'w2': w2, 'w3': w3}
    _L0_ffn_all = _L0_ffn_setup()
    _L0_ffn_in = {k: v for k, v in _L0_ffn_all.items() if k in ('gate_w', 'gate_b', 'w1', 'w2', 'w3')}
    del _L0_ffn_all

    def _L1_gnn_setup():
        import jax, jax.numpy as jnp
        import numpy as np
        N_NODES = 3125
        N_EDGES = 50000
        IN_SIZE = 256
        OUT_SIZE = 256
        key = jax.random.key(seed)
        kx, ks, kd, kw, kb = jax.random.split(key, 5)
        x = jax.random.normal(kx, (N_NODES, IN_SIZE), dtype=jnp.float32)
        src_rand = jax.random.randint(ks, (N_EDGES - N_NODES,), 0, N_NODES)
        src = jnp.concatenate([jnp.arange(N_NODES), src_rand]).astype(jnp.int64)
        dst = jax.random.randint(kd, (N_EDGES,), 0, N_NODES).astype(jnp.int64)
        edge_index = jnp.stack([src, dst])
        bound = 1.0 / np.sqrt(IN_SIZE)
        W = jax.random.uniform(kw, (OUT_SIZE, IN_SIZE), dtype=jnp.float32, minval=-bound, maxval=bound)
        b = jax.random.uniform(kb, (OUT_SIZE,), dtype=jnp.float32, minval=-bound, maxval=bound)
        return {'x': x, 'edge_index': edge_index, 'W': W, 'b': b}
    _L1_gnn_all = _L1_gnn_setup()
    _L1_gnn_in = {k: v for k, v in _L1_gnn_all.items() if k in ('W', 'b')}
    del _L1_gnn_all

    def _L1_ffn_setup():
        import jax, jax.numpy as jnp
        import numpy as np
        B, S, D = (8, 256, 256)
        H = 4 * D
        CAPACITY = 0.5
        key = jax.random.key(seed)
        ks = jax.random.split(key, 6)
        x = jax.random.normal(ks[0], (B, S, D), dtype=jnp.float32)
        attention_mask = jnp.zeros((B, 1, 1, S), dtype=jnp.float32)
        wr = jax.random.normal(ks[1], (D, 1), dtype=jnp.float32) * 0.02
        br = jnp.zeros((1,), dtype=jnp.float32)
        w1 = jax.random.normal(ks[2], (D, H), dtype=jnp.float32) * 0.02
        b1 = jnp.zeros((H,), dtype=jnp.float32)
        w2 = jax.random.normal(ks[3], (H, D), dtype=jnp.float32) * 0.02
        b2 = jnp.zeros((D,), dtype=jnp.float32)
        return {'x': x, 'attention_mask': attention_mask, 'wr': wr, 'br': br, 'w1': w1, 'b1': b1, 'w2': w2, 'b2': b2}
    _L1_ffn_all = _L1_ffn_setup()
    _L1_ffn_in = {k: v for k, v in _L1_ffn_all.items() if k in ('attention_mask', 'wr', 'br', 'w1', 'b1', 'w2', 'b2')}
    del _L1_ffn_all
    return {'x': x, 'src': src, 'dst': dst, 'edge_attr_64': edge_attr_64, 'L0_gnn_W1': _L0_gnn_in['W1'], 'L0_gnn_b1': _L0_gnn_in['b1'], 'L0_gnn_W2': _L0_gnn_in['W2'], 'L0_gnn_b2': _L0_gnn_in['b2'], 'L0_ffn_gate_w': _L0_ffn_in['gate_w'], 'L0_ffn_gate_b': _L0_ffn_in['gate_b'], 'L0_ffn_w1': _L0_ffn_in['w1'], 'L0_ffn_w2': _L0_ffn_in['w2'], 'L0_ffn_w3': _L0_ffn_in['w3'], 'L1_gnn_W': _L1_gnn_in['W'], 'L1_gnn_b': _L1_gnn_in['b'], 'L1_ffn_attention_mask': _L1_ffn_in['attention_mask'], 'L1_ffn_wr': _L1_ffn_in['wr'], 'L1_ffn_br': _L1_ffn_in['br'], 'L1_ffn_w1': _L1_ffn_in['w1'], 'L1_ffn_b1': _L1_ffn_in['b1'], 'L1_ffn_w2': _L1_ffn_in['w2'], 'L1_ffn_b2': _L1_ffn_in['b2']}

def reference(x, src, dst, edge_attr_64, L0_gnn_W1, L0_gnn_b1, L0_gnn_W2, L0_gnn_b2, L0_ffn_gate_w, L0_ffn_gate_b, L0_ffn_w1, L0_ffn_w2, L0_ffn_w3, L1_gnn_W, L1_gnn_b, L1_ffn_attention_mask, L1_ffn_wr, L1_ffn_br, L1_ffn_w1, L1_ffn_b1, L1_ffn_w2, L1_ffn_b2):
    import jax
    import jax.numpy as jnp

    def _L0_gnn_ref(node_features, edge_index, edge_features, W1, b1, W2, b2):
        import jax, jax.numpy as jnp
        import numpy as np
        N_NODES = 3125
        N_EDGES = 50000
        NODE_DIM = 256
        EDGE_DIM = 64
        HIDDEN = 512
        OUT_DIM = 256
        tgt = edge_index[1]
        agg = jax.ops.segment_sum(edge_features, tgt, num_segments=N_NODES)
        counts = jax.ops.segment_sum(jnp.ones((edge_features.shape[0],), edge_features.dtype), tgt, num_segments=N_NODES)
        agg = agg / jnp.maximum(counts, 1.0)[:, None]
        combined = jnp.concatenate([agg, node_features], axis=1)
        h = jax.nn.relu(combined @ W1 + b1)
        out = h @ W2 + b2
        return out

    def _L0_ffn_ref(x, gate_w, gate_b, w1, w2, w3):
        import jax, jax.numpy as jnp
        import numpy as np
        D_MODEL = 256
        N_EXPERTS = 16
        HIDDEN = 512
        SCALE = 0.02
        n_experts = w1.shape[0]
        logits = jnp.einsum('bsd,de->bse', x, gate_w) + gate_b
        probs = jax.nn.softmax(logits, axis=-1)
        top_probs, top_idx = jax.lax.top_k(probs, 2)
        top_probs = top_probs / jnp.sum(top_probs, axis=-1, keepdims=True)
        dispatch = jnp.sum(jax.nn.one_hot(top_idx, n_experts, dtype=x.dtype) * top_probs[..., None], axis=-2)
        h1 = jnp.einsum('bsd,edh->bseh', x, w1)
        h2 = jnp.einsum('bsd,edh->bseh', x, w2)
        hidden = jax.nn.silu(h1) * h2
        expert_out = jnp.einsum('bseh,eho->bseo', hidden, w3)
        return jnp.einsum('bseo,bse->bso', expert_out, dispatch)

    def _L1_gnn_ref(x, edge_index, W, b):
        import jax, jax.numpy as jnp
        import numpy as np
        N_NODES = 3125
        N_EDGES = 50000
        IN_SIZE = 256
        OUT_SIZE = 256
        N = x.shape[0]
        src, dst = (edge_index[0], edge_index[1])
        deg = jnp.zeros((N,), dtype=x.dtype).at[src].add(1.0)
        dinv = deg ** (-0.5)
        loop = jnp.arange(N, dtype=src.dtype)
        src_sl = jnp.concatenate([src, loop])
        dst_sl = jnp.concatenate([dst, loop])
        coef = dinv[src_sl] * dinv[dst_sl]
        msg = x[dst_sl] * coef[:, None]
        agg = jax.ops.segment_sum(msg, src_sl, num_segments=N)
        return jax.nn.relu(agg @ W.T + b)

    def _L1_ffn_ref(x, attention_mask, wr, br, w1, b1, w2, b2):
        import jax, jax.numpy as jnp
        import numpy as np
        B, S, D = (8, 256, 256)
        H = 4 * D
        CAPACITY = 0.5
        b, s, d = x.shape
        weights = (jnp.einsum('bsd,do->bso', x, wr) + br)[..., 0]
        k = max(1, int(CAPACITY * s))
        kk = k - 1 if k > 1 else 1
        _, idx = jax.lax.top_k(weights, k)
        sel_idx = idx[:, :kk]
        sel = jnp.take_along_axis(x, sel_idx[:, :, None], axis=1)
        h = jax.nn.gelu(jnp.einsum('bkd,dh->bkh', sel, w1) + b1)
        y = jnp.einsum('bkh,hd->bkd', h, w2) + b2
        w_sel = jnp.take_along_axis(weights, sel_idx, axis=1)
        y = y * w_sel[..., None]
        batch_idx = jnp.arange(b)[:, None]
        processed = jnp.zeros_like(x).at[batch_idx, sel_idx].set(y)
        return processed + x
    edge_index = jnp.stack([src, dst])
    x = x + _L0_gnn_ref(_layernorm(x, axis=-1), edge_index, edge_attr_64, L0_gnn_W1, L0_gnn_b1, L0_gnn_W2, L0_gnn_b2)
    x = x + _L0_ffn_ref(_layernorm(x, axis=-1)[None], L0_ffn_gate_w, L0_ffn_gate_b, L0_ffn_w1, L0_ffn_w2, L0_ffn_w3)[0]
    x = x + _L1_gnn_ref(_layernorm(x, axis=-1), edge_index, L1_gnn_W, L1_gnn_b)
    x = x + _L1_ffn_ref(_layernorm(x, axis=-1)[None], L1_ffn_attention_mask, L1_ffn_wr, L1_ffn_br, L1_ffn_w1, L1_ffn_b1, L1_ffn_w2, L1_ffn_b2)[0]
    return x

_drawn_inputs = setup_inputs


def setup_inputs(seed=0):
    import zlib

    import numpy as np

    out = dict(_drawn_inputs(seed))
    spreads = {'L0_gnn_b1': (0.0, 0.1),
     'L0_gnn_b2': (0.0, 0.1),
     'L0_ffn_gate_b': (0.0, 0.8),
     'L1_ffn_b1': (0.0, 0.8),
     'L1_ffn_b2': (0.0, 0.8)}
    factors = {'L0_ffn_gate_w': 4.335,
     'L0_ffn_w1': 4.048,
     'L0_ffn_w2': 3.996,
     'L0_ffn_w3': 3.994,
     'L1_ffn_wr': 4.474,
     'L1_ffn_w1': 5.894,
     'L1_ffn_w2': 5.362,
     'L1_gnn_b': 2.804}
    for name, (base, spread) in spreads.items():
        noise = np.random.default_rng([zlib.crc32(name.encode()), seed]).standard_normal(out[name].shape)
        drawn = base * np.exp(spread * noise) if base else spread * noise
        out[name] = jnp.asarray(drawn.astype(out[name].dtype))
    for name, factor in factors.items():
        out[name] = (out[name] * factor).astype(out[name].dtype)
    return out
```

```python
from contextlib import ExitStack

import concourse.bass as bass
from concourse import mybir

ALU = mybir.AluOpType
ACT = mybir.ActivationFunctionType
AX = mybir.AxisListType
F32 = mybir.dt.float32
BF16 = mybir.dt.bfloat16
I32 = mybir.dt.int32
U32 = mybir.dt.uint32


N = 3125
NT = 25
D = 256
NE = 100000
EP, EC = 125, 800
GE = 1024
NG = 98
NQ = NG + NT - 1
LASTROW = (NE - GE) // 8
PADS = NG * GE - NE
RA = 6
NX = 16
HID = 512
NS = 64
NSORT = 131072
SC = 1024
NTILE = 806
ZROW = 3200
YROWS = 3328
KEEP = 1561
LNEPS = 1e-5


class Token:
    def __init__(self, sem, val):
        self.sem, self.val = sem, val


class Queues:

    def __init__(self, sems):
        self.sems = sems
        self.count = {e: 0 for e in sems}
        self.todo = {e: [] for e in ("sp", "act", "pool", "dve", "pe")}
        self.dcount = {}
        self.last = {}

    def put(self, eng, fn, *after, sig=True, chain=None):
        if chain is None:
            chain = eng == "dve"
        after = [a for a in after if a is not None]
        if chain and self.count[eng]:
            after.append(Token(self.sems[eng], self.count[eng]))
        if sig:
            self.count[eng] += 1
        self.todo[eng].append((fn, after, (self.sems[eng], 1) if sig else None))
        return Token(self.sems[eng], self.count[eng])

    def dma(self, eng, sem, fn, *after):
        after = [a for a in after if a is not None]
        self.dcount[sem.name] = self.dcount.get(sem.name, 0) + 16
        self.todo[eng].append((fn, after, (sem, 16)))
        self.last[sem.name] = Token(sem, self.dcount[sem.name])
        return self.last[sem.name]

    def landed(self):
        return list(self.last.values())

    def run(self, eng, e):
        seen = {}
        for fn, after, inc in self.todo[eng]:
            for t in after:
                if seen.get(t.sem.name, 0) < t.val:
                    e.wait_ge(t.sem, t.val)
                    seen[t.sem.name] = t.val
            ins = fn(e)
            if inc:
                ins.then_inc(*inc)


def program(nc, x, src, dst, attr, gW1, gb1, gW2, gb2, gate_w, gate_b, ew1, ew2, ew3,
            cW, cb, amask, wr, br, fw1, fb1, fw2, fb2, out):
    ctx = ExitStack()
    with ctx:
        def sb(name, shape, dt=F32):
            return ctx.enter_context(nc.sbuf_tensor(name, shape, dt))

        def sem(name):
            return ctx.enter_context(nc.semaphore(name))

        PS = [ctx.enter_context(nc.psum_tensor(f"ps{i}", [128, 512], F32)) for i in range(8)]
        q = Queues({e: sem("s_" + e) for e in ("act", "pool", "dve", "pe")})
        put, dma = q.put, q.dma

        def V(fn, *after, **k):
            return put("dve", fn, *after, **k)

        def A(fn, *after, **k):
            return put("act", fn, *after, **k)

        def P(fn, *after, **k):
            return put("pe", fn, *after, **k)

        def G(fn, *after, **k):
            return put("pool", fn, *after, **k)

        X = sb("X", [128, NT, D])
        XB = sb("XB", [128, NT, D])
        ident = sb("ident", [128, 128])
        iof = sb("iof", [128, 128])
        iob = sb("iob", [128, 128], BF16)
        iop = sb("iop", [128, 1])
        tri = sb("tri", [128, 128])
        low = sb("low", [128, 128])
        ones = sb("ones", [128, 128])
        padc = sb("padc", [128, 1])
        w1a = sb("w1a", [64, HID])
        w1b = sb("w1b", [128, 2, HID])
        w2g = sb("w2g", [128, 4, D])
        b1g = sb("b1g", [128, 4])
        b2g = sb("b2g", [1, D])
        gw = sb("gw", [128, 2, NX])
        gb = sb("gb", [1, NX])
        cWn = sb("cWn", [128, 2, D])
        cWT = sb("cWT", [128, 2, D])
        cbr = sb("cbr", [1, D])
        wrr = sb("wrr", [128, D])
        brr = sb("brr", [128, 1])
        f1 = sb("f1", [128, 2, 1024])
        f2 = sb("f2", [128, 8, D])
        fb1c = sb("fb1c", [128, 8])
        fb2r = sb("fb2r", [1, D])
        keyA = sb("keyA", [128, SC])
        keyB = sb("keyB", [128, SC])
        dinv = sb("dinv", [128, NT])
        st6 = sb("st6", [128, NT, 6])
        mv = sb("mv", [128, NT, 2])
        rs = sb("rs", [128, NT])
        wsel = sb("wsel", [128, NT])
        top = sb("top", [128, NT, 2])
        gidx = sb("gidx", [128, NT * 2], U32)
        HB = 24576
        arena = sb("arena", [128, HB])
        epsc = sb("epsc", [128, 1])

        class Cut:
            def __init__(self, at=0):
                self.at = at

            def __call__(self, shape, dt=F32, parts=128):
                n = 1
                for s in shape:
                    n *= s
                words = n if dt != BF16 else (n + 1) // 2
                assert self.at + words <= HB, (self.at, words)
                v = arena[0:parts, self.at:self.at + words]
                self.at += words
                if dt == BF16:
                    v = v.bitcast(BF16)[:, 0:n]
                elif dt != F32:
                    v = v.bitcast(dt)
                if len(shape) == 2:
                    v = v.rearrange("p (a b) -> p a b", b=shape[1])
                elif len(shape) == 3:
                    v = v.rearrange("p (a b c) -> p a b c", b=shape[1], c=shape[2])
                return v

        xs_d = nc.dram_tensor("xs_scr", [NS * 128, D], F32).ap()
        ys_d = nc.dram_tensor("ys_scr", [NS * 128, D], F32).ap()
        yt_d = nc.dram_tensor("yt_scr", [YROWS, D], F32).ap()
        dp_d = nc.dram_tensor("dp_scr", [NG * GE], I32).ap()
        wt_d = nc.dram_tensor("wt_scr", [NT * 128], F32).ap()

        def bc(ap, axis, n):
            v = ap.unsqueeze(axis)
            shape = list(v.shape)
            shape[axis] = n
            return v.broadcast_to(shape)

        s_ld = [sem(f"s_ld{i}") for i in range(8)]
        ca = Cut()
        dsti = ca([EC], I32)
        dstf = ca([EC])
        junk = ca([EC], BF16)
        pre_end = ca.at
        neg1 = sb("neg1", [1, PADS], I32)
        t_neg = G(lambda e: e.memset(neg1[:, :], -1))
        t_dst = dma("sp", s_ld[0], lambda e: e.dma_start(dsti[0:EP, :], dst.rearrange("(p c) -> p c", p=EP)))
        s_dp = sem("s_dp")
        cut0 = (NG - 1) * GE
        dma("sp", s_dp, lambda e: e.dma_start(dp_d[0:cut0].rearrange("(p c) -> p c", c=GE),
                                              dst[0:cut0].rearrange("(p c) -> p c", c=GE)))
        dma("sp", s_dp, lambda e: e.dma_start(dp_d[cut0 + PADS:NG * GE].rearrange("(a c) -> a c", a=1),
                                              dst[cut0:NE].rearrange("(a c) -> a c", a=1)))
        t_dp = dma("sp", s_dp, lambda e: e.dma_start(dp_d[cut0:cut0 + PADS].rearrange("(a c) -> a c", a=1), neg1[:, :]),
                   t_neg)
        t_xz = V(lambda e: e.memset(X[:, NT - 1, :], 0.0))
        s_x = sem("s_x")
        dma("act", s_x, lambda e: e.dma_start(X[:, 0:NT - 1, :], x[0:(NT - 1) * 128, :].rearrange("(t p) d -> p t d", p=128)))
        t_x = dma("act", s_x, lambda e: e.dma_start(X[0:N - (NT - 1) * 128, NT - 1, :], x[(NT - 1) * 128:N, :]), t_xz)
        row = lambda v: v.rearrange("(a n) -> a n", a=1)
        dma("act", s_ld[2], lambda e: e.dma_start(w1a[:, :], gW1[0:64, :]))
        dma("act", s_ld[2], lambda e: e.dma_start(w1b[:, :, :], gW1[64:320, :].rearrange("(k p) n -> p k n", p=128)))
        dma("act", s_ld[2], lambda e: e.dma_start(w2g[:, :, :], gW2.rearrange("(k p) n -> p k n", p=128)))
        dma("act", s_ld[2], lambda e: e.dma_start(b1g[:, :], gb1.rearrange("(c p) -> p c", p=128), allow_slow_non_contiguous=True))
        dma("act", s_ld[2], lambda e: e.dma_start(b2g[:, :], row(gb2)))
        dma("act", s_ld[2], lambda e: e.dma_start(gw[:, :, :], gate_w.rearrange("(k p) n -> p k n", p=128)))
        t_w0 = dma("act", s_ld[2], lambda e: e.dma_start(gb[:, :], row(gate_b)))
        dma("act", s_ld[3], lambda e: e.dma_start(cWn[:, :, :], cW.rearrange("(k p) n -> p k n", p=128)))
        dma("act", s_ld[3], lambda e: e.dma_start(cbr[:, :], row(cb)))
        dma("act", s_ld[3], lambda e: e.dma_start(wrr[:, :], wr.rearrange("d o -> o d").broadcast_to([128, D])))
        dma("act", s_ld[3], lambda e: e.dma_start(brr[:, :], br.rearrange("(a n) -> a n", a=1).broadcast_to([128, 1])))
        dma("act", s_ld[3], lambda e: e.dma_start(f1[:, :, :], fw1.rearrange("(k p) n -> p k n", p=128)))
        dma("act", s_ld[3], lambda e: e.dma_start(f2[:, :, :], fw2.rearrange("(k p) n -> p k n", p=128)))
        dma("act", s_ld[3], lambda e: e.dma_start(fb1c[:, :], fb1.rearrange("(c p) -> p c", p=128), allow_slow_non_contiguous=True))
        t_w1 = dma("act", s_ld[3], lambda e: e.dma_start(fb2r[:, :], row(fb2)))

        def iota(ap, pattern, base=0, cm=0):
            return G(lambda e: e.iota(ap, pattern=pattern, base=base, channel_multiplier=cm,
                                      allow_small_or_imprecise_dtypes=True))

        ioq = ca([NQ])
        iog = ca([NG - 1])
        ioh = ca([NT - 1])
        io16 = sb("io16", [128, NX])
        io25 = sb("io25", [128, NT])
        iob25 = sb("iob25", [128, NT], BF16)
        io64 = sb("io64", [128, NS])
        iota(iof[:, :], [[1, 128]])
        iota(iop[:, :], [[0, 1]], cm=1)
        iota(iob[:, :], [[1, 128]])
        iota(ioq, [[1, NQ]])
        iota(iog, [[GE, NG - 1]], base=GE)
        iota(ioh, [[1, NT - 1]], base=1)
        iota(io16[:, :], [[1, NX]])
        iota(io25[:, :], [[128, NT]])
        iota(iob25[:, :], [[1, NT]])
        t_io = iota(io64[:, :], [[1, NS]])
        V(lambda e: e.memset(ones[:, :], 1.0))
        V(lambda e: e.memset(epsc[:, :], LNEPS))
        V(lambda e: e.tensor_scalar(ident[:, :], iof[:, :], iop[:, 0:1], None, ALU.is_equal), t_io)
        V(lambda e: e.tensor_scalar(tri[:, :], iof[:, :], iop[:, 0:1], None, ALU.is_gt))
        V(lambda e: e.tensor_scalar(low[:, :], iof[:, :], iop[:, 0:1], None, ALU.is_lt))
        t_cst = V(lambda e: e.tensor_scalar(padc[:, :], iop[:, :], float(N - (NT - 1) * 128), None, ALU.is_ge))

        cntp = ca([NT - 1])
        sta = ca([NT - 1])
        S = ca([NT])
        hq = ca([NQ])
        keep = ca([NQ])
        hp = ca([1])
        hp128 = ca([1])
        gpi = ca([1], U32)
        goff = ca([NQ], I32)
        qlast = ca([NT], I32)
        Di = ca([GE], I32)
        Df = ca([GE])
        drel = ca([8, NQ], BF16)
        big = ca([NQ, NT - 1])
        tmp = ca([NQ])
        V(lambda e: e.tensor_copy(dstf[0:EP, :], dsti[0:EP, :]), t_dst)
        for h in range(1, NT):
            t = V(lambda e, h=h: e.tensor_scalar(junk[0:EP, :], dstf[0:EP, :], 128.0 * h, 0.0, ALU.is_lt, ALU.add,
                                                 accum_out=cntp[0:EP, h - 1:h]))
        t = P(lambda e: e.matmul(PS[3][:, 0:NT - 1], ones[0:EP, :], cntp[0:EP, :], start=True, stop=True), t)
        V(lambda e: e.tensor_copy(sta, PS[3][:, 0:NT - 1]), t)
        fl = big.rearrange("p a b -> p (a b)")[:, 0:(NT - 1) * (NG - 1)].rearrange("p (a b) -> p a b", b=NG - 1)
        V(lambda e: e.tensor_tensor(fl, bc(sta, 2, NG - 1), bc(iog, 1, NT - 1), ALU.is_ge))
        V(lambda e: e.tensor_reduce(S[:, 1:NT], fl, AX.X, ALU.add))
        V(lambda e: e.memset(S[:, 0:1], 0.0))
        V(lambda e: e.tensor_tensor(S[:, 1:NT], S[:, 1:NT], ioh, ALU.add))
        V(lambda e: e.tensor_scalar(big[:, 0, :], S[:, 1:NT], iop[:, 0:1], 0.0, ALU.is_le, ALU.add, accum_out=hp))
        V(lambda e: e.tensor_tensor(gpi, iop[:, :], hp, ALU.subtract))
        t_gp = V(lambda e: e.tensor_scalar(hp128, hp, 128.0, None, ALU.mult))
        s_D = sem("s_D")
        t_D = dma("pool", s_D, lambda e: e.indirect_dma_start(
            Di[0:NQ, :], None, dp_d.rearrange("(g c) -> g c", c=GE),
            bass.IndirectOffsetOnAxis(ap=gpi[0:NQ, 0:1], axis=0)), t_gp, t_dp)
        V(lambda e: e.tensor_tensor(big, bc(ioq, 2, NT - 1), bc(S[:, 1:NT], 1, NQ), ALU.is_ge))
        V(lambda e: e.tensor_reduce(hq, big, AX.X, ALU.add))
        V(lambda e: e.tensor_tensor(tmp, ioq, hq, ALU.subtract))
        t_goff = V(lambda e: e.tensor_scalar(goff, tmp, 128.0, float(LASTROW), ALU.mult, ALU.min))
        V(lambda e: e.tensor_tensor(keep[:, 1:NQ], hq[:, 1:NQ], hq[:, 0:NQ - 1], ALU.is_equal))
        V(lambda e: e.tensor_scalar(qlast[:, 0:NT - 1], S[:, 1:NT], -1.0, None, ALU.add))
        V(lambda e: e.memset(qlast[:, NT - 1:NT], NQ - 1))
        t_Df = V(lambda e: e.tensor_scalar(Df[0:NQ, :], Di[0:NQ, :], hp128[0:NQ, 0:1], None, ALU.subtract), t_D)
        Dr = Df[0:NQ, :].rearrange("q (p r) -> q r p", r=8)
        t_dr = []
        for hf in range(2):
            for r in range(4):
                t = P(lambda e, hf=hf, r=r: e.transpose(PS[4 + hf][:, r * NQ:(r + 1) * NQ], Dr[:, 4 * hf + r, :],
                                                        ident[0:NQ, 0:NQ]), t_Df)
            t_dr.append(V(lambda e, hf=hf: e.tensor_copy(
                drel[:, 4 * hf:4 * hf + 4, :], PS[4 + hf][:, 0:4 * NQ].rearrange("p (r q) -> p r q", q=NQ)), t))

        def ln_stats(t, *after):
            V(lambda e: e.bn_stats(st6[:, t, :], X[:, t, :]), *after)
            return V(lambda e: e.bn_aggr(mv[:, t, :], st6[:, t, :]))

        def ln_scale(a, b, after):
            k = A(lambda e: e.activation(rs[:, a:b], mv[:, a:b, 1], ACT.Sqrt, bias=epsc[:, 0:1]), after)
            return V(lambda e: e.reciprocal(rs[:, a:b], rs[:, a:b]), k)

        def ln_apply(t, dest, *after):
            return V(lambda e: e.tensor_scalar(dest, X[:, t, :], mv[:, t, 0:1], rs[:, t:t + 1],
                                               ALU.subtract, ALU.mult), *after)

        for t in range(NT):
            k = ln_stats(t, t_x)
        ln_scale(0, NT, k)
        t_xh0 = [ln_apply(t, XB[:, t, :]) for t in range(NT)]

        ring = ca([RA, 512])
        r1 = ca([2, 512])
        lo = ca([2, 8, 65], BF16)
        oh = ca([2, 8, 128], BF16)
        store = ca([NQ, 65])
        agg = sb("agg", [128, NT, 65])
        s_ring = [sem(f"s_ring{i}") for i in range(RA)]
        attr_v = attr.rearrange("(a r) f -> a (r f)", r=8)
        for s in range(2):
            t_lo1 = V(lambda e, s=s: e.memset(lo[:, s, :, 64:65], 1.0))
        ringb = ring.bitcast(BF16).rearrange("p a (r f two) -> p a r f two", two=2, f=64)
        r1b = r1.bitcast(BF16).rearrange("p a (r f two) -> p a r f two", two=2, f=64)
        ringf = ring.rearrange("p a (r f) -> p a r f", f=64)
        r1f = r1.rearrange("p a (r f) -> p a r f", f=64)
        t_mm, t_ld, t_st, t_r1 = {}, {}, {}, {}

        def load_attr(k):
            def go(e):
                r = e.value_load(goff[0:1, k:k + 1], min_val=0, max_val=LASTROW)
                return e.dma_start(ring[:, k % RA, :], attr_v[bass.ds(r, 128), :])
            t_ld[k] = dma("sp", s_ring[k % RA], go, t_goff, t_mm.get(k - RA))

        def split_attr(k):
            s = k % 2
            t_r1[k] = G(lambda e: e.tensor_tensor(r1f[:, s, :, :], ringf[:, k % RA, :, :], ringb[:, k % RA, :, :, 1],
                                                  ALU.subtract), t_ld[k], t_mm.get(k - 2))

        for k in range(RA):
            load_attr(k)
        split_attr(0)
        for k in range(NQ):
            s, z = k % 2, PS[k % 3]
            if k + 1 < NQ:
                split_attr(k + 1)
            t1 = V(lambda e, k=k, s=s: e.tensor_tensor(oh[:, s, :, :], bc(iob[:, :], 1, 8), bc(drel[:, :, k], 2, 128),
                                                       ALU.is_equal), t_mm.get(k - 2), *t_dr)
            t2 = V(lambda e, s=s: e.tensor_tensor(lo[:, s, :, 0:64], r1f[:, s, :, :], r1b[:, s, :, :, 1],
                                                  ALU.subtract), t_r1[k], t_lo1)
            for r in range(8):
                P(lambda e, s=s, r=r, z=z: e.matmul(z[:, 0:65], oh[:, s, r, :], lo[:, s, r, :], start=(r == 0),
                                                    stop=False), t2, t1, t_st.get(k - 3), sig=False)
                P(lambda e, s=s, r=r, z=z: e.matmul(z[:, 0:64], oh[:, s, r, :], r1b[:, s, r, :, 1], start=False,
                                                    stop=False), t_r1[k], sig=False)
                t3 = P(lambda e, k=k, s=s, r=r, z=z: e.matmul(z[:, 0:64], oh[:, s, r, :], ringb[:, k % RA, r, :, 1],
                                                              start=False, stop=(r == 7)), t_ld[k], sig=(r == 7))
            t_mm[k] = t3
            if k + RA < NQ:
                load_attr(k + RA)
            j = k - 1
            for j in ([k - 1] if k else []) + ([k] if k == NQ - 1 else []):
                if j == 0:
                    t_st[j] = V(lambda e, z=PS[0]: e.tensor_copy(store[:, 0, :], z[:, 0:65]), t_mm[0])
                else:
                    t_st[j] = V(lambda e, j=j, z=PS[j % 3]: e.scalar_tensor_tensor(
                        store[:, j, :], store[:, j - 1, :], keep[:, j:j + 1], z[:, 0:65], ALU.mult, ALU.add), t_mm[j])
        for h in range(NT):
            def pick(e, h=h):
                r = e.value_load(qlast[0:1, h:h + 1], min_val=0, max_val=NQ - 1)
                return e.tensor_copy(agg[:, h, :], store[:, bass.ds(r, 1), :].rearrange("p a b -> p (a b)"))
            V(pick)
        cn = sb("cn", [128, NT])
        V(lambda e: e.tensor_scalar(cn[:, :], agg[:, :, 64], 1.0, None, ALU.max))
        V(lambda e: e.reciprocal(cn[:, :], cn[:, :]))
        t_agg = V(lambda e: e.tensor_tensor(agg[:, :, 0:64], agg[:, :, 0:64], bc(cn[:, :], 2, 64), ALU.mult))
        t_l0 = t_agg

        ca = Cut()
        CT = ca([2, 3, 512])
        HT = ca([2, 4, 512])
        XT1 = ca([2, 512])
        lg = ca([NT, NX])
        srci = ca([EC], I32)
        srcb = ca([EC], I32)
        slo = ca([EC], BF16)
        shi = ca([EC], BF16)
        ohl = ca([2, 16, 128], BF16)
        ohh = ca([2, 16, NT], BF16)
        srcf = ca([EC])
        dstf2 = ca([EC])
        dsti2 = ca([EC], I32)
        mlp_end = ca.at
        groups = [list(range(a, min(a + 4, NT))) for a in range(0, NT, 4)]
        t_ct, t_ht, t_tp, t_hmm, t_omm, t_x1, t_xh1, t_lg = {}, {}, {}, {}, {}, {}, {}, {}
        t_op = {}

        s_src = sem("s_src")
        t_src = dma("sp", s_src, lambda e: e.dma_start(srci[0:EP, :], src.rearrange("(p c) -> p c", p=EP)), t_l0)
        t_src = dma("sp", s_src, lambda e: e.dma_start(dsti2[0:EP, :], dst.rearrange("(p c) -> p c", p=EP)), t_l0)

        sorted_tok = {}

        def background():
            V(lambda e: e.tensor_scalar(srcb[0:EP, :], srci[0:EP, :], 127, None, ALU.bitwise_and), t_src, t_l0)
            V(lambda e: e.tensor_copy(slo[0:EP, :], srcb[0:EP, :]))
            V(lambda e: e.tensor_scalar(srcb[0:EP, :], srci[0:EP, :], 7, None, ALU.arith_shift_right))
            V(lambda e: e.tensor_copy(shi[0:EP, :], srcb[0:EP, :]))
            V(lambda e: e.tensor_copy(srcf[0:EP, :], srci[0:EP, :]))
            V(lambda e: e.tensor_copy(dstf2[0:EP, :], dsti2[0:EP, :]))
            yield
            t_d = {}
            for c in range(EC // 16):
                s = c % 2
                k1 = V(lambda e, c=c, s=s: e.tensor_tensor(ohl[0:EP, s, :, :], bc(iob[0:EP, :], 1, 16),
                                                           bc(slo[0:EP, 16 * c:16 * c + 16], 2, 128), ALU.is_equal),
                       t_d.get(c - 2))
                k2 = V(lambda e, c=c, s=s: e.tensor_tensor(ohh[0:EP, s, :, :], bc(iob25[0:EP, :], 1, 16),
                                                           bc(shi[0:EP, 16 * c:16 * c + 16], 2, NT), ALU.is_equal))
                for r in range(16):
                    t_d[c] = P(lambda e, c=c, s=s, r=r: e.matmul(
                        PS[7][:, 0:NT], ohl[0:EP, s, r, :], ohh[0:EP, s, r, :], start=(c == 0 and r == 0),
                        stop=(c == EC // 16 - 1 and r == 15)), k2, free.get(7), sig=(r == 15))
                yield
            k = V(lambda e: e.tensor_copy(dinv[:, :], PS[7][:, 0:NT]), t_d[EC // 16 - 1])
            degn = sb("degn", [128, NT])
            nb = V(lambda e: e.tensor_copy(degn[:, :], dinv[:, :]))
            V(lambda e: e.tensor_tensor(dinv[:, NT - 1:NT], dinv[:, NT - 1:NT], padc[:, :], ALU.add))
            k = A(lambda e: e.activation(dinv[:, :], dinv[:, :], ACT.Sqrt), Token(q.sems["dve"], q.count["dve"]))
            sorted_tok["dinv"] = V(lambda e: e.reciprocal(dinv[:, :], dinv[:, :]), k)
            yield
            need = sb("need", [128, NT])
            needi = sb("needi", [128, NT], I32)
            k = P(lambda e: e.matmul(PS[7][:, 32:32 + NT], ones[:, :], degn[:, :], start=True, stop=True), nb)
            V(lambda e: e.tensor_copy(needi[:, :], PS[7][:, 32:32 + NT]), k)
            V(lambda e: e.tensor_scalar(needi[:, :], needi[:, :], 127, None, ALU.bitwise_and))
            V(lambda e: e.tensor_copy(need[:, :], needi[:, :]))
            V(lambda e: e.memset(keyA[:, :], float(3900 * 4096 + ZROW)))
            V(lambda e: e.scalar_tensor_tensor(keyA[0:EP, 0:EC], srcf[0:EP, :], 4096.0, dstf2[0:EP, :],
                                               ALU.mult, ALU.add))
            ok = sb("ok", [128, NT])
            ok2 = sb("ok2", [128, NT])
            V(lambda e: e.tensor_scalar(ok[:, :], need[:, :], iop[:, 0:1], 128.0, ALU.add, ALU.is_lt))
            V(lambda e: e.tensor_scalar(ok2[:, :], need[:, :], 0.0, None, ALU.is_gt))
            V(lambda e: e.tensor_tensor(ok[:, :], ok[:, :], ok2[:, :], ALU.mult))
            big_key = float(3900 * 4096 + ZROW)
            V(lambda e: e.tensor_scalar(ok2[:, :], io25[:, :], 127.0, 4096.0, ALU.add, ALU.mult))
            V(lambda e: e.tensor_scalar(ok2[:, :], ok2[:, :], float(ZROW) - big_key, None, ALU.add))
            V(lambda e: e.tensor_tensor(ok2[:, :], ok2[:, :], ok[:, :], ALU.mult))
            V(lambda e: e.tensor_scalar(keyA[:, EC:EC + NT], ok2[:, :], big_key, None, ALU.add))
            yield
            yield from sort()

        cur = [keyA, keyB]
        sgn = sb("sgn", [128, 8])
        sgi = sb("sgi", [128, 8], I32)
        sgc = sb("sgc", [128, 1], I32)

        def stage(kbit, jbit, after=None):
            a, b = cur
            j = 1 << jbit
            if kbit >= 10:
                va = a[:, :].rearrange("p (m two j) -> p m two j", two=2, j=j)
                vb = b[:, :].rearrange("p (m two j) -> p m two j", two=2, j=j)
                V(lambda e: e.tensor_tensor(vb[:, :, 0, :], va[:, :, 0, :], va[:, :, 1, :], ALU.min), after)
                t = V(lambda e: e.tensor_tensor(vb[:, :, 1, :], va[:, :, 0, :], va[:, :, 1, :], ALU.max), chain=False)
            else:
                k = 1 << kbit
                va = a[:, :].rearrange("p (g up m two j) -> p g up m two j", up=2, two=2, j=j, m=k // (2 * j))
                vb = b[:, :].rearrange("p (g up m two j) -> p g up m two j", up=2, two=2, j=j, m=k // (2 * j))
                ops = [(0, 0, ALU.min), (0, 1, ALU.max), (1, 0, ALU.max), (1, 1, ALU.min)]
                for i, (up, w, op) in enumerate(ops):
                    t = V(lambda e, up=up, w=w, op=op: e.tensor_tensor(
                        vb[:, :, up, :, w, :], va[:, :, up, :, 0, :], va[:, :, up, :, 1, :], op),
                        after, chain=(i == 0))
            cur.reverse()
            return t

        def turn(scale, after):
            a, b = cur
            for h in range(2):
                for f in range(4):
                    c = (4 * h + f) * 128
                    t = P(lambda e, f=f, c=c: e.transpose(PS[7][:, f * 128:f * 128 + 128], a[:, c:c + 128], ident[:, :]),
                          after, free.get(7), sig=(f == 3))
                free[7] = A(lambda e, h=h: e.activation(b[:, h * 512:(h + 1) * 512], PS[7][:, :], ACT.Identity,
                                                        scale=scale), t)
                yield
            cur.reverse()

        def sort():
            V(lambda e: e.tensor_copy(sgc[:, :], iop[:, :]))
            for m in range(8):
                V(lambda e, m=m: e.tensor_scalar(sgi[:, m:m + 1], sgc[:, :], m, 1, ALU.logical_shift_right, ALU.bitwise_and))
            V(lambda e: e.tensor_copy(sgn[:, :], sgi[:, :]))
            V(lambda e: e.tensor_scalar(sgn[:, :], sgn[:, :], -2.0, 1.0, ALU.mult, ALU.add))
            yield
            for kbit in range(1, 10):
                for jbit in range(kbit - 1, -1, -1):
                    stage(kbit, jbit)
                    yield
            a = cur[0]
            V(lambda e, a=a: e.tensor_scalar(a[:, :], a[:, :], sgn[:, 0:1], None, ALU.mult))
            for jbit in range(9, -1, -1):
                t = stage(10, jbit)
                yield
            a = cur[0]
            t = V(lambda e, a=a: e.tensor_scalar(a[:, :], a[:, :], sgn[:, 0:1], None, ALU.mult))
            for m in range(1, 8):
                yield from turn(1.0, t)
                t = free[7]
                for jbit in range(m - 1, -1, -1):
                    t = stage(m if m < 7 else 10, jbit, t)
                    yield
                yield from turn(sgn[:, m:m + 1], t)
                t = free[7]
                for jbit in range(9, -1, -1):
                    t = stage(10, jbit, t)
                    yield
                if m < 7:
                    a = cur[0]
                    t = V(lambda e, a=a, m=m: e.tensor_scalar(a[:, :], a[:, :], sgn[:, m:m + 1], None, ALU.mult))
            yield from turn(1.0, t)
            sorted_tok["sort"] = free[7]

        bg = background()

        def step_bg(n):
            for _ in range(n):
                next(bg, None)

        free = {}

        def turned(bank, tiles, src_of, parts, *after):
            n = 128 * len(tiles)
            for j, t in enumerate(tiles):
                k = P(lambda e, j=j, t=t: e.transpose(PS[bank][0:parts, j * 128:(j + 1) * 128], src_of(t), ident[:, :]),
                      free.get(bank), *after, sig=(j == len(tiles) - 1))
            return k, n

        def transposes(gi):
            g, s = groups[gi], gi % 2
            for c in range(3):
                pp, b = (64, 0) if c == 0 else (128, c % 2)
                src_of = (lambda t: agg[:, t, 0:64]) if c == 0 else (lambda t, c=c: XB[:, t, (c - 1) * 128:c * 128])
                k, n = turned(b, g, src_of, pp, t_agg, t_xh0[g[-1]])
                t_tp[(gi, c)] = k
                if c < 2:
                    t_ct[(gi, c)] = A(lambda e, b=b, c=c, pp=pp: e.activation(
                        CT[0:pp, s, c, 0:n], PS[b][0:pp, 0:n], ACT.Identity), k, t_hmm.get(gi - 2), t_l0)
                else:
                    t_ct[(gi, c)] = V(lambda e, b=b, c=c, pp=pp: e.tensor_copy(
                        CT[0:pp, s, c, 0:n], PS[b][0:pp, 0:n]), k, t_hmm.get(gi - 2), t_l0)
                free[b] = t_ct[(gi, c)]

        def hidden(gi):
            g, s = groups[gi], gi % 2
            n = 128 * len(g)
            for c in range(4):
                z = PS[3 + c % 2]
                w = (t_ht.get((gi, c - 2)) if c >= 2 else t_ht.get((gi - 1, c + 2)))
                for i, (lhs, pp) in enumerate([(w1a[:, c * 128:(c + 1) * 128], 64), (w1b[:, 0, c * 128:(c + 1) * 128], 128),
                                               (w1b[:, 1, c * 128:(c + 1) * 128], 128)]):
                    k = P(lambda e, lhs=lhs, pp=pp, i=i, z=z: e.matmul(z[:, 0:n], lhs, CT[0:pp, s, i, 0:n],
                                                                      start=(i == 0), stop=(i == 2)),
                          t_w0, w, t_ct[(gi, i)], sig=(i == 2))
                t_ht[(gi, c)] = A(lambda e, c=c, z=z: e.activation(HT[:, s, c, 0:n], z[:, 0:n], ACT.Relu,
                                                                   bias=b1g[:, c:c + 1]), k, t_omm.get(gi - 2))
            t_hmm[gi] = k

        def output(gi):
            g, s = groups[gi], gi % 2
            for j, t in enumerate(g):
                z = PS[2 + 3 * (t % 2)][:, 0:256]
                for c in range(4):
                    P(lambda e, j=j, c=c, z=z: e.matmul(z, HT[:, s, c, j * 128:(j + 1) * 128], w2g[:, c, :],
                                                        start=(c == 0), stop=False), t_ht[(gi, c)], t_x1.get(t - 2),
                      sig=False)
                k = P(lambda e, z=z: e.matmul(z, ones[0:1, :], b2g[:, :], start=False, stop=True))
                t_x1[t] = V(lambda e, t=t, z=z: e.tensor_tensor(X[:, t, :], X[:, t, :], z, ALU.add), k)
                kk = ln_stats(t)
            t_omm[gi] = k
            kk = ln_scale(g[0], g[-1] + 1, kk)
            for t in g:
                t_xh1[t] = ln_apply(t, XB[:, t, :], t_tp[(gi, 2)])

        def gate(gi):
            g = groups[gi]
            for c in range(2):
                k, n = turned(c, g, lambda t, c=c: XB[:, t, c * 128:(c + 1) * 128], 128, t_xh1[g[-1]])
                free[c] = t_lg[("c", gi, c)] = A(lambda e, c=c, n=n: e.activation(XT1[:, c, 0:n], PS[c][:, 0:n],
                                                                                  ACT.Identity), k,
                                                 t_lg.get(("m", gi - 1)), t_l0)
            for j, t in enumerate(g):
                z = PS[6][:, NX * j:NX * j + NX]
                for c in range(2):
                    P(lambda e, c=c, j=j, z=z: e.matmul(z, XT1[:, c, j * 128:(j + 1) * 128], gw[:, c, :],
                                                        start=(c == 0), stop=False), t_lg[("c", gi, c)], free.get(6),
                      sig=False)
                k = P(lambda e, z=z: e.matmul(z, ones[0:1, :], gb[:, :], start=False, stop=True))
            t_lg[("m", gi)] = k
            free[6] = V(lambda e: e.tensor_copy(lg[:, g[0]:g[-1] + 1, :],
                                                PS[6][:, 0:NX * len(g)].rearrange("p (t x) -> p t x", x=NX)), k)

        for a in range(2):
            for b in range(2):
                k = P(lambda e, a=a, b=b: e.transpose(PS[7][:, b * 256 + a * 128:b * 256 + a * 128 + 128],
                                                      cWn[:, a, b * 128:(b + 1) * 128], ident[:, :]), t_w1, t_cst)
        t_cw = A(lambda e: e.activation(cWT[:, :, :], PS[7][:, :].rearrange("p (a b) -> p a b", b=256), ACT.Identity), k)
        free[7] = t_cw
        transposes(0)
        for gi in range(len(groups) + 1):
            if gi + 1 < len(groups):
                transposes(gi + 1)
            if gi < len(groups):
                hidden(gi)
            if gi:
                output(gi - 1)
                gate(gi - 1)
            step_bg(9)
        t_x1all = V(lambda e: e.memset(rs[:, 0:1], 0.0))

        s_out = sem("s_out")

        def finish(tok):
            dma("sp", s_out, lambda e: e.dma_start(out[0:(NT - 1) * 128, :].rearrange("(t p) d -> p t d", p=128),
                                                   X[:, 0:NT - 1, :]), tok)
            return dma("sp", s_out, lambda e: e.dma_start(out[(NT - 1) * 128:N, :], X[0:N - (NT - 1) * 128, NT - 1, :]), tok)

        def stages_after():
            ca = Cut(mlp_end)
            ex = ca([NT, NX])
            mx = ca([NT, 8])
            mi = ca([NT, 8], U32)
            sm = ca([NT])
            sm2 = ca([NT])
            idf = ca([NT, 2])
            M = ca([NT * 2, NX])
            pos = ca([NT * 2, NX])
            tot = ca([NT * 2, NX])
            inc = ca([NX, NT * 2])
            one50 = ca([NT * 2])
            til = ca([NX, NT])
            nt = ca([NX])
            end = ca([NX])
            base = ca([NX])
            slot = ca([NT * 2])
            cmp = ca([NS, NX])
            ei = sb("ei", [128, NS], I32)
            sidx = sb("sidx", [128, NT * 2], U32)
            V(lambda e: e.tensor_reduce(sm, lg, AX.X, ALU.max))
            k = V(lambda e: e.tensor_tensor(ex, lg, bc(sm, 2, NX), ALU.subtract))
            k = A(lambda e: e.activation(ex, ex, ACT.Exp), k)
            V(lambda e: e.tensor_reduce(sm, ex, AX.X, ALU.add), k)
            V(lambda e: e.reciprocal(sm, sm))
            V(lambda e: e.tensor_tensor(ex, ex, bc(sm, 2, NX), ALU.mult))
            for t in range(NT):
                V(lambda e, t=t: e.max(mx[:, t, :], ex[:, t, :]), chain=(t == 0))
            for t in range(NT):
                V(lambda e, t=t: e.max_index(mi[:, t, :], mx[:, t, :], ex[:, t, :]), chain=(t == 0))
            V(lambda e: e.tensor_tensor(sm2, mx[:, :, 0], mx[:, :, 1], ALU.add))
            V(lambda e: e.reciprocal(sm2, sm2))
            t_top = V(lambda e: e.tensor_tensor(top[:, :, :], mx[:, :, 0:2], bc(sm2, 2, 2), ALU.mult))
            V(lambda e: e.tensor_copy(idf, mi[:, :, 0:2]))
            V(lambda e: e.scalar_tensor_tensor(idf[:, NT - 1, :], bc(padc[:, 0], 1, 2), 100.0, idf[:, NT - 1, :], ALU.mult, ALU.add))
            idv = idf.rearrange("p t k -> p (t k)")
            t_M = V(lambda e: e.tensor_tensor(M, bc(io16[:, :], 1, NT * 2), bc(idv, 2, NX), ALU.is_equal))
            Mf = M.rearrange("p a e -> p (a e)")
            for (b, lhs) in ((0, tri), (2, ones)):
                P(lambda e, b=b, lhs=lhs: e.matmul(PS[b][:, 0:400], lhs[:, :], Mf[:, 0:400], start=True, stop=True), t_M)
                kp = P(lambda e, b=b, lhs=lhs: e.matmul(PS[b + 1][:, 0:400], lhs[:, :], Mf[:, 400:800], start=True, stop=True))
            posf, totf = pos.rearrange("p a e -> p (a e)"), tot.rearrange("p a e -> p (a e)")
            for b in range(2):
                V(lambda e, b=b: e.tensor_copy(posf[:, 400 * b:400 * b + 400], PS[b][:, 0:400]), kp)
                V(lambda e, b=b: e.tensor_copy(totf[:, 400 * b:400 * b + 400], PS[2 + b][:, 0:400]))
            V(lambda e: e.memset(one50, 1.0))
            for x_ in range(NX):
                V(lambda e, x_=x_: e.tensor_tensor_scan(inc[:, x_, :], one50, tot[:, :, x_], 0.0, ALU.mult, ALU.add))
            V(lambda e: e.tensor_tensor(til, bc(inc[:, :, NT * 2 - 1], 2, NT), bc(io25[:, :], 1, NX), ALU.is_gt))
            V(lambda e: e.tensor_reduce(nt, til, AX.X, ALU.add))
            V(lambda e: e.tensor_tensor_scan(end, one50[:, 0:NX], nt, 0.0, ALU.mult, ALU.add))
            V(lambda e: e.tensor_tensor(base, end, nt, ALU.subtract))
            V(lambda e: e.tensor_scalar(base, base, 128.0, None, ALU.mult))
            V(lambda e: e.tensor_tensor(cmp, bc(io64[:, :], 2, NX), bc(end, 1, NS), ALU.is_ge))
            V(lambda e: e.tensor_reduce(io64f[:, :], cmp, AX.X, ALU.add))
            t_ei = V(lambda e: e.tensor_scalar(ei[:, :], io64f[:, :], float(NX - 1), None, ALU.min))
            V(lambda e: e.tensor_tensor(pos, pos, inc.rearrange("p e a -> p a e"), ALU.add))
            V(lambda e: e.tensor_tensor(pos, pos, tot, ALU.subtract))
            V(lambda e: e.tensor_tensor(pos, pos, bc(base, 1, NT * 2), ALU.add))
            V(lambda e: e.tensor_tensor(pos, pos, M, ALU.mult))
            V(lambda e: e.tensor_reduce(slot, pos, AX.X, ALU.add))
            V(lambda e: e.tensor_copy(gidx[:, :], slot))
            V(lambda e: e.scalar_tensor_tensor(slot[:, NT * 2 - 2:NT * 2], bc(padc[:, 0], 1, 2), 100000.0,
                                               slot[:, NT * 2 - 2:NT * 2], ALU.mult, ALU.add))
            t_slot = V(lambda e: e.tensor_copy(sidx[:, :], slot))

            s_sc = sem("s_sc")
            for a in range(NT * 2):
                t_sc = dma("pool", s_sc, lambda e, a=a: e.indirect_dma_start(
                    xs_d, bass.IndirectOffsetOnAxis(ap=sidx[:, a:a + 1], axis=0), XB[:, a // 2, :], None,
                    bounds_check=NS * 128 - 1, oob_is_err=False), t_slot, t_zero)

            ca = Cut(mlp_end)
            NW = 3
            W1 = ca([NW, 2, HID])
            W2 = ca([NW, 2, HID])
            W3 = Cut(3072)([NW, 4, D])
            ca = Cut(0)
            xsb = ca([2, D])
            xT = ca([2, D])
            hs = ca([HID])
            hid = ca([HID])
            hT = ca([HID])
            yb = ca([2, D])
            assert ca.at <= 3072
            s_w = [[sem(f"s_w{j}{i}") for i in range(NW)] for j in range(3)]
            s_xs = [sem(f"s_xs{i}") for i in range(2)]
            s_ys = sem("s_ys")
            v1 = ew1.rearrange("e (k p) n -> p (e k) n", p=128)
            v2 = ew2.rearrange("e (k p) n -> p (e k) n", p=128)
            v3 = ew3.rearrange("e (k p) n -> p (e k) n", p=128)
            t_wl, t_xl, tB, tA, tC, tD, tx, thid, thT, tyb, tst = ({} for _ in range(11))
            e_reg = {}

            def loads(i):
                s = i % NW

                def w(v, W, n, first):
                    def go(e):
                        if first:
                            e_reg[i] = e.value_load(ei[0:1, i:i + 1], min_val=0, max_val=NX - 1)
                        return e.dma_start(W[:, s, :, :], v[:, bass.ds(e_reg[i] * n, n), :])
                    return go
                a = dma("sp", s_w[0][s], w(v1, W1, 2, True), t_ei, t_slot, tB.get(i - NW))
                b = dma("sp", s_w[1][s], w(v2, W2, 2, False), tB.get(i - NW))
                c = dma("sp", s_w[2][s], w(v3, W3, 4, False), tD.get(i - NW))
                t_wl[i] = (a, b, c)

            def load_x(i):
                t_xl[i] = dma("sp", s_xs[i % 2], lambda e: e.dma_start(xsb[:, i % 2, :], xs_d[i * 128:(i + 1) * 128, :]),
                              t_sc, tA.get(i - 2))

            def stA(i):
                for c in range(2):
                    tA[i] = P(lambda e, c=c: e.transpose(PS[4][:, c * 128:(c + 1) * 128],
                                                         xsb[:, i % 2, c * 128:(c + 1) * 128], ident[:, :]),
                              t_xl[i], tx.get(i - 1), sig=(c == 1))
                tx[i] = A(lambda e: e.activation(xT[:, i % 2, :], PS[4][:, 0:256], ACT.Identity), tA[i], tB.get(i - 2))

            def stB(i):
                s = i % NW
                for (b, W, j) in ((0, W1, 0), (2, W2, 1)):
                    for c in range(2):
                        k = P(lambda e, b=b, W=W, c=c: e.matmul(PS[b + i % 2][:, :], xT[:, i % 2, c * 128:(c + 1) * 128],
                                                                W[:, s, c, :], start=(c == 0), stop=(c == 1)),
                              tx[i], t_wl[i][j], thid.get(i - 2), sig=(c == 1))
                    if j == 0:
                        kh = k
                tB[i] = k
                ks = A(lambda e: e.activation(hs, PS[i % 2][:, :], ACT.Silu), kh, thid.get(i - 1))
                thid[i] = V(lambda e: e.tensor_tensor(hid, hs, PS[2 + i % 2][:, :], ALU.mult), ks, k,
                            tC.get(i - 1))

            def stC(i):
                for c in range(4):
                    tC[i] = P(lambda e, c=c: e.transpose(PS[5][:, c * 128:(c + 1) * 128], hid[:, c * 128:(c + 1) * 128],
                                                         ident[:, :]), thid[i], thT.get(i - 1), sig=(c == 3))
                thT[i] = A(lambda e: e.activation(hT, PS[5][:, :], ACT.Identity), tC[i], tD.get(i - 1))

            def stD(i):
                s = i % NW
                for c in range(4):
                    tD[i] = P(lambda e, c=c: e.matmul(PS[6][:, 0:256], hT[:, c * 128:(c + 1) * 128], W3[:, s, c, :],
                                                      start=(c == 0), stop=(c == 3)), thT[i], t_wl[i][2],
                              tyb.get(i - 1), sig=(c == 3))
                tyb[i] = V(lambda e: e.tensor_copy(yb[:, i % 2, :], PS[6][:, 0:256]), tD[i], tst.get(i - 2))
                tst[i] = dma("pool", s_yb[i % 2], lambda e: e.dma_start(ys_d[i * 128:(i + 1) * 128, :], yb[:, i % 2, :]),
                             tyb[i])

            s_yb = [sem(f"s_yb{i}") for i in range(2)]
            for i in range(min(NW, NS)):
                loads(i)
            load_x(0)
            load_x(1)
            stA(0)
            for i in range(NS + 1):
                if i + 1 < NS:
                    stA(i + 1)
                if i + 2 < NS:
                    load_x(i + 2)
                if i:
                    stC(i - 1)
                if i < NS:
                    stB(i)
                if i:
                    stD(i - 1)
                    if i - 1 + NW < NS:
                        loads(i - 1 + NW)
                step_bg(4)
            while next(bg, 1) is None:
                pass

            ca = Cut(0)
            RG = 16
            gr = ca([RG, D])
            s_g = [sem(f"s_g{i}") for i in range(RG)]
            t_g, t_c2 = {}, {}

            def fetch(a):
                t_g[a] = dma("pool", s_g[a % RG], lambda e: e.indirect_dma_start(
                    gr[:, a % RG, :], None, ys_d, bass.IndirectOffsetOnAxis(ap=gidx[:, a:a + 1], axis=0)),
                    tst[NS - 1], tst[NS - 2], t_c2.get(a - RG), tD[NS - 1])

            for a in range(RG):
                fetch(a)
            for t in range(NT):
                for j in range(2):
                    a = 2 * t + j
                    t_c2[a] = V(lambda e, t=t, j=j, a=a: e.scalar_tensor_tensor(
                        X[:, t, :], gr[:, a % RG, :], top[:, t, j:j + 1], X[:, t, :], ALU.mult, ALU.add), t_g[a])
                    if a + RG < NT * 2:
                        fetch(a + RG)
                kk = ln_stats(t)
            ln_scale(0, NT, kk)
            V(lambda e: e.tensor_tensor(rs[:, :], rs[:, :], dinv[:, :], ALU.mult), sorted_tok["dinv"])
            s_yt = sem("s_yt")
            for t in range(NT):
                kk = ln_apply(t, XB[:, t, :], t_sc)
                t_yt = dma("sp", s_yt, lambda e, t=t: e.dma_start(yt_d[t * 128:(t + 1) * 128, :], XB[:, t, :]), kk)
            zr = ca([D])
            kk = V(lambda e: e.memset(zr, 0.0))
            t_yt = dma("sp", s_yt, lambda e: e.dma_start(yt_d[ZROW:ZROW + 128, :], zr), kk)

            ks = cur[0][:, :].rearrange("f (b p) -> f p b", b=8)
            sk = ca([128, 8], I32)
            skd = ca([128 * 8], U32)
            skl = ca([128 * 8], I32)
            skf = ca([128 * 8])
            skb = ca([128 * 8], I32)
            skt = ca([128 * 8])
            RS = 16
            rg = ca([RS, D])
            oh8 = ca([2, 8, 128])
            assert ca.at <= HB
            t_s = sorted_tok["sort"]
            V(lambda e: e.tensor_copy(sk, ks), t_s)
            skv = sk.rearrange("f p b -> f (p b)")
            t_skd = V(lambda e: e.tensor_scalar(skd.bitcast(I32), skv, 4095, None, ALU.bitwise_and))
            V(lambda e: e.tensor_scalar(skl, skv, 12, 127, ALU.logical_shift_right, ALU.bitwise_and))
            V(lambda e: e.tensor_copy(skf, skl))
            V(lambda e: e.tensor_scalar(skl, skv, 19, None, ALU.logical_shift_right))
            V(lambda e: e.tensor_copy(skt, skl))
            V(lambda e: e.tensor_scalar(skt, skt, float(NT - 1), float(D), ALU.min, ALU.mult))
            V(lambda e: e.tensor_copy(skb, skt))
            s_rg = [sem(f"s_rg{i}") for i in range(RS)]
            t_gg, t_z, t_ac, t_oh = {}, {}, {}, {}
            agf = XB[:, :, :].rearrange("p t d -> p (t d)")

            def fetch_e(k):
                t_gg[k] = dma("pool", s_rg[k % RS], lambda e: e.indirect_dma_start(
                    rg[:, k % RS, :], None, yt_d, bass.IndirectOffsetOnAxis(ap=skd[:, k:k + 1], axis=0)),
                    t_skd, t_yt, t_z.get(k - RS))

            def onehots(c):
                s = c % 2
                t_oh[c] = V(lambda e: e.tensor_tensor(oh8[:, s, :, :], bc(iof[:, :], 1, 8),
                                                      bc(skf[:, 8 * c:8 * c + 8], 2, 128), ALU.is_equal),
                            t_z.get(8 * c - 9))

            for k in range(RS):
                fetch_e(k)
            onehots(0)
            LAG = 2
            for k in range(NTILE + LAG):
                if k < NTILE:
                    if k % 8 == 4 and 8 * (k // 8 + 1) < NTILE:
                        onehots(k // 8 + 1)
                    z = PS[k % 8][:, 0:256]
                    t_z[k] = P(lambda e, k=k, z=z: e.matmul(z, oh8[:, (k // 8) % 2, k % 8, :], rg[:, k % RS, :],
                                                            start=True, stop=True), t_oh[k // 8], t_gg[k], t_ac.get(k - 8))
                    if k + RS < NTILE:
                        fetch_e(k + RS)
                if k >= LAG:
                    j = k - LAG

                    def add(e, j=j):
                        z = PS[j % 8][:, 0:256]
                        r = e.value_load(skb[0:1, j:j + 1], min_val=0, max_val=(NT - 1) * D)
                        return e.tensor_tensor(agf[:, bass.ds(r, D)], agf[:, bass.ds(r, D)], z, ALU.add)
                    t_ac[j] = V(add, t_z[j], t_yt)
            t_sp = t_ac[NTILE - 1]

            ca = Cut(0)
            CT2 = ca([2, 2, 512])
            XT3 = ca([2, NT * 128])
            HT3 = ca([8, 512])
            wsum = ca([NT])
            wm = ca([NT])
            jk = ca([D])
            wrow = ca([NT, 128])
            junk2 = ca([NT * 128], BF16)
            t_s3, t_ctm, t_x3, t_xt, t_hm, t_h3, t_ob, t_y = ({} for _ in range(8))
            t_c1, t_om3 = {}, {}

            def conv(gi):
                g, s = groups[gi], gi % 2
                for t in g:
                    k = V(lambda e, t=t: e.tensor_scalar(XB[:, t, :], XB[:, t, :], dinv[:, t:t + 1], None, ALU.mult))
                n = 128 * len(g)
                for c in range(2):
                    for j, t in enumerate(g):
                        kk = P(lambda e, c=c, j=j, t=t: e.transpose(PS[c][:, j * 128:(j + 1) * 128],
                                                                    XB[:, t, c * 128:(c + 1) * 128], ident[:, :]),
                               k, t_xt.get((gi - 1, c)), sig=(j == len(g) - 1))
                    t_c1[(gi, c)] = A(lambda e, c=c: e.activation(CT2[:, s, c, 0:n], PS[c][:, 0:n], ACT.Identity), kk,
                                      t_ctm.get(gi - 2))
                for j, t in enumerate(g):
                    z = PS[2 + 5 * (t % 2)][:, 0:256]
                    for c in range(2):
                        P(lambda e, c=c, j=j, z=z: e.matmul(z, CT2[:, s, c, j * 128:(j + 1) * 128], cWT[:, c, :],
                                                            start=(c == 0), stop=False), t_c1[(gi, c)], t_cw,
                          t_x3.get(t - 2), sig=False)
                    kk = P(lambda e, z=z: e.matmul(z, ones[0:1, :], cbr[:, :], start=False, stop=True))
                    t_x3[t] = V(lambda e, t=t, z=z: e.scalar_tensor_tensor(X[:, t, :], z, 0.0, X[:, t, :], ALU.max, ALU.add), kk)
                    ks_ = ln_stats(t)
                t_ctm[gi] = kk
                ln_scale(g[0], g[-1] + 1, ks_)
                for t in g:
                    ln_apply(t, XB[:, t, :], t_c1[(gi, 1)])
                    V(lambda e, t=t: e.tensor_tensor_reduce(out=jk, in0=XB[:, t, :], in1=wrr[:, :], scale=1.0, scalar=0.0,
                                                            op0=ALU.mult, op1=ALU.add, accum_out=wsum[:, t:t + 1]))
                    k = V(lambda e, t=t: e.tensor_tensor(X[:, t, :], X[:, t, :], XB[:, t, :], ALU.add))
                for c in range(2):
                    for j, t in enumerate(g):
                        kk = P(lambda e, c=c, j=j, t=t: e.transpose(PS[c][:, j * 128:(j + 1) * 128],
                                                                    XB[:, t, c * 128:(c + 1) * 128], ident[:, :]),
                               k, t_c1[(gi, c)], sig=(j == len(g) - 1))
                    t_xt[(gi, c)] = A(lambda e, c=c: e.activation(XT3[:, c, g[0] * 128:g[0] * 128 + n], PS[c][:, 0:n], ACT.Identity), kk)

            def ffn(gi):
                g, s = groups[gi], gi % 2
                n = 128 * len(g)
                for c in range(8):
                    z = PS[3 + c % 2]
                    for i in range(2):
                        k = P(lambda e, c=c, i=i, z=z: e.matmul(z[:, 0:n], f1[:, i, c * 128:(c + 1) * 128], XT3[:, i, g[0] * 128:g[0] * 128 + n],
                                                                start=(i == 0), stop=(i == 1)), t_xt[(gi, i)],
                              t_h3.get((gi, c - 2)) if c >= 2 else t_h3.get((gi - 1, 7)), sig=(i == 1))
                    t_h3[(gi, c)] = A(lambda e, c=c, z=z: e.activation(HT3[:, c, 0:n], z[:, 0:n], ACT.Gelu_apprx_tanh,
                                                                       bias=fb1c[:, c:c + 1]), k, t_om3.get(gi - 1))
                t_hm[gi] = k
                for j, t in enumerate(g):
                    z = PS[5 + t % 2][:, 0:256]
                    for c in range(8):
                        P(lambda e, c=c, j=j, z=z: e.matmul(z, HT3[:, c, j * 128:(j + 1) * 128], f2[:, c, :],
                                                            start=(c == 0), stop=False), t_h3[(gi, c)], t_y.get(t - 2),
                          sig=False)
                    k = P(lambda e, z=z: e.matmul(z, ones[0:1, :], fb2r[:, :], start=False, stop=True))
                    t_y[t] = V(lambda e, t=t, z=z: e.tensor_copy(XB[:, t, :], z), k, t_xt[(gi, 1)])
                t_om3[gi] = k

            for gi in range(len(groups)):
                conv(gi)
            V(lambda e: e.tensor_scalar(wsum, wsum, brr[:, 0:1], None, ALU.add))
            V(lambda e: e.tensor_copy(wm, wsum))
            V(lambda e: e.tensor_scalar(jk[:, 0:1], padc[:, :], -1.0, 1.0, ALU.mult, ALU.add))
            V(lambda e: e.tensor_scalar(jk[:, 1:2], padc[:, :], -3.0e38, None, ALU.mult))
            k = V(lambda e: e.scalar_tensor_tensor(wm[:, NT - 1:NT], wm[:, NT - 1:NT], jk[:, 0:1], jk[:, 1:2], ALU.mult, ALU.add))
            k = P(lambda e: e.transpose(PS[7][0:NT, 0:128], wm, ident[:, :]), k, t_cw)
            wts = jk.rearrange("p (a b) -> p a b", b=128)[0:NT, 1, :]
            k = V(lambda e: e.tensor_copy(wts, PS[7][0:NT, 0:128]), k)
            s_wt = sem("s_wt")
            s_wb = sem("s_wb")
            k = dma("sp", s_wt, lambda e: e.dma_start(wt_d.rearrange("(t p) -> t p", p=128), wts), k)
            k = dma("sp", s_wb, lambda e: e.dma_start(wrow.rearrange("p a b -> p (a b)"),
                                                      wt_d.rearrange("(a n) -> a n", a=1).broadcast_to([128, NT * 128])), k,
                    t_sp)
            wrf = wrow.rearrange("p a b -> p (a b)")
            ra = sb("ra", [128, 3, NT])
            V(lambda e: e.memset(ra[:, :, :], 0.0))

            def rank(t):
                if t:
                    V(lambda e: e.tensor_scalar(junk2[:, 0:t * 128], wrf[:, 0:t * 128], wm[:, t:t + 1], 0.0, ALU.is_ge, ALU.add,
                                                accum_out=ra[:, 0, t:t + 1]), k)
                V(lambda e: e.tensor_scalar(junk2[:, t * 128:NT * 128], wrf[:, t * 128:NT * 128], wm[:, t:t + 1], 0.0,
                                            ALU.is_gt, ALU.add, accum_out=ra[:, 1, t:t + 1]), k)
                V(lambda e: e.scalar_tensor_tensor(junk2[:, 0:128], wrow[:, t, :], wm[:, t:t + 1], low[:, :], ALU.is_equal,
                                                   ALU.mult, accum_out=ra[:, 2, t:t + 1]))

            per = (NT + len(groups) - 1) // len(groups)
            for gi in range(len(groups)):
                ffn(gi)
                for t in range(per * gi, min(per * gi + per, NT)):
                    rank(t)
            V(lambda e: e.tensor_tensor(ra[:, 0, :], ra[:, 0, :], ra[:, 1, :], ALU.add))
            V(lambda e: e.tensor_tensor(ra[:, 0, :], ra[:, 0, :], ra[:, 2, :], ALU.add))
            V(lambda e: e.tensor_scalar(ra[:, 0, :], ra[:, 0, :], float(KEEP), None, ALU.is_lt))
            V(lambda e: e.tensor_tensor(wsel[:, :], ra[:, 0, :], wsum, ALU.mult))
            for t in range(NT):
                kk = V(lambda e, t=t: e.scalar_tensor_tensor(X[:, t, :], XB[:, t, :], wsel[:, t:t + 1], X[:, t, :],
                                                             ALU.mult, ALU.add))
            return kk

        io64f = sb("io64f", [128, NS])
        zero = sb("zero", [128, 512])
        kz = G(lambda e: e.memset(zero[:, :], 0.0))
        s_z = sem("s_z")
        for i in range(32):
            t_zero = dma("sp", s_z, lambda e, i=i: e.dma_start(
                xs_d[i * 256:(i + 1) * 256, :].rearrange("(p r) d -> p (r d)", p=128), zero[:, :]), kz)

        last = stages_after()
        finish(last)

        block = ctx.enter_context(nc.Block())

        @block.sync
        def _(e):
            q.run("sp", e)
            for t in q.landed():
                e.wait_ge(t.sem, t.val)

        @block.gpsimd
        def _(e):
            q.run("pool", e)

        @block.scalar
        def _(e):
            q.run("act", e)

        @block.vector
        def _(e):
            q.run("dve", e)

        @block.tensor
        def _(e):
            q.run("pe", e)


_INS = ["x", "src", "dst", "edge_attr_64", "L0_gnn_W1", "L0_gnn_b1", "L0_gnn_W2", "L0_gnn_b2", "L0_ffn_gate_w",
        "L0_ffn_gate_b", "L0_ffn_w1", "L0_ffn_w2", "L0_ffn_w3", "L1_gnn_W", "L1_gnn_b", "L1_ffn_attention_mask",
        "L1_ffn_wr", "L1_ffn_br", "L1_ffn_w1", "L1_ffn_b1", "L1_ffn_w2", "L1_ffn_b2"]
_OUTS = [((3125, 256), "float32")]


def kernel(**inputs):
    import numpy as _np
    import concourse.bacc as _bacc
    from concourse import mybir as _mybir
    from concourse.bass_utils import run_bass_kernel_spmd as _run

    nc = _bacc.Bacc("TRN2", target_bir_lowering=False, num_devices=1)
    arrays, args = {}, []
    for name in _INS:
        a = _np.ascontiguousarray(inputs[name])
        arrays[f"in_{name}_dram"] = a
        args.append(nc.dram_tensor(f"in_{name}_dram", a.shape, _mybir.dt.from_np(a.dtype), kind="ExternalInput").ap())
    for i, (shape, dtype) in enumerate(_OUTS):
        args.append(nc.dram_tensor(f"out_{i}_dram", shape, _mybir.dt.from_np(_np.dtype(dtype)), kind="ExternalOutput").ap())
    program(nc, *args)
    r = _run(nc, [arrays], core_ids=[0])
    return r.results[0]["out_0_dram"]
```

```python
from contextlib import ExitStack

import concourse.bass as bass
from concourse import mybir

ALU = mybir.AluOpType
ACT = mybir.ActivationFunctionType
AX = mybir.AxisListType
F32 = mybir.dt.float32
BF16 = mybir.dt.bfloat16
F16 = mybir.dt.float16
I32 = mybir.dt.int32
U32 = mybir.dt.uint32

SPLIT, SC_PRE, SC_L0, SC_MLP, SC_GAP, SC_MOE = 1000, 20, 2, 22, 20, 8

N = 3125
NT = 25
D = 256
NE = 100000
E0 = 782
EL = NE - 127 * E0
EC = 784
GE = 1024
NG = 98
NQ = NG + NT - 1
LASTROW = (NE - GE) // 8
PADS = NG * GE - NE
RA = 6
NX = 16
HID = 512
NS = 64
SC = 1024
NV = 26
VW = NV * 128
NA = NT * 128 * VW
PADNODE = 4095
KEEP = 1561
LNEPS = 1e-5


class Token:
    def __init__(self, sem, val):
        self.sem, self.val = sem, val


class Queues:

    def __init__(self, sems):
        self.sems = sems
        self.count = {e: 0 for e in sems}
        self.todo = {e: [] for e in ("sp", "act", "pool", "dve", "pe")}
        self.dcount = {}
        self.last = {}

    def put(self, eng, fn, *after, sig=True, chain=None):
        if chain is None:
            chain = eng == "dve"
        after = [a for a in after if a is not None]
        if chain and self.count[eng]:
            after.append(Token(self.sems[eng], self.count[eng]))
        if sig:
            self.count[eng] += 1
        self.todo[eng].append((fn, after, (self.sems[eng], 1) if sig else None))
        return Token(self.sems[eng], self.count[eng])

    def ahead(self, eng, fn):
        self.todo[eng].append((fn, [], None))

    def dma(self, eng, sem, fn, *after):
        after = [a for a in after if a is not None]
        self.dcount[sem.name] = self.dcount.get(sem.name, 0) + 16
        self.todo[eng].append((fn, after, (sem, 16)))
        self.last[sem.name] = Token(sem, self.dcount[sem.name])
        return self.last[sem.name]

    def landed(self):
        return list(self.last.values())

    def run(self, eng, e):
        seen = {}
        for fn, after, inc in self.todo[eng]:
            for t in after:
                if seen.get(t.sem.name, 0) < t.val:
                    e.wait_ge(t.sem, t.val)
                    seen[t.sem.name] = t.val
            ins = fn(e)
            if inc:
                ins.then_inc(*inc)


def program(nc, x, src, dst, attr, gW1, gb1, gW2, gb2, gate_w, gate_b, ew1, ew2, ew3,
            cW, cb, amask, wr, br, fw1, fb1, fw2, fb2, out):
    ctx = ExitStack()
    with ctx:
        def sb(name, shape, dt=F32):
            return ctx.enter_context(nc.sbuf_tensor(name, shape, dt))

        def sem(name):
            return ctx.enter_context(nc.semaphore(name))

        PS = [ctx.enter_context(nc.psum_tensor(f"ps{i}", [128, 512], F32)) for i in range(8)]
        q = Queues({e: sem("s_" + e) for e in ("act", "pool", "dve", "pe")})
        put, dma = q.put, q.dma

        def V(fn, *after, **k):
            return put("dve", fn, *after, **k)

        def A(fn, *after, **k):
            return put("act", fn, *after, **k)

        def P(fn, *after, **k):
            return put("pe", fn, *after, **k)

        def G(fn, *after, **k):
            return put("pool", fn, *after, **k)

        X = sb("X", [128, NT, D])
        XB = sb("XB", [128, NT, D])
        ident = sb("ident", [128, 128])
        iof = sb("iof", [128, 128])
        iop = sb("iop", [128, 1])
        tri = sb("tri", [128, 128])
        low = sb("low", [128, 128])
        ones = sb("ones", [128, 128])
        padc = sb("padc", [128, 1])
        w1a = sb("w1a", [64, HID])
        w1b = sb("w1b", [128, 2, HID])
        w2g = sb("w2g", [128, 4, D])
        b1g = sb("b1g", [128, 4])
        b2g = sb("b2g", [128, D])
        gw = sb("gw", [128, 2, NX])
        gb = sb("gb", [128, NX])
        cWT = sb("cWT", [128, 2, D])
        cbr = sb("cbr", [128, D])
        wrr = sb("wrr", [128, D])
        brr = sb("brr", [128, 1])
        f1 = sb("f1", [128, 2, 1024])
        f2 = sb("f2", [128, 8, D])
        fb1c = sb("fb1c", [128, 8])
        fb2r = sb("fb2r", [128, D])
        keyA = sb("keyA", [128, SC])
        keyB = sb("keyB", [128, SC])
        dinv = sb("dinv", [128, NT])
        st6 = sb("st6", [128, NT, 6])
        mv = sb("mv", [128, NT, 2])
        rs = sb("rs", [128, NT])
        nm = sb("nm", [128, NT])
        wsel = sb("wsel", [128, NT])
        top = sb("top", [128, NT, 2])
        gidx = sb("gidx", [128, NT * 2], U32)
        HB = 24512
        arena = sb("arena", [128, HB])
        epsc = sb("epsc", [128, 1])

        class Cut:
            def __init__(self, at=0):
                self.at = at

            def __call__(self, shape, dt=F32, parts=128):
                n = 1
                for s in shape:
                    n *= s
                words = n if dt not in (BF16, F16) else (n + 1) // 2
                assert self.at + words <= HB, (self.at, words)
                v = arena[0:parts, self.at:self.at + words]
                self.at += words
                if dt in (BF16, F16):
                    v = v.bitcast(dt)[:, 0:n]
                elif dt != F32:
                    v = v.bitcast(dt)
                if len(shape) == 2:
                    v = v.rearrange("p (a b) -> p a b", b=shape[1])
                elif len(shape) == 3:
                    v = v.rearrange("p (a b c) -> p a b c", b=shape[1], c=shape[2])
                return v

        xs_d = nc.dram_tensor("xs_scr", [NS * 128, D], F32).ap()
        ys_d = nc.dram_tensor("ys_scr", [NS * 128, D], F32).ap()
        yt_d = nc.dram_tensor("yt_scr", [NT * 128, D], F32).ap()
        a_d = nc.dram_tensor("a_scr", [NA], F16).ap()
        dp_d = nc.dram_tensor("dp_scr", [NG * GE], I32).ap()
        wt_d = nc.dram_tensor("wt_scr", [NT * 128], F32).ap()

        def bc(ap, axis, n):
            v = ap.unsqueeze(axis)
            shape = list(v.shape)
            shape[axis] = n
            return v.broadcast_to(shape)

        s_ld = [sem(f"s_ld{i}") for i in range(8)]
        ca = Cut()
        azero = ca([VW], F16)
        early = ca.at
        dsti, srci, vi, v2, s1, s2 = (ca([EC], I32) for _ in range(6))
        junk = ca([EC], BF16)
        big = ca([NQ, NT - 1])
        neg1 = sb("neg1", [1, PADS], I32)
        t_neg = G(lambda e: e.memset(neg1[:, :], -1))
        t_azm = G(lambda e: e.memset(azero, 0.0))

        def edges(s_, to, frm):
            k = V(lambda e: e.memset(to[:, EL:EC], PADNODE))
            dma("sp", s_, lambda e: e.dma_start(to[0:127, 0:E0], frm[0:127 * E0].rearrange("(p c) -> p c", c=E0)), k)
            return dma("sp", s_, lambda e: e.dma_start(to[127:128, 0:EL], frm[127 * E0:NE].rearrange("(p c) -> p c", c=EL)))

        t_dst = edges(s_ld[0], dsti, dst)
        t_src = edges(s_ld[1], srci, src)
        s_dp = sem("s_dp")
        cut0 = (NG - 1) * GE
        dma("sp", s_dp, lambda e: e.dma_start(dp_d[0:cut0].rearrange("(p c) -> p c", c=GE),
                                              dst[0:cut0].rearrange("(p c) -> p c", c=GE)))
        dma("sp", s_dp, lambda e: e.dma_start(dp_d[cut0 + PADS:NG * GE].rearrange("(a c) -> a c", a=1),
                                              dst[cut0:NE].rearrange("(a c) -> a c", a=1)))
        t_dp = dma("sp", s_dp, lambda e: e.dma_start(dp_d[cut0:cut0 + PADS].rearrange("(a c) -> a c", a=1), neg1[:, :]),
                   t_neg)
        s_az = sem("s_az")
        for t in range(NT):
            t_az = dma("sp", s_az, lambda e, t=t: e.dma_start(
                a_d[t * 128 * VW:(t + 1) * 128 * VW].rearrange("(p c) -> p c", c=VW), azero), t_azm)
        s_z = sem("s_z")
        azf = arena[:, 0:512]
        for i in range(32):
            t_zero = dma("sp", s_z, lambda e, i=i: e.dma_start(
                xs_d[i * 256:(i + 1) * 256, :].rearrange("(p r) d -> p (r d)", p=128), azf), t_azm)
        t_xz = V(lambda e: e.memset(X[:, NT - 1, :], 0.0))
        t_edges = [t_dst, t_src]
        s_x = sem("s_x")
        dma("act", s_x, lambda e: e.dma_start(X[:, 0:NT - 1, :], x[0:(NT - 1) * 128, :].rearrange("(t p) d -> p t d", p=128)),
            *t_edges)
        t_x = dma("act", s_x, lambda e: e.dma_start(X[0:N - (NT - 1) * 128, NT - 1, :], x[(NT - 1) * 128:N, :]), t_xz)
        row = lambda v: v.rearrange("(a n) -> a n", a=1)
        dma("act", s_ld[2], lambda e: e.dma_start(w1a[:, :], gW1[0:64, :]))
        dma("act", s_ld[2], lambda e: e.dma_start(w1b[:, :, :], gW1[64:320, :].rearrange("(k p) n -> p k n", p=128)))
        dma("act", s_ld[2], lambda e: e.dma_start(w2g[:, :, :], gW2.rearrange("(k p) n -> p k n", p=128)))
        dma("act", s_ld[2], lambda e: e.dma_start(b1g[:, :], gb1.rearrange("(c p) -> p c", p=128), allow_slow_non_contiguous=True))
        dma("act", s_ld[2], lambda e: e.dma_start(b2g[:, :], row(gb2).broadcast_to([128, D])))
        dma("act", s_ld[2], lambda e: e.dma_start(gw[:, :, :], gate_w.rearrange("(k p) n -> p k n", p=128)))
        t_w0 = dma("act", s_ld[2], lambda e: e.dma_start(gb[:, :], row(gate_b).broadcast_to([128, NX])))
        dma("act", s_ld[3], lambda e: e.dma_start(cbr[:, :], row(cb).broadcast_to([128, D])))
        dma("act", s_ld[3], lambda e: e.dma_start(wrr[:, :], wr.rearrange("d o -> o d").broadcast_to([128, D])))
        dma("act", s_ld[3], lambda e: e.dma_start(brr[:, :], br.rearrange("(a n) -> a n", a=1).broadcast_to([128, 1])))
        dma("act", s_ld[3], lambda e: e.dma_start(f1[:, :, :], fw1.rearrange("(k p) n -> p k n", p=128)))
        dma("act", s_ld[3], lambda e: e.dma_start(f2[:, :, :], fw2.rearrange("(k p) n -> p k n", p=128)))
        dma("act", s_ld[3], lambda e: e.dma_start(fb1c[:, :], fb1.rearrange("(c p) -> p c", p=128), allow_slow_non_contiguous=True))
        t_w1 = dma("act", s_ld[3], lambda e: e.dma_start(fb2r[:, :], row(fb2).broadcast_to([128, D])))

        def iota(ap, pattern, base=0, cm=0):
            return G(lambda e: e.iota(ap, pattern=pattern, base=base, channel_multiplier=cm,
                                      allow_small_or_imprecise_dtypes=True))

        ioq = ca([NQ])
        iog = ca([NG - 1])
        ioh = ca([NT - 1])
        ios = ca([NT - 1])
        io16 = sb("io16", [128, NX])
        io25 = sb("io25", [128, NT])
        iob25 = sb("iob25", [128, NT], BF16)
        iob8 = sb("iob8", [128, 128, 8], BF16)
        io64 = sb("io64", [128, NS])
        iota(iof[:, :], [[1, 128]])
        iota(iop[:, :], [[0, 1]], cm=1)
        iota(ioq, [[1, NQ]])
        iota(iog, [[GE, NG - 1]], base=GE)
        iota(ioh, [[1, NT - 1]], base=1)
        iota(ios, [[-256, NT - 1]], base=-255)
        iota(io16[:, :], [[1, NX]])
        iota(io25[:, :], [[128, NT]])
        iota(iob25[:, :], [[1, NT]])
        iota(iob8[:, :, :], [[1, 128], [0, 8]])
        t_io = iota(io64[:, :], [[1, NS]])
        V(lambda e: e.memset(ones[:, :], 1.0))
        V(lambda e: e.memset(epsc[:, :], LNEPS))
        V(lambda e: e.tensor_scalar(ident[:, :], iof[:, :], iop[:, 0:1], None, ALU.is_equal), t_io)
        V(lambda e: e.tensor_scalar(tri[:, :], iof[:, :], iop[:, 0:1], None, ALU.is_gt))
        V(lambda e: e.tensor_scalar(low[:, :], iof[:, :], iop[:, 0:1], None, ALU.is_lt))
        t_cst = V(lambda e: e.tensor_scalar(padc[:, :], iop[:, :], float(N - (NT - 1) * 128), None, ALU.is_ge))

        cur = [keyA, keyB]
        v0 = sb("v0", [128, 1])
        slo = sb("slo", [128, EC], BF16)
        shi = sb("shi", [128, EC], BF16)
        acnt = sb("acnt", [128, EC], F16)
        vidx = sb("vidx", [128, NV], U32)

        def stage(kbit, jbit):
            a, b = cur
            j = 1 << jbit
            if kbit >= 10:
                va = a[:, :].rearrange("p (m two j) -> p m two j", two=2, j=j)
                vb = b[:, :].rearrange("p (m two j) -> p m two j", two=2, j=j)
                V(lambda e: e.tensor_tensor(vb[:, :, 0, :], va[:, :, 0, :], va[:, :, 1, :], ALU.min))
                V(lambda e: e.tensor_tensor(vb[:, :, 1, :], va[:, :, 0, :], va[:, :, 1, :], ALU.max), chain=False)
            else:
                k = 1 << kbit
                va = a[:, :].rearrange("p (g up m two j) -> p g up m two j", up=2, two=2, j=j, m=k // (2 * j))
                vb = b[:, :].rearrange("p (g up m two j) -> p g up m two j", up=2, two=2, j=j, m=k // (2 * j))
                ops = [(0, 0, ALU.min), (0, 1, ALU.max), (1, 0, ALU.max), (1, 1, ALU.min)]
                for i, (up, w, op) in enumerate(ops):
                    V(lambda e, up=up, w=w, op=op: e.tensor_tensor(
                        vb[:, :, up, :, w, :], va[:, :, up, :, 0, :], va[:, :, up, :, 1, :], op), chain=(i == 0))
            cur.reverse()

        key = keyA[:, 0:EC]
        V(lambda e: e.memset(keyA[:, EC:SC], float((1 << 24) - 1)))
        V(lambda e: e.tensor_scalar(vi, dsti, iop[:, 0:1], None, ALU.add), t_dst, t_io)
        V(lambda e: e.tensor_scalar(s1, srci, 7, None, ALU.logical_shift_right), t_src)
        V(lambda e: e.tensor_scalar(s2, srci, 127, None, ALU.bitwise_and), chain=False)
        V(lambda e: e.tensor_scalar(v2, vi, 127, None, ALU.bitwise_and), chain=False)
        V(lambda e: e.tensor_scalar(vi, vi, 7, None, ALU.logical_shift_right))
        V(lambda e: e.scalar_tensor_tensor(key, s1, float(128 * VW), s2, ALU.mult, ALU.add))
        V(lambda e: e.scalar_tensor_tensor(key, v2, float(VW), key, ALU.mult, ALU.add))
        V(lambda e: e.scalar_tensor_tensor(key, vi, 128.0, key, ALU.mult, ALU.add))
        V(lambda e: e.tensor_tensor(v0[:, :], dsti[:, 0:1], iop[:, :], ALU.add), chain=False)
        V(lambda e: e.tensor_copy(slo[:, :], s2))
        t_sk = V(lambda e: e.tensor_copy(shi[:, :], s1))
        def sort_rows(a, b):
            for kbit in range(a, b):
                for jbit in range(kbit - 1, -1, -1):
                    stage(kbit, jbit)

        sort_rows(1, 10)

        cntp = ca([NT - 1])
        sta = ca([NT - 1])
        S = ca([NT])
        hq = ca([NQ])
        keep = ca([NQ])
        hp = ca([1])
        hp128 = ca([1])
        gpi = ca([1], U32)
        goff = ca([NQ], I32)
        qlast = ca([NT], I32)
        Di = ca([GE], I32)
        Df = ca([GE])
        drel = ca([NQ, 8], BF16)
        tmp = ca([NQ])
        for h in range(1, NT):
            t = A(lambda e, h=h: e.activation(junk, dsti, ACT.Sign, bias=ios[:, h - 1:h], scale=2.0,
                                              accum_out=cntp[:, h - 1:h]), t_dst, t_io, chain=True)
        t = P(lambda e: e.matmul(PS[3][:, 0:NT - 1], ones[:, :], cntp, start=True, stop=True), t, t_cst)
        V(lambda e: e.tensor_scalar(sta, PS[3][:, 0:NT - 1], -0.5, 64.0 * EC, ALU.mult, ALU.add), t)
        fl = big.rearrange("p a b -> p (a b)")[:, 0:(NT - 1) * (NG - 1)].rearrange("p (a b) -> p a b", b=NG - 1)
        V(lambda e: e.tensor_tensor(fl, bc(sta, 2, NG - 1), bc(iog, 1, NT - 1), ALU.is_ge))
        V(lambda e: e.tensor_reduce(S[:, 1:NT], fl, AX.X, ALU.add))
        V(lambda e: e.memset(S[:, 0:1], 0.0))
        V(lambda e: e.tensor_tensor(S[:, 1:NT], S[:, 1:NT], ioh, ALU.add))
        V(lambda e: e.tensor_scalar(big[:, 0, :], S[:, 1:NT], iop[:, 0:1], 0.0, ALU.is_le, ALU.add, accum_out=hp))
        V(lambda e: e.tensor_tensor(gpi, iop[:, :], hp, ALU.subtract))
        t_gp = V(lambda e: e.tensor_scalar(hp128, hp, 128.0, None, ALU.mult))
        s_D = sem("s_D")
        t_D = dma("pool", s_D, lambda e: e.indirect_dma_start(
            Di[0:NQ, :], None, dp_d.rearrange("(g c) -> g c", c=GE),
            bass.IndirectOffsetOnAxis(ap=gpi[0:NQ, 0:1], axis=0)), t_gp, t_dp)
        V(lambda e: e.tensor_tensor(big, bc(ioq, 2, NT - 1), bc(S[:, 1:NT], 1, NQ), ALU.is_ge))
        V(lambda e: e.tensor_reduce(hq, big, AX.X, ALU.add))
        V(lambda e: e.tensor_tensor(tmp, ioq, hq, ALU.subtract))
        t_goff = V(lambda e: e.tensor_scalar(goff, tmp, 128.0, float(LASTROW), ALU.mult, ALU.min))
        V(lambda e: e.tensor_tensor(keep[:, 1:NQ], hq[:, 1:NQ], hq[:, 0:NQ - 1], ALU.is_equal))
        V(lambda e: e.tensor_scalar(qlast[:, 0:NT - 1], S[:, 1:NT], -1.0, None, ALU.add))
        V(lambda e: e.memset(qlast[:, NT - 1:NT], NQ - 1))
        sort_rows(10, 11)
        srt, same = cur
        V(lambda e: e.memset(same[:, 0:1], 0.0))
        V(lambda e: e.tensor_tensor(same[:, 1:EC + 1], srt[:, 1:EC + 1], srt[:, 0:EC], ALU.is_equal))
        V(lambda e: e.tensor_tensor_scan(acnt[:, :], same[:, 0:EC], ones[:, 0:1].broadcast_to([128, EC]), 0.0,
                                         ALU.mult, ALU.add))
        aidx = srt[:, 0:EC].bitcast(U32)
        t_idx = V(lambda e: e.scalar_tensor_tensor(aidx, same[:, 1:EC + 1], float(1 << 24), srt[:, 0:EC],
                                                   ALU.mult, ALU.add))
        s_A = [sem(f"s_A{i}") for i in range(4)]
        t_A = [None] * 4
        done = [0]

        def scatter(n):
            for c in range(done[0], min(done[0] + n, E0)):
                t_A[c % 4] = dma("pool", s_A[c % 4], lambda e, c=c: e.indirect_dma_start(
                    a_d.rearrange("(a b) -> a b", b=1), bass.IndirectOffsetOnAxis(ap=aidx[:, c:c + 1], axis=0),
                    acnt[:, c:c + 1], None, bounds_check=NA - 1, oob_is_err=False), t_idx, t_az)
            done[0] = min(done[0] + n, E0)

        t_Df = V(lambda e: e.tensor_scalar(Df[0:NQ, :], Di[0:NQ, :], hp128[0:NQ, 0:1], None, ALU.subtract), t_D)
        Dr = Df[0:NQ, :].rearrange("q (p r) -> q r p", r=8)
        t_dr = []
        for hf in range(2):
            for r in range(4):
                t = P(lambda e, hf=hf, r=r: e.transpose(PS[4 + hf][:, r * NQ:(r + 1) * NQ], Dr[:, 4 * hf + r, :],
                                                        ident[0:NQ, 0:NQ]), t_Df)
            t_dr.append(V(lambda e, hf=hf: e.tensor_copy(
                drel[:, :, 4 * hf:4 * hf + 4], PS[4 + hf][:, 0:4 * NQ].rearrange("p (r q) -> p q r", q=NQ)), t))

        def ln_stats(t, *after):
            V(lambda e: e.bn_stats(st6[:, t, :], X[:, t, :]), *after)
            return V(lambda e: e.bn_aggr(mv[:, t, :], st6[:, t, :]))

        def ln_scale(a, b, after):
            k = A(lambda e: e.activation(rs[:, a:b], mv[:, a:b, 1], ACT.Sqrt, bias=epsc[:, 0:1]), after)
            V(lambda e: e.reciprocal(rs[:, a:b], rs[:, a:b]), k)
            return ln_shift(a, b)

        def ln_shift(a, b):
            return V(lambda e: e.scalar_tensor_tensor(nm[:, a:b], mv[:, a:b, 0], -1.0, rs[:, a:b], ALU.mult, ALU.mult))

        def ln_apply(t, dest, *after):
            return A(lambda e: e.activation(dest, X[:, t, :], ACT.Identity, bias=nm[:, t:t + 1], scale=rs[:, t:t + 1]),
                     *after)

        for t in range(NT):
            k = ln_stats(t, t_x)
        k = ln_scale(0, NT, k)
        t_xh0 = [ln_apply(t, XB[:, t, :], k) for t in range(NT)]

        ring = ca([RA, 512])
        DB = 3
        r1 = ca([DB, 512])
        lo = ca([DB, 8, 65], BF16)
        oh = ca([DB, 128, 8], BF16)
        store = Cut(early)([NQ, 65])
        agg = sb("agg", [128, NT, 65])
        s_ring = [sem(f"s_ring{i}") for i in range(RA)]
        attr_v = attr.rearrange("(a r) f -> a (r f)", r=8)
        for s in range(DB):
            t_lo1 = V(lambda e, s=s: e.memset(lo[:, s, :, 64:65], 1.0))
        ringb = ring.bitcast(BF16).rearrange("p a (r f two) -> p a r f two", two=2, f=64)
        r1b = r1.bitcast(BF16).rearrange("p a (r f two) -> p a r f two", two=2, f=64)
        ringf = ring.rearrange("p a (r f) -> p a r f", f=64)
        r1f = r1.rearrange("p a (r f) -> p a r f", f=64)
        t_mm, t_ld, t_st, t_r1 = {}, {}, {}, {}

        def load_attr(k):
            def go(e):
                r = e.value_load(goff[0:1, k:k + 1], min_val=0, max_val=LASTROW)
                return e.dma_start(ring[:, k % RA, :], attr_v[bass.ds(r, 128), :])
            t_ld[k] = dma("sp", s_ring[k % RA], go, t_goff, t_mm.get(k - RA))

        def split_attr(k):
            s = k % DB
            on = G if k % SPLIT == 0 else V
            t_r1[k] = on(lambda e: e.tensor_tensor(r1f[:, s, :, :], ringf[:, k % RA, :, :], ringb[:, k % RA, :, :, 1],
                                                   ALU.subtract), t_ld[k], t_mm.get(k - DB), chain=False)

        scatter(SC_PRE)
        for k in range(RA):
            load_attr(k)
        split_attr(0)
        for k in range(NQ):
            s, z = k % DB, PS[k % 3]
            if k + 1 < NQ:
                split_attr(k + 1)
            t1 = V(lambda e, k=k, s=s: e.tensor_tensor(oh[:, s, :, :], iob8[:, :, :], bc(drel[:, k, :], 1, 128),
                                                       ALU.is_equal), t_mm.get(k - DB), *t_dr, chain=False)
            t2 = V(lambda e, s=s: e.tensor_tensor(lo[:, s, :, 0:64], r1f[:, s, :, :], r1b[:, s, :, :, 1],
                                                  ALU.subtract), t_r1[k], t_lo1, t_mm.get(k - DB), chain=False)
            for r in range(8):
                P(lambda e, s=s, r=r, z=z: e.matmul(z[:, 0:65], oh[:, s, :, r], lo[:, s, r, :], start=(r == 0),
                                                    stop=False), t2, t1, t_st.get(k - 3), sig=False)
                P(lambda e, s=s, r=r, z=z: e.matmul(z[:, 0:64], oh[:, s, :, r], r1b[:, s, r, :, 1], start=False,
                                                    stop=False), t_r1[k], sig=False)
                t3 = P(lambda e, k=k, s=s, r=r, z=z: e.matmul(z[:, 0:64], oh[:, s, :, r], ringb[:, k % RA, r, :, 1],
                                                              start=False, stop=(r == 7)), t_ld[k], sig=(r == 7))
            t_mm[k] = t3
            scatter(SC_L0)
            if k + RA < NQ:
                load_attr(k + RA)
            j = k - 1
            for j in ([k - 1] if k else []) + ([k] if k == NQ - 1 else []):
                if j == 0:
                    t_st[j] = V(lambda e, z=PS[0]: e.tensor_copy(store[:, 0, :], z[:, 0:65]), t_mm[0])
                else:
                    t_st[j] = V(lambda e, j=j, z=PS[j % 3]: e.scalar_tensor_tensor(
                        store[:, j, :], store[:, j - 1, :], keep[:, j:j + 1], z[:, 0:65], ALU.mult, ALU.add), t_mm[j],
                        t_st[j - 1], chain=False)
        t_xb = [G(lambda e, t=t: e.tensor_tensor(X[:, t, :], X[:, t, :], b2g[:, :], ALU.add), t_xh0[t], t_w0)
                for t in range(NT)]
        V(lambda e: e.memset(agg[:, 0, 0:1], 0.0), t_az, t_zero)
        for h in range(NT):
            def pick(e, h=h):
                r = e.value_load(qlast[0:1, h:h + 1], min_val=0, max_val=NQ - 1)
                return e.tensor_copy(agg[:, h, :], store[:, bass.ds(r, 1), :].rearrange("p a b -> p (a b)"))
            V(pick)
        cn = sb("cn", [128, NT])
        V(lambda e: e.tensor_scalar(cn[:, :], agg[:, :, 64], 1.0, None, ALU.max))
        V(lambda e: e.reciprocal(cn[:, :], cn[:, :]))
        t_agg = V(lambda e: e.tensor_tensor(agg[:, :, 0:64], agg[:, :, 0:64], bc(cn[:, :], 2, 64), ALU.mult))
        t_l0 = t_agg

        ca = Cut()
        CT = ca([2, 3, 512])
        HT = ca([2, 4, 512])
        XT1 = ca([2, 512])
        lg = ca([NT, NX])
        cWn = ca([2, D])
        t_cwn = dma("sp", s_ld[4], lambda e: e.dma_start(cWn, cW.rearrange("(k p) n -> p k n", p=128)), t_l0)
        ohl = ca([4, 128, 8], BF16)
        ohh = ca([3, 16, NT], BF16)
        mlp_end = ca.at
        groups = [list(range(a, min(a + 4, NT))) for a in range(0, NT, 4)]
        t_ct, t_ht, t_tp, t_hmm, t_omm, t_x1, t_xh1, t_lg = {}, {}, {}, {}, {}, {}, {}, {}
        t_op = {}

        sorted_tok = {}

        def background():
            t_d = {}
            t_hh, oh_tok = {}, {}

            def count(c):
                for r in range(8):
                    t_d[c] = P(lambda e, c=c, r=r: e.matmul(
                        PS[7][:, 0:NT], ohl[:, c % 4, :, r], ohh[:, (c // 2) % 3, 8 * (c % 2) + r, :],
                        start=(c == 0 and r == 0), stop=(c == EC // 8 - 1 and r == 7)),
                        oh_tok[c], t_hh[c // 2], free.get(7), sig=(r == 7))

            for c in range(EC // 8):
                c2 = c // 2
                if c % 2 == 0:
                    t_hh[c2] = V(lambda e, c2=c2: e.tensor_tensor(
                        ohh[:, c2 % 3, :, :], bc(iob25[:, :], 1, 16), bc(shi[:, 16 * c2:16 * c2 + 16], 2, NT),
                        ALU.is_equal), t_d.get(c - 5), t_l0, chain=False)
                k1 = V(lambda e, c=c, s=s: e.tensor_tensor(
                    ohl[:, c % 4, :, :], iob8[:, :, :], bc(slo[:, 8 * c:8 * c + 8], 1, 128), ALU.is_equal),
                    t_d.get(c - 4), t_l0, chain=False)
                oh_tok[c] = k1
                if c > 1:
                    count(c - 2)
                if c % 2:
                    yield
            count(EC // 8 - 2)
            count(EC // 8 - 1)
            k = V(lambda e: e.tensor_copy(dinv[:, :], PS[7][:, 0:NT]), t_d[EC // 8 - 1])
            V(lambda e: e.tensor_tensor(dinv[:, NT - 1:NT], dinv[:, NT - 1:NT], padc[:, :], ALU.add))
            k = A(lambda e: e.activation(dinv[:, :], dinv[:, :], ACT.Sqrt), Token(q.sems["dve"], q.count["dve"]))
            sorted_tok["dinv"] = V(lambda e: e.reciprocal(dinv[:, :], dinv[:, :]), k)

        bg = background()

        def step_bg(n):
            for _ in range(n):
                next(bg, None)

        free = {}

        def turned(bank, tiles, src_of, parts, *after):
            n = 128 * len(tiles)
            for j, t in enumerate(tiles):
                k = P(lambda e, j=j, t=t: e.transpose(PS[bank][0:parts, j * 128:(j + 1) * 128], src_of(t), ident[:, :]),
                      free.get(bank), *after, sig=(j == len(tiles) - 1))
            return k, n

        def transposes(gi):
            g, s = groups[gi], gi % 2
            for c in range(3):
                pp, b = (64, 0) if c == 0 else (128, c % 2)
                src_of = (lambda t: agg[:, t, 0:64]) if c == 0 else (lambda t, c=c: XB[:, t, (c - 1) * 128:c * 128])
                k, n = turned(b, g, src_of, pp, t_agg, t_xh0[g[-1]])
                t_tp[(gi, c)] = k
                if c < 2:
                    t_ct[(gi, c)] = A(lambda e, b=b, c=c, pp=pp: e.activation(
                        CT[0:pp, s, c, 0:n], PS[b][0:pp, 0:n], ACT.Identity), k, t_hmm.get(gi - 2), t_l0)
                else:
                    t_ct[(gi, c)] = V(lambda e, b=b, c=c, pp=pp: e.tensor_copy(
                        CT[0:pp, s, c, 0:n], PS[b][0:pp, 0:n]), k, t_hmm.get(gi - 2), t_l0)
                free[b] = t_ct[(gi, c)]

        def hidden(gi):
            g, s = groups[gi], gi % 2
            n = 128 * len(g)
            for c in range(4):
                z = PS[3 + c % 2]
                w = (t_ht.get((gi, c - 2)) if c >= 2 else t_ht.get((gi - 1, c + 2)))
                for i, (lhs, pp) in enumerate([(w1a[:, c * 128:(c + 1) * 128], 64), (w1b[:, 0, c * 128:(c + 1) * 128], 128),
                                               (w1b[:, 1, c * 128:(c + 1) * 128], 128)]):
                    k = P(lambda e, lhs=lhs, pp=pp, i=i, z=z: e.matmul(z[:, 0:n], lhs, CT[0:pp, s, i, 0:n],
                                                                      start=(i == 0), stop=(i == 2)),
                          t_w0, w, t_ct[(gi, i)], sig=(i == 2))
                t_ht[(gi, c)] = A(lambda e, c=c, z=z: e.activation(HT[:, s, c, 0:n], z[:, 0:n], ACT.Relu,
                                                                   bias=b1g[:, c:c + 1]), k, t_omm.get(gi - 2))
                if c % 2:
                    step_bg(1)
            t_hmm[gi] = k

        def output(gi):
            g, s = groups[gi], gi % 2
            for j, t in enumerate(g):
                z = PS[2 + 3 * (t % 2)][:, 0:256]
                for c in range(4):
                    k = P(lambda e, j=j, c=c, z=z: e.matmul(z, HT[:, s, c, j * 128:(j + 1) * 128], w2g[:, c, :],
                                                            start=(c == 0), stop=(c == 3)), t_ht[(gi, c)],
                          t_x1.get(t - 2), sig=(c == 3))
                t_x1[t] = V(lambda e, t=t, z=z: e.tensor_tensor(X[:, t, :], X[:, t, :], z, ALU.add), k, t_xb[t])
                kk = ln_stats(t)
            t_omm[gi] = k
            kk = ln_scale(g[0], g[-1] + 1, kk)
            for t in g:
                t_xh1[t] = ln_apply(t, XB[:, t, :], t_tp[(gi, 2)], kk)

        def gate(gi):
            g = groups[gi]
            for c in range(2):
                k, n = turned(c, g, lambda t, c=c: XB[:, t, c * 128:(c + 1) * 128], 128, t_xh1[g[-1]])
                free[c] = t_lg[("c", gi, c)] = A(lambda e, c=c, n=n: e.activation(XT1[:, c, 0:n], PS[c][:, 0:n],
                                                                                  ACT.Identity), k,
                                                 t_lg.get(("m", gi - 1)), t_l0)
            for j, t in enumerate(g):
                z = PS[6][:, NX * j:NX * j + NX]
                for c in range(2):
                    k = P(lambda e, c=c, j=j, z=z: e.matmul(z, XT1[:, c, j * 128:(j + 1) * 128], gw[:, c, :],
                                                            start=(c == 0), stop=(c == 1)), t_lg[("c", gi, c)],
                          free.get(6), sig=(c == 1))
            t_lg[("m", gi)] = k
            free[6] = V(lambda e: e.tensor_tensor(lg[:, g[0]:g[-1] + 1, :],
                                                  PS[6][:, 0:NX * len(g)].rearrange("p (t x) -> p t x", x=NX),
                                                  bc(gb[:, :], 1, len(g)), ALU.add), k)

        ex = ca([NT, NX])
        mx = ca([NT, 8])
        mi = ca([NT, 8], U32)
        sm = ca([NT])
        mlp_end = ca.at

        def two_best(gi):
            a, b = groups[gi][0], groups[gi][-1] + 1
            V(lambda e: e.tensor_reduce(sm[:, a:b], lg[:, a:b, :], AX.X, ALU.max))
            k = V(lambda e: e.tensor_tensor(ex[:, a:b, :], lg[:, a:b, :], bc(sm[:, a:b], 2, NX), ALU.subtract))
            k = A(lambda e: e.activation(ex[:, a:b, :], ex[:, a:b, :], ACT.Exp), k)
            V(lambda e: e.tensor_reduce(sm[:, a:b], ex[:, a:b, :], AX.X, ALU.add), k)
            V(lambda e: e.reciprocal(sm[:, a:b], sm[:, a:b]))
            V(lambda e: e.tensor_tensor(ex[:, a:b, :], ex[:, a:b, :], bc(sm[:, a:b], 2, NX), ALU.mult))
            for t in range(a, b):
                V(lambda e, t=t: e.max(mx[:, t, :], ex[:, t, :]), chain=(t == a))
            for t in range(a, b):
                V(lambda e, t=t: e.max_index(mi[:, t, :], mx[:, t, :], ex[:, t, :]), chain=(t == a))

        transposes(0)
        for gi in range(len(groups) + 2):
            if gi + 1 < len(groups):
                transposes(gi + 1)
            if gi < len(groups):
                hidden(gi)
            if 0 < gi <= len(groups):
                output(gi - 1)
            if gi > 1:
                gate(gi - 2)
            if gi > 2:
                two_best(gi - 3)
            scatter(SC_MLP)
        two_best(len(groups) - 1)
        t_x1all = V(lambda e: e.memset(rs[:, 0:1], 0.0))

        s_out = sem("s_out")

        def finish(tok):
            dma("sp", s_out, lambda e: e.dma_start(out[0:(NT - 1) * 128, :].rearrange("(t p) d -> p t d", p=128),
                                                   X[:, 0:NT - 1, :]), tok)
            return dma("sp", s_out, lambda e: e.dma_start(out[(NT - 1) * 128:N, :], X[0:N - (NT - 1) * 128, NT - 1, :]), tok)

        def stages_after():
            ca = Cut(mlp_end)
            sm2 = ca([NT])
            idf = ca([NT, 2])
            M = ca([NT * 2, NX])
            pos = ca([NT * 2, NX])
            tot = ca([NT * 2, NX])
            inc = ca([NX, NT * 2])
            one50 = ca([NT * 2])
            til = ca([NX, NT])
            nt = ca([NX])
            end = ca([NX])
            base = ca([NX])
            slot = ca([NT * 2])
            cmp = ca([NS, NX])
            ei = sb("ei", [128, NS], I32)
            sidx = sb("sidx", [128, NT * 2], U32)
            V(lambda e: e.tensor_tensor(sm2, mx[:, :, 0], mx[:, :, 1], ALU.add))
            V(lambda e: e.reciprocal(sm2, sm2))
            t_top = V(lambda e: e.tensor_tensor(top[:, :, :], mx[:, :, 0:2], bc(sm2, 2, 2), ALU.mult))
            V(lambda e: e.tensor_copy(idf, mi[:, :, 0:2]))
            V(lambda e: e.scalar_tensor_tensor(idf[:, NT - 1, :], bc(padc[:, 0], 1, 2), 100.0, idf[:, NT - 1, :], ALU.mult, ALU.add))
            idv = idf.rearrange("p t k -> p (t k)")
            t_M = V(lambda e: e.tensor_tensor(M, bc(io16[:, :], 1, NT * 2), bc(idv, 2, NX), ALU.is_equal))
            Mf = M.rearrange("p a e -> p (a e)")
            for (b, lhs) in ((0, tri), (2, ones)):
                P(lambda e, b=b, lhs=lhs: e.matmul(PS[b][:, 0:400], lhs[:, :], Mf[:, 0:400], start=True, stop=True), t_M)
                kp = P(lambda e, b=b, lhs=lhs: e.matmul(PS[b + 1][:, 0:400], lhs[:, :], Mf[:, 400:800], start=True, stop=True))
            posf, totf = pos.rearrange("p a e -> p (a e)"), tot.rearrange("p a e -> p (a e)")
            for b in range(2):
                V(lambda e, b=b: e.tensor_copy(posf[:, 400 * b:400 * b + 400], PS[b][:, 0:400]), kp)
                V(lambda e, b=b: e.tensor_copy(totf[:, 400 * b:400 * b + 400], PS[2 + b][:, 0:400]))
            V(lambda e: e.memset(one50, 1.0))
            for x_ in range(NX):
                V(lambda e, x_=x_: e.tensor_tensor_scan(inc[:, x_, :], one50, tot[:, :, x_], 0.0, ALU.mult, ALU.add))
            V(lambda e: e.tensor_tensor(til, bc(inc[:, :, NT * 2 - 1], 2, NT), bc(io25[:, :], 1, NX), ALU.is_gt))
            V(lambda e: e.tensor_reduce(nt, til, AX.X, ALU.add))
            V(lambda e: e.tensor_tensor_scan(end, one50[:, 0:NX], nt, 0.0, ALU.mult, ALU.add))
            V(lambda e: e.tensor_tensor(base, end, nt, ALU.subtract))
            V(lambda e: e.tensor_scalar(base, base, 128.0, None, ALU.mult))
            V(lambda e: e.tensor_tensor(cmp, bc(io64[:, :], 2, NX), bc(end, 1, NS), ALU.is_ge))
            V(lambda e: e.tensor_reduce(io64f[:, :], cmp, AX.X, ALU.add))
            t_ei = V(lambda e: e.tensor_scalar(ei[:, :], io64f[:, :], float(NX - 1), None, ALU.min))
            V(lambda e: e.tensor_tensor(pos, pos, inc.rearrange("p e a -> p a e"), ALU.add))
            V(lambda e: e.tensor_tensor(pos, pos, tot, ALU.subtract))
            V(lambda e: e.tensor_tensor(pos, pos, bc(base, 1, NT * 2), ALU.add))
            V(lambda e: e.tensor_tensor(pos, pos, M, ALU.mult))
            V(lambda e: e.tensor_reduce(slot, pos, AX.X, ALU.add))
            V(lambda e: e.tensor_copy(gidx[:, :], slot))
            V(lambda e: e.scalar_tensor_tensor(slot[:, NT * 2 - 2:NT * 2], bc(padc[:, 0], 1, 2), 100000.0,
                                               slot[:, NT * 2 - 2:NT * 2], ALU.mult, ALU.add))
            t_slot = V(lambda e: e.tensor_copy(sidx[:, :], slot))

            scatter(SC_GAP)
            s_sc = sem("s_sc")
            for a in range(NT * 2):
                t_sc = dma("pool", s_sc, lambda e, a=a: e.indirect_dma_start(
                    xs_d, bass.IndirectOffsetOnAxis(ap=sidx[:, a:a + 1], axis=0), XB[:, a // 2, :], None,
                    bounds_check=NS * 128 - 1, oob_is_err=False), t_slot, t_zero)

            while next(bg, 1) is None:
                pass
            for a in range(2):
                for b in range(2):
                    k = P(lambda e, a=a, b=b: e.transpose(PS[7][:, b * 256 + a * 128:b * 256 + a * 128 + 128],
                                                          cWn[:, a, b * 128:(b + 1) * 128], ident[:, :]), t_w1, t_cst, t_cwn, sorted_tok["dinv"])
            t_cw = A(lambda e: e.activation(cWT[:, :, :], PS[7][:, :].rearrange("p (a b) -> p a b", b=256), ACT.Identity), k)
            free[7] = t_cw

            ca = Cut(mlp_end)
            NW = 3
            W1 = ca([NW, 2, HID])
            W2 = ca([NW, 2, HID])
            yb = ca([4, D])
            W3 = Cut(3072)([NW, 4, D])
            ca = Cut(0)
            xsb = ca([4, D])
            xT = ca([2, D])
            hs = ca([HID])
            hid = ca([2, HID])
            assert ca.at <= 3072
            s_w = [[sem(f"s_w{j}{i}") for i in range(NW)] for j in range(3)]
            s_xs = [sem(f"s_xs{i}") for i in range(4)]
            s_ys = sem("s_ys")
            v1 = ew1.rearrange("e (k p) n -> p (e k) n", p=128)
            v2 = ew2.rearrange("e (k p) n -> p (e k) n", p=128)
            v3 = ew3.rearrange("e (k p) n -> p (e k) n", p=128)
            t_wl, t_xl, tB, tA, tC, tD, tx, thid, thT, tyb, tst = ({} for _ in range(11))
            e_reg = {}

            def loads(i):
                s = i % NW

                def w(v, W, n, first):
                    def go(e):
                        if first:
                            e_reg[i] = e.value_load(ei[0:1, i:i + 1], min_val=0, max_val=NX - 1)
                        return e.dma_start(W[:, s, :, :], v[:, bass.ds(e_reg[i] * n, n), :])
                    return go
                a = dma("sp", s_w[0][s], w(v1, W1, 2, True), t_ei, t_slot, tB.get(i - NW))
                b = dma("sp", s_w[1][s], w(v2, W2, 2, False), tB.get(i - NW))
                c = dma("sp", s_w[2][s], w(v3, W3, 4, False), tD.get(i - NW))
                t_wl[i] = (a, b, c)

            def load_x(i):
                t_xl[i] = dma("sp", s_xs[i % 4], lambda e: e.dma_start(xsb[:, i % 4, :], xs_d[i * 128:(i + 1) * 128, :]),
                              t_sc, tA.get(i - 4))

            def stA(i):
                for c in range(2):
                    tA[i] = P(lambda e, c=c: e.transpose(PS[4][:, c * 128:(c + 1) * 128],
                                                         xsb[:, i % 4, c * 128:(c + 1) * 128], ident[:, :]),
                              t_xl[i], tx.get(i - 1), sig=(c == 1))
                tx[i] = A(lambda e: e.activation(xT[:, i % 2, :], PS[4][:, 0:256], ACT.Identity), tA[i], tB.get(i - 2))

            def stB(i):
                s = i % NW
                for (b, W, j) in ((0, W1, 0), (2, W2, 1)):
                    for h in range(4):
                        for c in range(2):
                            k = P(lambda e, b=b, W=W, c=c, h=h: e.matmul(
                                PS[b + i % 2][:, h * 128:(h + 1) * 128], W[:, s, c, h * 128:(h + 1) * 128],
                                xT[:, i % 2, c * 128:(c + 1) * 128], start=(c == 0), stop=(c == 1)),
                                tx[i], t_wl[i][j], thid.get(i - 2), sig=(c == 1 and h == 3))
                    if j == 0:
                        kh = k
                tB[i] = k
                ks = A(lambda e: e.activation(hs, PS[i % 2][:, :], ACT.Silu), kh, thid.get(i - 1))
                thid[i] = V(lambda e: e.tensor_tensor(hid[:, i % 2, :], hs, PS[2 + i % 2][:, :], ALU.mult), ks, k,
                            tD.get(i - 2))

            def stD(i):
                s = i % NW
                for c in range(4):
                    tD[i] = P(lambda e, c=c: e.matmul(PS[6][:, 0:256], hid[:, i % 2, c * 128:(c + 1) * 128], W3[:, s, c, :],
                                                      start=(c == 0), stop=(c == 3)), thid[i], t_wl[i][2],
                              tyb.get(i - 1), sig=(c == 3))
                tyb[i] = V(lambda e: e.tensor_copy(yb[:, i % 4, :], PS[6][:, 0:256]), tD[i], tst.get(i - 4))
                tst[i] = dma("sp", s_yb[i % 4], lambda e: e.dma_start(ys_d[i * 128:(i + 1) * 128, :], yb[:, i % 4, :]),
                             tyb[i])

            s_yb = [sem(f"s_yb{i}") for i in range(4)]
            for i in range(min(NW, NS)):
                loads(i)
            for i in range(4):
                load_x(i)
            stA(0)
            for i in range(NS + 1):
                if i + 1 < NS:
                    stA(i + 1)
                if i + 4 < NS:
                    load_x(i + 4)
                if i < NS:
                    stB(i)
                if i:
                    stD(i - 1)
                    if i - 1 + NW < NS:
                        loads(i - 1 + NW)
                scatter(SC_MOE)
            scatter(E0)

            ca = Cut(0)
            RG = 16
            gr = ca([RG, D])
            s_g = [sem(f"s_g{i}") for i in range(RG)]
            t_g, t_c2 = {}, {}

            def fetch(a):
                t_g[a] = dma("pool", s_g[a % RG], lambda e: e.indirect_dma_start(
                    gr[:, a % RG, :], None, ys_d, bass.IndirectOffsetOnAxis(ap=gidx[:, a:a + 1], axis=0)),
                    tst[NS - 1], tst[NS - 2], tst[NS - 3], tst[NS - 4], t_c2.get(a - RG), tD[NS - 1])

            for a in range(RG):
                fetch(a)
            dv = ca([128])
            vrow = ca([128])
            vall = ca([NV])
            vc = ca([NV, 128], BF16)
            t_v = G(lambda e: e.iota(vall, pattern=[[128, NV]], base=0, channel_multiplier=1,
                                     allow_small_or_imprecise_dtypes=True), tD[NS - 1])
            k = V(lambda e: e.tensor_scalar(dv, ident[:, :], v0[:, 0:1], None, ALU.mult), tD[NS - 1])
            k = P(lambda e: e.matmul(PS[6][:, 0:128], ones[:, :], dv, start=True, stop=True), k, tyb[NS - 1])
            V(lambda e: e.tensor_copy(vrow, PS[6][:, 0:128]), k)
            V(lambda e: e.tensor_tensor(vc, bc(vall, 2, 128), bc(vrow, 1, NV), ALU.is_ge), t_v)
            V(lambda e: e.tensor_reduce(dv[:, 0:NV], vc, AX.X, ALU.add))
            V(lambda e: e.tensor_tensor(vall, vall, dv[:, 0:NV], ALU.subtract))
            V(lambda e: e.tensor_scalar(vall, vall, 1.0, 0.0, ALU.add, ALU.max))
            t_vidx = V(lambda e: e.tensor_scalar(vidx[:, :], vall, float(N - 1), None, ALU.min))
            for t in range(NT):
                for j in range(2):
                    a = 2 * t + j
                    t_c2[a] = V(lambda e, t=t, j=j, a=a: e.scalar_tensor_tensor(
                        X[:, t, :], gr[:, a % RG, :], top[:, t, j:j + 1], X[:, t, :], ALU.mult, ALU.add), t_g[a])
                    if a + RG < NT * 2:
                        fetch(a + RG)
                kk = ln_stats(t)
            ln_scale(0, NT, kk)
            V(lambda e: e.tensor_tensor(rs[:, :], rs[:, :], dinv[:, :], ALU.mult), sorted_tok["dinv"])
            kx = ln_shift(0, NT)
            s_yt = sem("s_yt")
            for t in range(NT):
                kk = ln_apply(t, XB[:, t, :], t_sc, kx)
                t_yt = dma("sp", s_yt, lambda e, t=t: e.dma_start(yt_d[t * 128:(t + 1) * 128, :], XB[:, t, :]), kk)

            ca = Cut(0)
            CT2 = ca([2, 2, 512])
            yv = ca([NV, D])
            yr = ca([NV, D])
            yl = ca([NV, D], BF16)
            NAB = 3
            ab = ca([NAB, VW], F16)
            cw = ca
            yhb = yv.bitcast(BF16).rearrange("p j (f two) -> p j f two", two=2)
            yrb = yr.bitcast(BF16).rearrange("p j (f two) -> p j f two", two=2)
            s_yv = [sem(f"s_yv{i}") for i in range(NV)]
            s_ab = [sem(f"s_ab{i}") for i in range(NAB)]
            t_yv, t_yr, t_yl, t_ab, t_ap, t_ev = {}, {}, {}, {}, {}, {}
            for j in range(NV):
                t_yv[j] = dma("pool", s_yv[j], lambda e, j=j: e.indirect_dma_start(
                    yv[:, j, :], None, yt_d, bass.IndirectOffsetOnAxis(ap=vidx[:, j:j + 1], axis=0)), t_yt, t_vidx)
                t_yr[j] = V(lambda e, j=j: e.tensor_tensor(yr[:, j, :], yv[:, j, :], yhb[:, j, :, 1], ALU.subtract), t_yv[j])
                t_yl[j] = V(lambda e, j=j: e.tensor_tensor(yl[:, j, :], yr[:, j, :], yrb[:, j, :, 1], ALU.subtract))

            def load_a(t):
                t_ab[t] = dma("sp", s_ab[t % NAB], lambda e: e.dma_start(
                    ab[:, t % NAB, :], a_d[t * 128 * VW:(t + 1) * 128 * VW].rearrange("(p c) -> p c", c=VW)),
                    *t_A, tD[NS - 1], t_ap.get(t - NAB))

            def apply(t):
                z = PS[5 + t % 2][:, 0:256]
                for j in range(NV):
                    lhs = ab[:, t % NAB, j * 128:(j + 1) * 128]
                    for i, (rhs, tok) in enumerate(((yhb[:, j, :, 1], t_yv[j]), (yrb[:, j, :, 1], t_yr[j]),
                                                    (yl[:, j, :], t_yl[j]))):
                        last_ = j == NV - 1 and i == 2
                        t_ap[t] = P(lambda e, lhs=lhs, rhs=rhs, z=z, i=i, j=j, last_=last_: e.matmul(
                            z, lhs, rhs, start=(i + j == 0), stop=last_), t_ab[t], tok, t_ev.get(t - 2), sig=last_)
                t_ev[t] = V(lambda e: e.tensor_tensor(XB[:, t, :], XB[:, t, :], z, ALU.add), t_ap[t], t_yt)
                if t + NAB < NT:
                    load_a(t + NAB)

            for t in range(NAB):
                load_a(t)

            ca = Cut(2048)
            XT3 = ca([2, 2, 512])
            HT3 = ca([8, 512])
            wrow = ca([NT, 128])
            junk2 = ca([NT * 128], BF16)
            wsum = cw([NT])
            wm = cw([NT])
            jk = cw([D])
            cz = cw([2, D])
            t_s3, t_ctm, t_x3, t_xt, t_hm, t_h3, t_ob, t_y = ({} for _ in range(8))
            t_c1, t_om3, t_k3 = {}, {}, {}

            def conv(gi):
                g, s = groups[gi], gi % 2
                for t in g:
                    k = A(lambda e, t=t: e.activation(XB[:, t, :], XB[:, t, :], ACT.Identity, scale=dinv[:, t:t + 1]), t_ev[t])
                n = 128 * len(g)
                for c in range(2):
                    for j, t in enumerate(g):
                        kk = P(lambda e, c=c, j=j, t=t: e.transpose(PS[c][:, j * 128:(j + 1) * 128],
                                                                    XB[:, t, c * 128:(c + 1) * 128], ident[:, :]),
                               k, t_c1.get((gi - 1, c)), sig=(j == len(g) - 1))
                    t_c1[(gi, c)] = A(lambda e, c=c: e.activation(CT2[:, s, c, 0:n], PS[c][:, 0:n], ACT.Identity), kk,
                                      t_ctm.get(gi - 2))
                for j, t in enumerate(g):
                    z = PS[2 + 5 * (t % 2)][:, 0:256]
                    for c in range(2):
                        kk = P(lambda e, c=c, j=j, z=z: e.matmul(z, CT2[:, s, c, j * 128:(j + 1) * 128], cWT[:, c, :],
                                                                 start=(c == 0), stop=(c == 1)), t_c1[(gi, c)], t_cw,
                               t_x3.get(t - 2), sig=(c == 1))
                    kb = V(lambda e, t=t, z=z: e.tensor_tensor(cz[:, t % 2, :], z, cbr[:, :], ALU.add), kk)
                    t_x3[t] = V(lambda e, t=t: e.scalar_tensor_tensor(X[:, t, :], cz[:, t % 2, :], 0.0, X[:, t, :], ALU.max, ALU.add))
                    ks_ = ln_stats(t)
                t_ctm[gi] = kk
                ks_ = ln_scale(g[0], g[-1] + 1, ks_)
                for t in g:
                    kh = ln_apply(t, XB[:, t, :], t_c1[(gi, 1)], ks_)
                    V(lambda e, t=t: e.tensor_tensor_reduce(out=jk, in0=XB[:, t, :], in1=wrr[:, :], scale=1.0, scalar=0.0,
                                                            op0=ALU.mult, op1=ALU.add, accum_out=wsum[:, t:t + 1]), kh)
                    k = V(lambda e, t=t: e.tensor_tensor(X[:, t, :], X[:, t, :], XB[:, t, :], ALU.add))
                t_k3[gi] = k

            def turn3(gi):
                g, s = groups[gi], gi % 2
                n = 128 * len(g)
                for c in range(2):
                    for j, t in enumerate(g):
                        kk = P(lambda e, c=c, j=j, t=t: e.transpose(PS[c][:, j * 128:(j + 1) * 128],
                                                                    XB[:, t, c * 128:(c + 1) * 128], ident[:, :]),
                               t_k3[gi], t_c1[(len(groups) - 1, c)], t_xt.get((gi - 1, c)), sig=(j == len(g) - 1))
                    t_xt[(gi, c)] = A(lambda e, c=c: e.activation(XT3[:, s, c, 0:n], PS[c][:, 0:n], ACT.Identity), kk,
                                      t_hm.get(gi - 2))

            def ffn(gi):
                g, s = groups[gi], gi % 2
                n = 128 * len(g)
                for c in range(8):
                    z = PS[3 + c % 2]
                    for i in range(2):
                        k = P(lambda e, c=c, i=i, z=z: e.matmul(z[:, 0:n], f1[:, i, c * 128:(c + 1) * 128], XT3[:, s, i, 0:n],
                                                                start=(i == 0), stop=(i == 1)), t_xt[(gi, i)],
                              t_h3.get((gi, c - 2)) if c >= 2 else t_h3.get((gi - 1, 7)), sig=(i == 1))
                    t_h3[(gi, c)] = A(lambda e, c=c, z=z: e.activation(HT3[:, c, 0:n], z[:, 0:n], ACT.Gelu_apprx_tanh,
                                                                       bias=fb1c[:, c:c + 1]), k, t_om3.get(gi - 1))
                t_hm[gi] = k
                for j, t in enumerate(g):
                    z = PS[5 + t % 2][:, 0:256]
                    for c in range(8):
                        k = P(lambda e, c=c, j=j, z=z: e.matmul(z, HT3[:, c, j * 128:(j + 1) * 128], f2[:, c, :],
                                                                start=(c == 0), stop=(c == 7)), t_h3[(gi, c)],
                              t_y.get(t - 2), sig=(c == 7))
                    t_y[t] = V(lambda e, t=t, z=z: e.tensor_tensor(XB[:, t, :], z, fb2r[:, :], ALU.add), k, t_xt[(gi, 1)])
                t_om3[gi] = k

            for gi in range(len(groups) + 1):
                if gi < len(groups):
                    for t in groups[gi]:
                        apply(t)
                if gi:
                    conv(gi - 1)
            t_sp = t_ap[NT - 1]
            turn3(0)
            V(lambda e: e.tensor_scalar(wsum, wsum, brr[:, 0:1], None, ALU.add))
            V(lambda e: e.tensor_copy(wm, wsum))
            V(lambda e: e.tensor_scalar(jk[:, 0:1], padc[:, :], -1.0, 1.0, ALU.mult, ALU.add))
            V(lambda e: e.tensor_scalar(jk[:, 1:2], padc[:, :], -3.0e38, None, ALU.mult))
            k = V(lambda e: e.scalar_tensor_tensor(wm[:, NT - 1:NT], wm[:, NT - 1:NT], jk[:, 0:1], jk[:, 1:2], ALU.mult, ALU.add))
            k = P(lambda e: e.transpose(PS[7][0:NT, 0:128], wm, ident[:, :]), k, t_cw)
            wts = jk.rearrange("p (a b) -> p a b", b=128)[0:NT, 1, :]
            k = V(lambda e: e.tensor_copy(wts, PS[7][0:NT, 0:128]), k)
            s_wt = sem("s_wt")
            s_wb = sem("s_wb")
            k = dma("sp", s_wt, lambda e: e.dma_start(wt_d.rearrange("(t p) -> t p", p=128), wts), k)
            k = dma("sp", s_wb, lambda e: e.dma_start(wrow.rearrange("p a b -> p (a b)"),
                                                      wt_d.rearrange("(a n) -> a n", a=1).broadcast_to([128, NT * 128])), k,
                    t_sp)
            wrf = wrow.rearrange("p a b -> p (a b)")
            ra = sb("ra", [128, 3, NT])
            V(lambda e: e.memset(ra[:, :, :], 0.0))

            def rank(t):
                if t:
                    V(lambda e: e.tensor_scalar(junk2[:, 0:t * 128], wrf[:, 0:t * 128], wm[:, t:t + 1], 0.0, ALU.is_ge, ALU.add,
                                                accum_out=ra[:, 0, t:t + 1]), k)
                V(lambda e: e.tensor_scalar(junk2[:, t * 128:NT * 128], wrf[:, t * 128:NT * 128], wm[:, t:t + 1], 0.0,
                                            ALU.is_gt, ALU.add, accum_out=ra[:, 1, t:t + 1]), k)
                V(lambda e: e.scalar_tensor_tensor(junk2[:, 0:128], wrow[:, t, :], wm[:, t:t + 1], low[:, :], ALU.is_equal,
                                                   ALU.mult, accum_out=ra[:, 2, t:t + 1]))

            per = (NT + len(groups) - 1) // len(groups)
            for gi in range(len(groups)):
                if gi + 1 < len(groups):
                    turn3(gi + 1)
                ffn(gi)
                for t in range(per * gi, min(per * gi + per, NT)):
                    rank(t)
            V(lambda e: e.tensor_tensor(ra[:, 0, :], ra[:, 0, :], ra[:, 1, :], ALU.add))
            V(lambda e: e.tensor_tensor(ra[:, 0, :], ra[:, 0, :], ra[:, 2, :], ALU.add))
            V(lambda e: e.tensor_scalar(ra[:, 0, :], ra[:, 0, :], float(KEEP), None, ALU.is_lt))
            V(lambda e: e.tensor_tensor(wsel[:, :], ra[:, 0, :], wsum, ALU.mult))
            for t in range(NT):
                kk = V(lambda e, t=t: e.scalar_tensor_tensor(X[:, t, :], XB[:, t, :], wsel[:, t:t + 1], X[:, t, :],
                                                             ALU.mult, ALU.add))
            return kk

        io64f = sb("io64f", [128, NS])
        last = stages_after()
        finish(last)

        block = ctx.enter_context(nc.Block())

        @block.sync
        def _(e):
            q.run("sp", e)
            for t in q.landed():
                e.wait_ge(t.sem, t.val)

        @block.gpsimd
        def _(e):
            q.run("pool", e)

        @block.scalar
        def _(e):
            q.run("act", e)

        @block.vector
        def _(e):
            q.run("dve", e)

        @block.tensor
        def _(e):
            q.run("pe", e)


_INS = ["x", "src", "dst", "edge_attr_64", "L0_gnn_W1", "L0_gnn_b1", "L0_gnn_W2", "L0_gnn_b2", "L0_ffn_gate_w",
        "L0_ffn_gate_b", "L0_ffn_w1", "L0_ffn_w2", "L0_ffn_w3", "L1_gnn_W", "L1_gnn_b", "L1_ffn_attention_mask",
        "L1_ffn_wr", "L1_ffn_br", "L1_ffn_w1", "L1_ffn_b1", "L1_ffn_w2", "L1_ffn_b2"]
_OUTS = [((3125, 256), "float32")]


def kernel(**inputs):
    import numpy as _np
    import concourse.bacc as _bacc
    from concourse import mybir as _mybir
    from concourse.bass_utils import run_bass_kernel_spmd as _run

    nc = _bacc.Bacc("TRN2", target_bir_lowering=False, num_devices=1)
    arrays, args = {}, []
    for name in _INS:
        a = _np.ascontiguousarray(inputs[name])
        arrays[f"in_{name}_dram"] = a
        args.append(nc.dram_tensor(f"in_{name}_dram", a.shape, _mybir.dt.from_np(a.dtype), kind="ExternalInput").ap())
    for i, (shape, dtype) in enumerate(_OUTS):
        args.append(nc.dram_tensor(f"out_{i}_dram", shape, _mybir.dt.from_np(_np.dtype(dtype)), kind="ExternalOutput").ap())
    program(nc, *args)
    r = _run(nc, [arrays], core_ids=[0])
    return r.results[0]["out_0_dram"]
```

```python
from contextlib import ExitStack

import concourse.bass as bass
from concourse import mybir

ALU = mybir.AluOpType
ACT = mybir.ActivationFunctionType
AX = mybir.AxisListType
F32 = mybir.dt.float32
BF16 = mybir.dt.bfloat16
F16 = mybir.dt.float16
I32 = mybir.dt.int32
U32 = mybir.dt.uint32

SPLIT, SC_PRE, SC_L0, SC_MLP, SC_GAP, SC_MOE, TAIL = 1000, 20, 2, 18, 33, 8, 8

N = 3125
NT = 25
D = 256
NE = 100000
E0 = 782
EL = NE - 127 * E0
EC = 784
GE = 1024
NG = 98
NQ = NG + NT - 1
LASTROW = (NE - GE) // 8
PADS = NG * GE - NE
RA = 8
NX = 16
HID = 512
NS = 64
SC = 1024
NV = 26
VW = NV * 128
NA = NT * 128 * VW
PADNODE = 4095
YS = 1024.0
KEEP = 1561
NR = 13
LNEPS = 1e-5


class Token:
    def __init__(self, sem, val):
        self.sem, self.val = sem, val


class Queues:

    def __init__(self, sems):
        self.sems = sems
        self.count = {e: 0 for e in sems}
        self.todo = {e: [] for e in ("sp", "act", "pool", "dve", "pe")}
        self.dcount = {}
        self.last = {}

    def put(self, eng, fn, *after, sig=True, chain=None):
        if chain is None:
            chain = eng == "dve"
        after = [a for a in after if a is not None]
        if chain and self.count[eng]:
            after.append(Token(self.sems[eng], self.count[eng]))
        if sig:
            self.count[eng] += 1
        self.todo[eng].append((fn, after, (self.sems[eng], 1) if sig else None))
        return Token(self.sems[eng], self.count[eng])

    def ahead(self, eng, fn, *after):
        self.todo[eng].append((fn, list(after), None))

    def dma(self, eng, sem, fn, *after):
        after = [a for a in after if a is not None]
        self.dcount[sem.name] = self.dcount.get(sem.name, 0) + 16
        self.todo[eng].append((fn, after, (sem, 16)))
        self.last[sem.name] = Token(sem, self.dcount[sem.name])
        return self.last[sem.name]

    def dma_if(self, eng, flag, moves, *after):
        toks = []
        for sem, _ in moves:
            self.dcount[sem.name] = self.dcount.get(sem.name, 0) + 16
            toks.append(Token(sem, self.dcount[sem.name]))
            self.last[sem.name] = toks[-1]

        def go(e):
            with e.If(flag(e)):
                for sem, start in moves:
                    start(e).then_inc(sem, 16)
            with e.Else():
                for sem, _ in moves:
                    e.sem_inc(sem, 16)
        self.todo[eng].append((go, [a for a in after if a is not None], None))
        return toks

    def landed(self):
        return list(self.last.values())

    def run(self, eng, e):
        seen = {}
        for fn, after, inc in self.todo[eng]:
            for t in after:
                if seen.get(t.sem.name, 0) < t.val:
                    e.wait_ge(t.sem, t.val)
                    seen[t.sem.name] = t.val
            ins = fn(e)
            if inc:
                ins.then_inc(*inc)


def program(nc, x, src, dst, attr, gW1, gb1, gW2, gb2, gate_w, gate_b, ew1, ew2, ew3,
            cW, cb, amask, wr, br, fw1, fb1, fw2, fb2, out):
    ctx = ExitStack()
    with ctx:
        def sb(name, shape, dt=F32):
            return ctx.enter_context(nc.sbuf_tensor(name, shape, dt))

        def sem(name):
            return ctx.enter_context(nc.semaphore(name))

        PS = [ctx.enter_context(nc.psum_tensor(f"ps{i}", [128, 512], F32)) for i in range(8)]
        q = Queues({e: sem("s_" + e) for e in ("act", "pool", "dve", "pe")})
        put, dma = q.put, q.dma

        def V(fn, *after, **k):
            return put("dve", fn, *after, **k)

        def A(fn, *after, **k):
            return put("act", fn, *after, **k)

        def P(fn, *after, **k):
            return put("pe", fn, *after, **k)

        def G(fn, *after, **k):
            return put("pool", fn, *after, **k)

        X = sb("X", [128, NT, D])
        XB = sb("XB", [128, NT, D])
        ident = sb("ident", [128, 128])
        iof = sb("iof", [128, 128])
        iop = sb("iop", [128, 1])
        tri = sb("tri", [128, 128])
        ones = sb("ones", [128, 128])
        padc = sb("padc", [128, 1])
        w1a = sb("w1a", [64, HID])
        w1b = sb("w1b", [128, 2, HID])
        w2g = sb("w2g", [128, 4, D])
        b1g = sb("b1g", [128, 4])
        b2g = sb("b2g", [128, D])
        gw = sb("gw", [128, 2, NX])
        gb = sb("gb", [128, NX])
        cWT = sb("cWT", [128, 2, D])
        cbr = sb("cbr", [128, D])
        wrr = sb("wrr", [128, D])
        brr = sb("brr", [128, 1])
        f1 = sb("f1", [128, 2, 1024])
        f2 = sb("f2", [128, 8, D])
        fb1c = sb("fb1c", [128, 8])
        fb2r = sb("fb2r", [128, D])
        keyA = sb("keyA", [128, SC])
        keyB = sb("keyB", [128, SC])
        dinv = sb("dinv", [128, NT])
        st6 = sb("st6", [128, NT, 6])
        mv = sb("mv", [128, NT, 2])
        rs = sb("rs", [128, NT])
        nm = sb("nm", [128, NT])
        wsel = sb("wsel", [128, NT])
        top = sb("top", [128, NT, 2])
        gidx = sb("gidx", [128, NT * 2], U32)
        HB = 24512
        arena = sb("arena", [128, HB])
        epsc = sb("epsc", [128, 1])

        class Cut:
            def __init__(self, at=0):
                self.at = at

            def __call__(self, shape, dt=F32, parts=128):
                n = 1
                for s in shape:
                    n *= s
                words = n if dt not in (BF16, F16) else (n + 1) // 2
                assert self.at + words <= HB, (self.at, words)
                v = arena[0:parts, self.at:self.at + words]
                self.at += words
                if dt in (BF16, F16):
                    v = v.bitcast(dt)[:, 0:n]
                elif dt != F32:
                    v = v.bitcast(dt)
                if len(shape) == 2:
                    v = v.rearrange("p (a b) -> p a b", b=shape[1])
                elif len(shape) == 3:
                    v = v.rearrange("p (a b c) -> p a b c", b=shape[1], c=shape[2])
                return v

        xs_d = nc.dram_tensor("xs_scr", [NS * 128, D], F32).ap()
        ys_d = nc.dram_tensor("ys_scr", [NS * 128, D], F32).ap()
        a_d = nc.dram_tensor("a_scr", [NA], F16).ap()
        xh_d = nc.dram_tensor("xh_scr", [NT * 128, D], F32).ap()
        x3_d = nc.dram_tensor("x3_scr", [NT * 128, D], F32).ap()
        dp_d = nc.dram_tensor("dp_scr", [NG * GE], I32).ap()

        def bc(ap, axis, n):
            v = ap.unsqueeze(axis)
            shape = list(v.shape)
            shape[axis] = n
            return v.broadcast_to(shape)

        s_ld = [sem(f"s_ld{i}") for i in range(8)]
        ca = Cut()
        azero = ca([VW], F16)
        early = ca.at
        dsti, srci, vi, v2, s1, s2 = (ca([EC], I32) for _ in range(6))
        junk = ca([EC], BF16)
        big = ca([NQ, NT - 1])
        neg1 = sb("neg1", [1, PADS], I32)
        t_neg = G(lambda e: e.memset(neg1[:, :], -1))
        t_azm = G(lambda e: e.memset(azero, 0.0))

        def edges(s_, to, frm):
            k = V(lambda e: e.memset(to[:, EL:EC], PADNODE))
            dma("sp", s_, lambda e: e.dma_start(to[0:127, 0:E0], frm[0:127 * E0].rearrange("(p c) -> p c", c=E0)), k)
            return dma("sp", s_, lambda e: e.dma_start(to[127:128, 0:EL], frm[127 * E0:NE].rearrange("(p c) -> p c", c=EL)))

        t_dst = edges(s_ld[0], dsti, dst)
        t_src = edges(s_ld[1], srci, src)
        s_dp = sem("s_dp")
        cut0 = (NG - 1) * GE
        dma("sp", s_dp, lambda e: e.dma_start(dp_d[0:cut0].rearrange("(p c) -> p c", c=GE),
                                              dst[0:cut0].rearrange("(p c) -> p c", c=GE)))
        dma("sp", s_dp, lambda e: e.dma_start(dp_d[cut0 + PADS:NG * GE].rearrange("(a c) -> a c", a=1),
                                              dst[cut0:NE].rearrange("(a c) -> a c", a=1)))
        t_dp = dma("sp", s_dp, lambda e: e.dma_start(dp_d[cut0:cut0 + PADS].rearrange("(a c) -> a c", a=1), neg1[:, :]),
                   t_neg)
        s_az = sem("s_az")
        for t in range(NT):
            t_az = dma("sp", s_az, lambda e, t=t: e.dma_start(
                a_d[t * 128 * VW:(t + 1) * 128 * VW].rearrange("(p c) -> p c", c=VW), azero), t_azm)
        s_z = sem("s_z")
        azf = arena[:, 0:512]
        for i in range(32):
            t_zero = dma("sp", s_z, lambda e, i=i: e.dma_start(
                xs_d[i * 256:(i + 1) * 256, :].rearrange("(p r) d -> p (r d)", p=128), azf), t_azm)
        t_xz = V(lambda e: e.memset(X[:, NT - 1, :], 0.0))
        t_edges = [t_dst, t_src]
        s_x = sem("s_x")
        dma("act", s_x, lambda e: e.dma_start(X[:, 0:NT - 1, :], x[0:(NT - 1) * 128, :].rearrange("(t p) d -> p t d", p=128)),
            *t_edges)
        t_x = dma("act", s_x, lambda e: e.dma_start(X[0:N - (NT - 1) * 128, NT - 1, :], x[(NT - 1) * 128:N, :]), t_xz)
        row = lambda v: v.rearrange("(a n) -> a n", a=1)
        dma("act", s_ld[2], lambda e: e.dma_start(w1a[:, :], gW1[0:64, :]))
        dma("act", s_ld[2], lambda e: e.dma_start(w1b[:, :, :], gW1[64:320, :].rearrange("(k p) n -> p k n", p=128)))
        dma("act", s_ld[2], lambda e: e.dma_start(w2g[:, :, :], gW2.rearrange("(k p) n -> p k n", p=128)))
        dma("act", s_ld[2], lambda e: e.dma_start(b1g[:, :], gb1.rearrange("(c p) -> p c", p=128), allow_slow_non_contiguous=True))
        dma("act", s_ld[2], lambda e: e.dma_start(b2g[:, :], row(gb2).broadcast_to([128, D])))
        dma("act", s_ld[2], lambda e: e.dma_start(gw[:, :, :], gate_w.rearrange("(k p) n -> p k n", p=128)))
        t_w0 = dma("act", s_ld[2], lambda e: e.dma_start(gb[:, :], row(gate_b).broadcast_to([128, NX])))
        dma("act", s_ld[3], lambda e: e.dma_start(cbr[:, :], row(cb).broadcast_to([128, D])))
        dma("act", s_ld[3], lambda e: e.dma_start(wrr[:, :], wr.rearrange("d o -> o d").broadcast_to([128, D])))
        dma("act", s_ld[3], lambda e: e.dma_start(brr[:, :], br.rearrange("(a n) -> a n", a=1).broadcast_to([128, 1])))
        dma("act", s_ld[3], lambda e: e.dma_start(f1[:, :, :], fw1.rearrange("(k p) n -> p k n", p=128)))
        dma("act", s_ld[3], lambda e: e.dma_start(f2[:, :, :], fw2.rearrange("(k p) n -> p k n", p=128)))
        dma("act", s_ld[3], lambda e: e.dma_start(fb1c[:, :], fb1.rearrange("(c p) -> p c", p=128), allow_slow_non_contiguous=True))
        t_w1 = dma("act", s_ld[3], lambda e: e.dma_start(fb2r[:, :], row(fb2).broadcast_to([128, D])))

        def iota(ap, pattern, base=0, cm=0):
            return G(lambda e: e.iota(ap, pattern=pattern, base=base, channel_multiplier=cm,
                                      allow_small_or_imprecise_dtypes=True))

        ioq = ca([NQ])
        iog = ca([NG - 1])
        ioh = ca([NT - 1])
        ios = ca([NT - 1])
        io16 = sb("io16", [128, NX])
        io25 = sb("io25", [128, NT])
        iob25 = sb("iob25", [128, NT], BF16)
        iob8 = sb("iob8", [128, 128, 8], BF16)
        io64 = sb("io64", [128, NS])
        iota(iof[:, :], [[1, 128]])
        iota(iop[:, :], [[0, 1]], cm=1)
        iota(ioq, [[1, NQ]])
        iota(iog, [[GE, NG - 1]], base=GE)
        iota(ioh, [[1, NT - 1]], base=1)
        iota(ios, [[-256, NT - 1]], base=-255)
        iota(io16[:, :], [[1, NX]])
        iota(io25[:, :], [[128, NT]])
        iota(iob25[:, :], [[1, NT]])
        iota(iob8[:, :, :], [[1, 128], [0, 8]])
        t_io = iota(io64[:, :], [[1, NS]])
        V(lambda e: e.memset(ones[:, :], 1.0))
        V(lambda e: e.memset(epsc[:, :], LNEPS))
        V(lambda e: e.tensor_scalar(ident[:, :], iof[:, :], iop[:, 0:1], None, ALU.is_equal), t_io)
        V(lambda e: e.tensor_scalar(tri[:, :], iof[:, :], iop[:, 0:1], None, ALU.is_gt))
        t_cst = V(lambda e: e.tensor_scalar(padc[:, :], iop[:, :], float(N - (NT - 1) * 128), None, ALU.is_ge))

        def ln_stats(t, *after):
            V(lambda e: e.bn_stats(st6[:, t, :], X[:, t, :]), *after)
            return V(lambda e: e.bn_aggr(mv[:, t, :], st6[:, t, :]))

        def ln_scale(a, b, after):
            k = A(lambda e: e.activation(rs[:, a:b], mv[:, a:b, 1], ACT.Sqrt, bias=epsc[:, 0:1]), after)
            V(lambda e: e.reciprocal(rs[:, a:b], rs[:, a:b]), k)
            return ln_shift(a, b)

        def ln_shift(a, b):
            return V(lambda e: e.scalar_tensor_tensor(nm[:, a:b], mv[:, a:b, 0], -1.0, rs[:, a:b], ALU.mult, ALU.mult))

        def ln_apply(t, dest, *after):
            return A(lambda e: e.activation(dest, X[:, t, :], ACT.Identity, bias=nm[:, t:t + 1], scale=rs[:, t:t + 1]),
                     *after)

        cur = [keyA, keyB]
        v0 = sb("v0", [128, 1])
        slo = sb("slo", [128, EC], BF16)
        shi = sb("shi", [128, EC], BF16)
        acnt = sb("acnt", [128, EC], F16)

        def stage(kbit, jbit):
            a, b = cur
            j = 1 << jbit
            if kbit >= 10:
                va = a[:, :].rearrange("p (m two j) -> p m two j", two=2, j=j)
                vb = b[:, :].rearrange("p (m two j) -> p m two j", two=2, j=j)
                V(lambda e: e.tensor_tensor(vb[:, :, 0, :], va[:, :, 0, :], va[:, :, 1, :], ALU.min))
                V(lambda e: e.tensor_tensor(vb[:, :, 1, :], va[:, :, 0, :], va[:, :, 1, :], ALU.max), chain=False)
            else:
                k = 1 << kbit
                va = a[:, :].rearrange("p (g up m two j) -> p g up m two j", up=2, two=2, j=j, m=k // (2 * j))
                vb = b[:, :].rearrange("p (g up m two j) -> p g up m two j", up=2, two=2, j=j, m=k // (2 * j))
                ops = [(0, 0, ALU.min), (0, 1, ALU.max), (1, 0, ALU.max), (1, 1, ALU.min)]
                for i, (up, w, op) in enumerate(ops):
                    V(lambda e, up=up, w=w, op=op: e.tensor_tensor(
                        vb[:, :, up, :, w, :], va[:, :, up, :, 0, :], va[:, :, up, :, 1, :], op), chain=(i == 0))
            cur.reverse()

        key = keyA[:, 0:EC]
        V(lambda e: e.memset(keyA[:, EC:SC], float((1 << 24) - 1)))
        V(lambda e: e.tensor_scalar(vi, dsti, iop[:, 0:1], None, ALU.add), t_dst, t_io)
        V(lambda e: e.tensor_scalar(s1, srci, 7, None, ALU.logical_shift_right), t_src)
        V(lambda e: e.tensor_scalar(s2, srci, 127, None, ALU.bitwise_and), chain=False)
        V(lambda e: e.tensor_scalar(v2, vi, 127, None, ALU.bitwise_and), chain=False)
        V(lambda e: e.tensor_scalar(vi, vi, 7, None, ALU.logical_shift_right))
        V(lambda e: e.scalar_tensor_tensor(key, s1, float(128 * VW), s2, ALU.mult, ALU.add))
        V(lambda e: e.scalar_tensor_tensor(key, v2, float(VW), key, ALU.mult, ALU.add))
        V(lambda e: e.scalar_tensor_tensor(key, vi, 128.0, key, ALU.mult, ALU.add))
        V(lambda e: e.tensor_tensor(v0[:, :], dsti[:, 0:1], iop[:, :], ALU.add), chain=False)
        V(lambda e: e.tensor_copy(slo[:, :], s2))
        t_sk = V(lambda e: e.tensor_copy(shi[:, :], s1))
        cntp = ca([NT - 1])
        for h in range(1, NT):
            t_cnt = A(lambda e, h=h: e.activation(junk, dsti, ACT.Sign, bias=ios[:, h - 1:h], scale=2.0,
                                              accum_out=cntp[:, h - 1:h]), t_dst, t_io, chain=True)

        t_s1 = [A(lambda e, t=t: e.activation(XB[:, t, :], X[:, t, :], ACT.Identity, scale=1.0 / D,
                                              accum_out=mv[:, t, 0:1]), t_x) for t in range(NT)]

        def sort_rows(a, b):
            for kbit in range(a, b):
                for jbit in range(kbit - 1, -1, -1):
                    stage(kbit, jbit)

        sort_rows(1, 9)
        k = V(lambda e: e.tensor_scalar(nm[:, :], mv[:, :, 0], -1.0, None, ALU.mult), t_s1[NT - 1])
        t_s2 = [A(lambda e, t=t: e.activation(XB[:, t, :], X[:, t, :], ACT.Square, bias=nm[:, t:t + 1],
                                              accum_out=mv[:, t, 1:2]), k, t_s1[t]) for t in range(NT)]
        sort_rows(9, 10)

        sta = ca([NT - 1])
        S = ca([NT])
        hq = ca([NQ])
        keep = ca([NQ])
        hp = ca([1])
        hp128 = ca([1])
        gpi = ca([1], U32)
        goff = ca([NQ], I32)
        qlast = ca([NT], I32)
        r1 = Cut(ca.at)([6, 512])
        Di = ca([GE], I32)
        Df = ca([GE])
        ca([1024])
        drel = ca([NQ, 8], BF16)
        tmp = ca([NQ])
        t = P(lambda e: e.matmul(PS[3][:, 0:NT - 1], ones[:, :], cntp, start=True, stop=True), t_cnt, t_cst)
        V(lambda e: e.tensor_scalar(sta, PS[3][:, 0:NT - 1], -0.5, 64.0 * EC, ALU.mult, ALU.add), t)
        fl = big.rearrange("p a b -> p (a b)")[:, 0:(NT - 1) * (NG - 1)].rearrange("p (a b) -> p a b", b=NG - 1)
        V(lambda e: e.tensor_tensor(fl, bc(sta, 2, NG - 1), bc(iog, 1, NT - 1), ALU.is_ge))
        V(lambda e: e.tensor_reduce(S[:, 1:NT], fl, AX.X, ALU.add))
        V(lambda e: e.memset(S[:, 0:1], 0.0))
        V(lambda e: e.tensor_tensor(S[:, 1:NT], S[:, 1:NT], ioh, ALU.add))
        V(lambda e: e.tensor_scalar(big[:, 0, :], S[:, 1:NT], iop[:, 0:1], 0.0, ALU.is_le, ALU.add, accum_out=hp))
        V(lambda e: e.tensor_tensor(gpi, iop[:, :], hp, ALU.subtract))
        t_gp = V(lambda e: e.tensor_scalar(hp128, hp, 128.0, None, ALU.mult))
        s_D = sem("s_D")
        t_D = dma("pool", s_D, lambda e: e.indirect_dma_start(
            Di[0:NQ, :], None, dp_d.rearrange("(g c) -> g c", c=GE),
            bass.IndirectOffsetOnAxis(ap=gpi[0:NQ, 0:1], axis=0)), t_gp, t_dp)
        V(lambda e: e.tensor_tensor(big, bc(ioq, 2, NT - 1), bc(S[:, 1:NT], 1, NQ), ALU.is_ge))
        V(lambda e: e.tensor_reduce(hq, big, AX.X, ALU.add))
        V(lambda e: e.tensor_tensor(tmp, ioq, hq, ALU.subtract))
        t_goff = V(lambda e: e.tensor_scalar(goff, tmp, 128.0, float(LASTROW), ALU.mult, ALU.min))
        V(lambda e: e.tensor_tensor(keep[:, 1:NQ], hq[:, 1:NQ], hq[:, 0:NQ - 1], ALU.is_equal))
        V(lambda e: e.tensor_scalar(qlast[:, 0:NT - 1], S[:, 1:NT], -1.0, None, ALU.add))
        t_ql = V(lambda e: e.memset(qlast[:, NT - 1:NT], NQ - 1))
        sort_rows(10, 11)
        k = A(lambda e: e.activation(rs[:, :], mv[:, :, 1], ACT.Sqrt, bias=epsc[:, 0:1], scale=1.0 / D), t_s2[NT - 1])
        V(lambda e: e.reciprocal(rs[:, :], rs[:, :]), k)
        k = V(lambda e: e.tensor_tensor(nm[:, :], nm[:, :], rs[:, :], ALU.mult))
        t_xh0 = [ln_apply(t, XB[:, t, :], k) for t in range(NT)]
        srt, same = cur
        V(lambda e: e.memset(same[:, 0:1], 0.0))
        V(lambda e: e.tensor_tensor(same[:, 1:EC + 1], srt[:, 1:EC + 1], srt[:, 0:EC], ALU.is_equal))
        V(lambda e: e.tensor_tensor_scan(acnt[:, :], same[:, 0:EC], ones[:, 0:1].broadcast_to([128, EC]), 0.0,
                                         ALU.mult, ALU.add))
        aidx = srt[:, 0:EC].bitcast(U32)
        t_idx = V(lambda e: e.scalar_tensor_tensor(aidx, same[:, 1:EC + 1], float(1 << 24), srt[:, 0:EC],
                                                   ALU.mult, ALU.add))
        s_A = [sem(f"s_A{i}") for i in range(4)]
        t_A = [None] * 4
        done = [0]

        def scatter(n):
            for c in range(done[0], min(done[0] + n, E0)):
                t_A[c % 4] = dma("pool", s_A[c % 4], lambda e, c=c: e.indirect_dma_start(
                    a_d.rearrange("(a b) -> a b", b=1), bass.IndirectOffsetOnAxis(ap=aidx[:, c:c + 1], axis=0),
                    acnt[:, c:c + 1], None, bounds_check=NA - 1, oob_is_err=False), t_idx, t_az)
            done[0] = min(done[0] + n, E0)

        t_Df = V(lambda e: e.tensor_scalar(Df[0:NQ, :], Di[0:NQ, :], hp128[0:NQ, 0:1], None, ALU.subtract), t_D)
        Dr = Df[0:NQ, :].rearrange("q (p r) -> q r p", r=8)
        t_dr = []
        for hf in range(2):
            for r in range(4):
                t = P(lambda e, hf=hf, r=r: e.transpose(PS[4 + hf][:, r * NQ:(r + 1) * NQ], Dr[:, 4 * hf + r, :],
                                                        ident[0:NQ, 0:NQ]), t_Df)
            t_dr.append(V(lambda e, hf=hf: e.tensor_copy(
                drel[:, :, 4 * hf:4 * hf + 4], PS[4 + hf][:, 0:4 * NQ].rearrange("p (r q) -> p q r", q=NQ)), t))

        ring = ca([RA, 512])
        DB = 6
        lo = ca([DB, 8, 65], BF16)
        oh = ca([DB, 128, 8], BF16)
        store = Cut(early)([NQ, 65])
        agg = sb("agg", [128, NT, 65])
        s_ring = [sem(f"s_ring{i}") for i in range(RA)]
        attr_v = attr.rearrange("(a r) f -> a (r f)", r=8)
        for s in range(DB):
            t_lo1 = V(lambda e, s=s: e.memset(lo[:, s, :, 64:65], 1.0))
        ringb = ring.bitcast(BF16).rearrange("p a (r f two) -> p a r f two", two=2, f=64)
        r1b = r1.bitcast(BF16).rearrange("p a (r f two) -> p a r f two", two=2, f=64)
        ringf = ring.rearrange("p a (r f) -> p a r f", f=64)
        r1f = r1.rearrange("p a (r f) -> p a r f", f=64)
        t_mm, t_ld, t_st, t_r1 = {}, {}, {}, {}

        def load_attr(k):
            def go(e):
                r = e.value_load(goff[0:1, k:k + 1], min_val=0, max_val=LASTROW)
                return e.dma_start(ring[:, k % RA, :], attr_v[bass.ds(r, 128), :])
            t_ld[k] = dma("sp", s_ring[k % RA], go, t_goff, t_mm.get(k - RA))

        def split_attr(k):
            s, a = k % DB, k % RA
            on = G if k // 2 % SPLIT == SPLIT - 1 else V
            t_r1[k] = on(lambda e: e.tensor_tensor(r1f[:, s:s + 2, :, :], ringf[:, a:a + 2, :, :], ringb[:, a:a + 2, :, :, 1],
                                                   ALU.subtract), t_ld[k], t_ld[k + 1], t_mm.get(k - DB + 1), *t_dr,
                          chain=False)

        qv = {}

        def note_last(h):
            def go(e):
                qv[h] = e.value_load(qlast[0:1, h:h + 1], min_val=0, max_val=NQ - 1)
            q.ahead("dve", go, t_ql)

        scatter(SC_PRE)
        for k in range(RA):
            load_attr(k)
        split_attr(0)

        def keep_sum(j):
            if j == 0:
                t_st[j] = V(lambda e: e.tensor_copy(store[:, 0, :], PS[0][:, 0:65]), t_mm[0])
            else:
                t_st[j] = V(lambda e: e.scalar_tensor_tensor(
                    store[:, j, :], store[:, j - 1, :], keep[:, j:j + 1], PS[j % 4][:, 0:65], ALU.mult, ALU.add), t_mm[j],
                    t_st[j - 1], chain=False)

        for k in range(0, NQ, 2):
            s = k % DB
            if k + 2 < NQ:
                split_attr(k + 2)
            t1 = V(lambda e, k=k, s=s: e.tensor_tensor(
                oh[:, s:s + 2, :, :], bc(iob8[:, :, :], 1, 2), bc(drel[:, k:k + 2, :], 2, 128), ALU.is_equal),
                t_mm.get(k - DB + 1), *t_dr, chain=False)
            t2 = V(lambda e, s=s: e.tensor_tensor(lo[:, s:s + 2, :, 0:64], r1f[:, s:s + 2, :, :], r1b[:, s:s + 2, :, :, 1],
                                                  ALU.subtract), t_r1[k], t_lo1, t_mm.get(k - DB + 1), chain=False)
            for m in range(k, k + 2):
                z, s = PS[m % 4], m % DB
                for r in range(8):
                    P(lambda e, s=s, r=r, z=z: e.matmul(z[:, 0:65], oh[:, s, :, r], lo[:, s, r, :], start=(r == 0),
                                                        stop=False), t2, t1, t_st.get(m - 4), sig=False)
                    P(lambda e, s=s, r=r, z=z: e.matmul(z[:, 0:64], oh[:, s, :, r], r1b[:, s, r, :, 1], start=False,
                                                        stop=False), t_r1[k], sig=False)
                    t3 = P(lambda e, m=m, s=s, r=r, z=z: e.matmul(z[:, 0:64], oh[:, s, :, r], ringb[:, m % RA, r, :, 1],
                                                                  start=False, stop=(r == 7)), t_ld[m], sig=(r == 7))
                t_mm[m] = t3
                scatter(SC_L0 if m % 5 else 1)
                if m + RA < NQ:
                    load_attr(m + RA)
            if k % 4 == 0 and k // 4 < NT:
                note_last(k // 4)
            if k:
                keep_sum(k - 2)
                keep_sum(k - 1)
        keep_sum(NQ - 2)
        keep_sum(NQ - 1)
        t_xb = {}
        V(lambda e: e.memset(agg[:, 0, 0:1], 0.0), t_az, t_zero)
        for h in range(NT):
            t_pk = V(lambda e, h=h: e.tensor_copy(agg[:, h, :], store[:, bass.ds(qv[h], 1), :].rearrange("p a b -> p (a b)")),
                     t_st[NQ - 1], chain=(h == 0))
        cn = sb("cn", [128, NT])
        V(lambda e: e.tensor_scalar(cn[:, :], agg[:, :, 64], 1.0, None, ALU.max))
        V(lambda e: e.reciprocal(cn[:, :], cn[:, :]))
        t_agg = V(lambda e: e.tensor_tensor(agg[:, :, 0:64], agg[:, :, 0:64], bc(cn[:, :], 2, 64), ALU.mult))
        t_l0 = t_agg

        ca = Cut()
        CT = ca([2, 3, 512])
        HT = ca([2, 4, 512])
        XT1 = ca([2, 512])
        lg = ca([NT, NX])
        cWn = ca([2, D])
        t_cwn = dma("sp", s_ld[4], lambda e: e.dma_start(cWn, cW.rearrange("(k p) n -> p k n", p=128)), t_l0)
        ohl = ca([4, 128, 8], BF16)
        ohh = ca([3, 16, NT], BF16)
        mlp_end = ca.at
        groups = [list(range(a, min(a + 4, NT))) for a in range(0, NT, 4)]
        t_ct, t_ht, t_tp, t_hmm, t_omm, t_x1, t_xh1, t_lg = {}, {}, {}, {}, {}, {}, {}, {}
        t_op = {}

        sorted_tok = {}

        def background():
            t_d = {}
            t_hh, oh_tok = {}, {}

            def count(c):
                for r in range(8):
                    t_d[c] = P(lambda e, c=c, r=r: e.matmul(
                        PS[7][:, 0:NT], ohl[:, c % 4, :, r], ohh[:, (c // 2) % 3, 8 * (c % 2) + r, :],
                        start=(c == 0 and r == 0), stop=(c == EC // 8 - 1 and r == 7)),
                        oh_tok[c], t_hh[c // 2], free.get(7), sig=(r == 7))

            for c in range(EC // 8):
                c2 = c // 2
                if c % 2 == 0:
                    t_hh[c2] = V(lambda e, c2=c2: e.tensor_tensor(
                        ohh[:, c2 % 3, :, :], bc(iob25[:, :], 1, 16), bc(shi[:, 16 * c2:16 * c2 + 16], 2, NT),
                        ALU.is_equal), t_d.get(c - 5), t_l0, chain=False)
                k1 = V(lambda e, c=c, s=s: e.tensor_tensor(
                    ohl[:, c % 4, :, :], iob8[:, :, :], bc(slo[:, 8 * c:8 * c + 8], 1, 128), ALU.is_equal),
                    t_d.get(c - 4), t_l0, chain=False)
                oh_tok[c] = k1
                if c > 1:
                    count(c - 2)
                if c % 2:
                    yield
            count(EC // 8 - 2)
            count(EC // 8 - 1)
            k = V(lambda e: e.tensor_copy(dinv[:, :], PS[7][:, 0:NT]), t_d[EC // 8 - 1])
            V(lambda e: e.tensor_tensor(dinv[:, NT - 1:NT], dinv[:, NT - 1:NT], padc[:, :], ALU.add))
            k = A(lambda e: e.activation(dinv[:, :], dinv[:, :], ACT.Sqrt), Token(q.sems["dve"], q.count["dve"]))
            sorted_tok["dinv"] = V(lambda e: e.reciprocal(dinv[:, :], dinv[:, :]), k)

        bg = background()

        def step_bg(n):
            for _ in range(n):
                next(bg, None)

        free = {}

        def turned(bank, tiles, src_of, parts, *after):
            n = 128 * len(tiles)
            for j, t in enumerate(tiles):
                k = P(lambda e, j=j, t=t: e.transpose(PS[bank][0:parts, j * 128:(j + 1) * 128], src_of(t), ident[:, :]),
                      free.get(bank), *after, sig=(j == len(tiles) - 1))
            return k, n

        def transposes(gi, cs):
            if gi >= len(groups):
                return
            g, s = groups[gi], gi % 2
            for c in cs:
                pp, b = (64, 0) if c == 0 else (128, c % 2)
                src_of = (lambda t: agg[:, t, 0:64]) if c == 0 else (lambda t, c=c: XB[:, t, (c - 1) * 128:c * 128])
                k, n = turned(b, g, src_of, pp, t_agg, t_xh0[g[-1]])
                t_tp[(gi, c)] = k
                if c < 2:
                    t_ct[(gi, c)] = A(lambda e, b=b, c=c, pp=pp: e.activation(
                        CT[0:pp, s, c, 0:n], PS[b][0:pp, 0:n], ACT.Identity), k, t_hmm.get(gi - 2), t_l0)
                else:
                    t_ct[(gi, c)] = V(lambda e, b=b, c=c, pp=pp: e.tensor_copy(
                        CT[0:pp, s, c, 0:n], PS[b][0:pp, 0:n]), k, t_hmm.get(gi - 2), t_l0)
                free[b] = t_ct[(gi, c)]

        def hidden(gi):
            g, s = groups[gi], gi % 2
            n = 128 * len(g)
            for c in range(4):
                z = PS[3 + c % 2]
                w = (t_ht.get((gi, c - 2)) if c >= 2 else t_ht.get((gi - 1, c + 2)))
                for i, (lhs, pp) in enumerate([(w1a[:, c * 128:(c + 1) * 128], 64), (w1b[:, 0, c * 128:(c + 1) * 128], 128),
                                               (w1b[:, 1, c * 128:(c + 1) * 128], 128)]):
                    k = P(lambda e, lhs=lhs, pp=pp, i=i, z=z: e.matmul(z[:, 0:n], lhs, CT[0:pp, s, i, 0:n],
                                                                      start=(i == 0), stop=(i == 2)),
                          t_w0, w, t_ct[(gi, i)], sig=(i == 2))
                t_ht[(gi, c)] = A(lambda e, c=c, z=z: e.activation(HT[:, s, c, 0:n], z[:, 0:n], ACT.Relu,
                                                                   bias=b1g[:, c:c + 1]), k, t_omm.get(gi - 2))
                transposes(gi + 1, (c,) if c < 3 else ())
                step_bg(1)
            t_hmm[gi] = k

        def output(gi):
            g, s = groups[gi], gi % 2
            for t in g:
                t_xb[t] = V(lambda e, t=t: e.tensor_tensor(X[:, t, :], X[:, t, :], b2g[:, :], ALU.add), t_xh0[t], t_w0)
            for j, t in enumerate(g):
                z = PS[2 + 3 * (t % 2)][:, 0:256]
                for c in range(4):
                    k = P(lambda e, j=j, c=c, z=z: e.matmul(z, HT[:, s, c, j * 128:(j + 1) * 128], w2g[:, c, :],
                                                            start=(c == 0), stop=(c == 3)), t_ht[(gi, c)],
                          t_x1.get(t - 2), sig=(c == 3))
                t_x1[t] = V(lambda e, t=t, z=z: e.tensor_tensor(X[:, t, :], X[:, t, :], z, ALU.add), k, t_xb[t])
                kk = ln_stats(t)
                if j < 2:
                    gate_turn(gi - 1, j)
            if len(g) < 2:
                gate_turn(gi - 1, 1)
            t_omm[gi] = k
            kk = ln_scale(g[0], g[-1] + 1, kk)
            for t in g:
                t_xh1[t] = ln_apply(t, XB[:, t, :], t_tp[(gi, 2)], kk)

        def gate_turn(gi, c):
            if not 0 <= gi < len(groups):
                return
            g = groups[gi]
            k, n = turned(c, g, lambda t, c=c: XB[:, t, c * 128:(c + 1) * 128], 128, t_xh1[g[-1]])
            free[c] = t_lg[("c", gi, c)] = A(lambda e, c=c, n=n: e.activation(XT1[:, c, 0:n], PS[c][:, 0:n],
                                                                              ACT.Identity), k,
                                             t_lg.get(("m", gi - 1)), t_l0)

        def gate(gi):
            if not 0 <= gi < len(groups):
                return
            g = groups[gi]
            for j, t in enumerate(g):
                z = PS[6][:, NX * j:NX * j + NX]
                for c in range(2):
                    k = P(lambda e, c=c, j=j, z=z: e.matmul(z, XT1[:, c, j * 128:(j + 1) * 128], gw[:, c, :],
                                                            start=(c == 0), stop=(c == 1)), t_lg[("c", gi, c)],
                          free.get(6), sig=(c == 1))
            t_lg[("m", gi)] = k
            free[6] = V(lambda e: e.tensor_tensor(lg[:, g[0]:g[-1] + 1, :],
                                                  PS[6][:, 0:NX * len(g)].rearrange("p (t x) -> p t x", x=NX),
                                                  bc(gb[:, :], 1, len(g)), ALU.add), k)

        ex = ca([NT, NX])
        mx = ca([NT, 8])
        mi = ca([NT, 8], U32)
        sm = ca([NT])
        mlp_end = ca.at

        def two_best(gi):
            a, b = groups[gi][0], groups[gi][-1] + 1
            V(lambda e: e.tensor_reduce(sm[:, a:b], lg[:, a:b, :], AX.X, ALU.max))
            k = V(lambda e: e.tensor_tensor(ex[:, a:b, :], lg[:, a:b, :], bc(sm[:, a:b], 2, NX), ALU.subtract))
            k = A(lambda e: e.activation(ex[:, a:b, :], ex[:, a:b, :], ACT.Exp), k)
            V(lambda e: e.tensor_reduce(sm[:, a:b], ex[:, a:b, :], AX.X, ALU.add), k)
            V(lambda e: e.reciprocal(sm[:, a:b], sm[:, a:b]))
            V(lambda e: e.tensor_tensor(ex[:, a:b, :], ex[:, a:b, :], bc(sm[:, a:b], 2, NX), ALU.mult))
            for t in range(a, b):
                V(lambda e, t=t: e.max(mx[:, t, :], ex[:, t, :]), chain=(t == a))
            for t in range(a, b):
                V(lambda e, t=t: e.max_index(mi[:, t, :], mx[:, t, :], ex[:, t, :]), chain=(t == a))

        transposes(0, (0, 1, 2))
        for gi in range(len(groups) + 2):
            if gi < len(groups):
                hidden(gi)
            if 0 < gi <= len(groups):
                output(gi - 1)
            if gi > len(groups):
                gate_turn(gi - 2, 0)
                gate_turn(gi - 2, 1)
            gate(gi - 2)
            if gi > 2:
                two_best(gi - 3)
            scatter(SC_MLP)
        two_best(len(groups) - 1)
        s_out = sem("s_out")

        def stages_after():
            ca = Cut(mlp_end)
            sm2 = ca([NT])
            idf = ca([NT, 2])
            M = ca([NT * 2, NX])
            pos = ca([NT * 2, NX])
            tot = ca([NT * 2, NX])
            inc = ca([NX, NT * 2])
            one50 = ca([NT * 2])
            til = ca([NX, NT])
            nt = ca([NX])
            end = ca([NX])
            base = ca([NX])
            slot = ca([NT * 2])
            cmp = ca([NS, NX])
            ei = sb("ei", [128, NS], I32)
            newx = sb("newx", [128, NS], I32)
            sidx = sb("sidx", [128, NT * 2], U32)
            V(lambda e: e.tensor_tensor(sm2, mx[:, :, 0], mx[:, :, 1], ALU.add))
            V(lambda e: e.reciprocal(sm2, sm2))
            t_top = V(lambda e: e.tensor_tensor(top[:, :, :], mx[:, :, 0:2], bc(sm2, 2, 2), ALU.mult))
            V(lambda e: e.tensor_copy(idf, mi[:, :, 0:2]))
            V(lambda e: e.scalar_tensor_tensor(idf[:, NT - 1, :], bc(padc[:, 0], 1, 2), 100.0, idf[:, NT - 1, :], ALU.mult, ALU.add))
            idv = idf.rearrange("p t k -> p (t k)")
            t_M = V(lambda e: e.tensor_tensor(M, bc(io16[:, :], 1, NT * 2), bc(idv, 2, NX), ALU.is_equal))
            Mf = M.rearrange("p a e -> p (a e)")
            for (b, lhs) in ((0, tri), (2, ones)):
                P(lambda e, b=b, lhs=lhs: e.matmul(PS[b][:, 0:400], lhs[:, :], Mf[:, 0:400], start=True, stop=True), t_M)
                kp = P(lambda e, b=b, lhs=lhs: e.matmul(PS[b + 1][:, 0:400], lhs[:, :], Mf[:, 400:800], start=True, stop=True))
            posf, totf = pos.rearrange("p a e -> p (a e)"), tot.rearrange("p a e -> p (a e)")
            for b in range(2):
                V(lambda e, b=b: e.tensor_copy(posf[:, 400 * b:400 * b + 400], PS[b][:, 0:400]), kp)
                V(lambda e, b=b: e.tensor_copy(totf[:, 400 * b:400 * b + 400], PS[2 + b][:, 0:400]))
            V(lambda e: e.memset(one50, 1.0))
            for x_ in range(NX):
                V(lambda e, x_=x_: e.tensor_tensor_scan(inc[:, x_, :], one50, tot[:, :, x_], 0.0, ALU.mult, ALU.add))
            V(lambda e: e.tensor_tensor(til, bc(inc[:, :, NT * 2 - 1], 2, NT), bc(io25[:, :], 1, NX), ALU.is_gt))
            V(lambda e: e.tensor_reduce(nt, til, AX.X, ALU.add))
            V(lambda e: e.tensor_tensor_scan(end, one50[:, 0:NX], nt, 0.0, ALU.mult, ALU.add))
            V(lambda e: e.tensor_tensor(base, end, nt, ALU.subtract))
            V(lambda e: e.tensor_scalar(base, base, 128.0, None, ALU.mult))
            V(lambda e: e.tensor_tensor(cmp, bc(io64[:, :], 2, NX), bc(end, 1, NS), ALU.is_ge))
            V(lambda e: e.tensor_reduce(io64f[:, :], cmp, AX.X, ALU.add))
            t_ei = V(lambda e: e.tensor_scalar(ei[:, :], io64f[:, :], float(NX - 1), None, ALU.min))
            V(lambda e: e.tensor_tensor(newx[:, 1:NS], ei[:, 1:NS], ei[:, 0:NS - 1], ALU.not_equal))
            for m in (0, 22, 43):
                t_ei = V(lambda e, m=m: e.memset(newx[:, m:m + 1], 1))
            V(lambda e: e.tensor_tensor(pos, pos, inc.rearrange("p e a -> p a e"), ALU.add))
            V(lambda e: e.tensor_tensor(pos, pos, tot, ALU.subtract))
            V(lambda e: e.tensor_tensor(pos, pos, bc(base, 1, NT * 2), ALU.add))
            V(lambda e: e.tensor_tensor(pos, pos, M, ALU.mult))
            V(lambda e: e.tensor_reduce(slot, pos, AX.X, ALU.add))
            V(lambda e: e.tensor_copy(gidx[:, :], slot))
            V(lambda e: e.scalar_tensor_tensor(slot[:, NT * 2 - 2:NT * 2], bc(padc[:, 0], 1, 2), 100000.0,
                                               slot[:, NT * 2 - 2:NT * 2], ALU.mult, ALU.add))
            t_slot = V(lambda e: e.tensor_copy(sidx[:, :], slot))

            scatter(SC_GAP)
            s_sc = sem("s_sc")
            for a in range(NT * 2):
                t_sc = dma("pool", s_sc, lambda e, a=a: e.indirect_dma_start(
                    xs_d, bass.IndirectOffsetOnAxis(ap=sidx[:, a:a + 1], axis=0), XB[:, a // 2, :], None,
                    bounds_check=NS * 128 - 1, oob_is_err=False), t_slot, t_zero)

            while next(bg, 1) is None:
                pass
            for a in range(2):
                for b in range(2):
                    k = P(lambda e, a=a, b=b: e.transpose(PS[7][:, b * 256 + a * 128:b * 256 + a * 128 + 128],
                                                          cWn[:, a, b * 128:(b + 1) * 128], ident[:, :]), t_w1, t_cst, t_cwn, sorted_tok["dinv"])
            t_cw = A(lambda e: e.activation(cWT[:, :, :], PS[7][:, :].rearrange("p (a b) -> p a b", b=256), ACT.Identity), k)
            free[7] = t_cw

            ca = Cut(mlp_end)
            NW = 3
            starts = [0, 22, 43]

            def sl(i):
                return starts[i % NW] + i // NW

            W1 = ca([NW, 2, HID])
            W2 = ca([NW, 2, HID])
            yb = ca([4, D])
            W3 = Cut(3072)([NW, 4, D])
            ca = Cut(0)
            xsb = ca([4, D])
            xT = ca([2, D])
            hs = ca([HID])
            hid = ca([2, HID])
            assert ca.at <= 3072
            s_w = [[sem(f"s_w{j}{i}") for i in range(NW)] for j in range(3)]
            s_xs = [sem(f"s_xs{i}") for i in range(4)]
            s_ys = sem("s_ys")
            v1 = ew1.rearrange("e (k p) n -> p (e k) n", p=128)
            v2 = ew2.rearrange("e (k p) n -> p (e k) n", p=128)
            v3 = ew3.rearrange("e (k p) n -> p (e k) n", p=128)
            t_wl, t_xl, tB, tA, tC, tD, tx, thid, thT, tyb, tst = ({} for _ in range(11))
            e_reg = {}

            def loads(i):
                s, m = i % NW, sl(i)

                def fresh(e):
                    return e.value_load(newx[0:1, m:m + 1], min_val=0, max_val=1)

                def w(v, W, n):
                    def go(e):
                        r = e.value_load(ei[0:1, m:m + 1], min_val=0, max_val=NX - 1)
                        return e.dma_start(W[:, s, :, :], v[:, bass.ds(r * n, n), :])
                    return go
                a, b = q.dma_if("sp", fresh, [(s_w[0][s], w(v1, W1, 2)), (s_w[1][s], w(v2, W2, 2))],
                                t_ei, t_slot, tB.get(i - NW))
                c, = q.dma_if("sp", fresh, [(s_w[2][s], w(v3, W3, 4))], tD.get(i - NW))
                t_wl[i] = (a, b, c)

            def load_x(i):
                t_xl[i] = dma("sp", s_xs[i % 4], lambda e: e.dma_start(xsb[:, i % 4, :], xs_d[sl(i) * 128:(sl(i) + 1) * 128, :]),
                              t_sc, tA.get(i - 4))

            def stA(i):
                for c in range(2):
                    tA[i] = P(lambda e, c=c: e.transpose(PS[4][:, c * 128:(c + 1) * 128],
                                                         xsb[:, i % 4, c * 128:(c + 1) * 128], ident[:, :]),
                              t_xl[i], tx.get(i - 1), sig=(c == 1))
                tx[i] = A(lambda e: e.activation(xT[:, i % 2, :], PS[4][:, 0:256], ACT.Identity), tA[i], tB.get(i - 2))

            def stB(i):
                s = i % NW
                for (b, W, j) in ((0, W1, 0), (2, W2, 1)):
                    for h in range(4):
                        for c in range(2):
                            k = P(lambda e, b=b, W=W, c=c, h=h: e.matmul(
                                PS[b + i % 2][:, h * 128:(h + 1) * 128], W[:, s, c, h * 128:(h + 1) * 128],
                                xT[:, i % 2, c * 128:(c + 1) * 128], start=(c == 0), stop=(c == 1)),
                                tx[i], t_wl[i][j], thid.get(i - 2), sig=(c == 1 and h == 3))
                    if j == 0:
                        kh = k
                tB[i] = k
                ks = A(lambda e: e.activation(hs, PS[i % 2][:, :], ACT.Silu), kh, thid.get(i - 1))
                thid[i] = V(lambda e: e.tensor_tensor(hid[:, i % 2, :], hs, PS[2 + i % 2][:, :], ALU.mult), ks, k,
                            tD.get(i - 2))

            def stD(i):
                s = i % NW
                for c in range(4):
                    tD[i] = P(lambda e, c=c: e.matmul(PS[6][:, 0:256], hid[:, i % 2, c * 128:(c + 1) * 128], W3[:, s, c, :],
                                                      start=(c == 0), stop=(c == 3)), thid[i], t_wl[i][2],
                              tyb.get(i - 1), sig=(c == 3))
                tyb[i] = V(lambda e: e.tensor_copy(yb[:, i % 4, :], PS[6][:, 0:256]), tD[i], tst.get(i - 4))
                tst[i] = dma("sp", s_yb[i % 4], lambda e: e.dma_start(ys_d[sl(i) * 128:(sl(i) + 1) * 128, :], yb[:, i % 4, :]),
                             tyb[i])

            s_yb = [sem(f"s_yb{i}") for i in range(4)]

            SEL = HB - 270 - NV * 128
            assert mlp_end + 3 * 2048 + 1024 <= SEL
            ca = Cut(SEL)
            sel = ca([NV * 2, 128], F16)
            vall = ca([NV])
            dv = ca([128])
            vc = Cut(SEL)([NV, 128], BF16)
            t_v = G(lambda e: e.iota(vall, pattern=[[128, NV]], base=0, channel_multiplier=1,
                                     allow_small_or_imprecise_dtypes=True), t_slot)
            k = V(lambda e: e.tensor_scalar(dv, ident[:, :], v0[:, 0:1], None, ALU.mult), t_slot)
            k = P(lambda e: e.matmul(PS[5][:, 0:128], ones[:, :], dv, start=True, stop=True), k, t_x1[NT - 1])
            V(lambda e: e.tensor_tensor(vc, bc(vall, 2, 128), bc(PS[5][:, 0:128], 1, NV), ALU.is_ge), t_v, k)
            V(lambda e: e.tensor_reduce(dv[:, 0:NV], vc, AX.X, ALU.add))
            V(lambda e: e.tensor_scalar(dv[:, 0:NV], dv[:, 0:NV], 1.0, None, ALU.max))
            V(lambda e: e.tensor_tensor(vall, vall, dv[:, 0:NV], ALU.subtract))
            V(lambda e: e.tensor_scalar(vall, vall, 1.0, float(N - 1), ALU.add, ALU.min))
            t_dg, t_dr2, t_sel = {}, {}, {}

            def pick_rows(i):
                j = i - 6
                if 0 <= j < NV:
                    for o in range(2):
                        t_sel[j] = V(lambda e, j=j, o=o: e.tensor_scalar(
                            sel[:, 2 * j + o, :], PS[5 + 2 * (j % 2)][:, 0:128], 128.0 * (j - o), iop[:, 0:1],
                            ALU.subtract, ALU.is_equal), t_dr2[j])
                j = i - 5
                if 0 <= j < NV:
                    t_dr2[j] = P(lambda e, j=j: e.matmul(PS[5 + 2 * (j % 2)][:, 0:128], ones[:, :], dv, start=True, stop=True),
                                 t_dg[j], t_sel.get(j - 2), t_cw)
                j = i - 4
                if 0 <= j < NV:
                    t_dg[j] = V(lambda e, j=j: e.tensor_scalar(dv, ident[:, :], vall[:, j:j + 1], None, ALU.mult),
                                t_dr2.get(j - 1))

            for i in range(min(NW, NS)):
                loads(i)
            for i in range(4):
                load_x(i)
            stA(0)
            for i in range(NS + 1):
                if i + 1 < NS:
                    stA(i + 1)
                if i + 4 < NS:
                    load_x(i + 4)
                if i < NS:
                    stB(i)
                if i:
                    stD(i - 1)
                    if i - 1 + NW < NS:
                        loads(i - 1 + NW)
                pick_rows(i)
                scatter(SC_MOE)
            scatter(E0 - TAIL - done[0])

            ca = Cut(0)
            CT2 = ca([2, 2, 512])
            yv = ca([NV, 512], F16)
            RG = 16
            gr = Cut(ca.at)([RG, D])
            NAB = 3
            ab = ca([NAB, VW], F16)
            cw = Cut(ca.at)
            ca(([818]))
            yhl = ca([NT, 512], F16)
            assert ca.at <= SEL
            s_g = [sem(f"s_g{i}") for i in range(RG)]
            s_ab = [sem(f"s_ab{i}") for i in range(NAB)]
            t_g, t_c2, t_yh, t_yl, t_yz, t_yv, t_ab, t_ap, t_ev = ({} for _ in range(9))

            order = [(t, j) for g in groups for j in range(2) for t in g]
            place = {tj: o for o, tj in enumerate(order)}

            def fetch(o):
                a = 2 * order[o][0] + order[o][1]
                t_g[o] = dma("pool", s_g[o % RG], lambda e: e.indirect_dma_start(
                    gr[:, o % RG, :], None, ys_d, bass.IndirectOffsetOnAxis(ap=gidx[:, a:a + 1], axis=0)),
                    tst[NS - 1], tst[NS - 2], tst[NS - 3], tst[NS - 4], t_c2.get(o - RG), tD[NS - 1])

            for o in range(RG):
                fetch(o)

            def combine(gi):
                g = groups[gi]
                a, b = g[0], g[-1] + 1
                for j in range(2):
                    for t in g:
                        o = place[t, j]
                        t_c2[o] = V(lambda e, t=t, j=j, o=o: e.scalar_tensor_tensor(
                            X[:, t, :], gr[:, o % RG, :], top[:, t, j:j + 1], X[:, t, :], ALU.mult, ALU.add), t_g[o],
                            t_c2.get(place[t, 0]) if j else None, chain=False)
                        if o + RG < NT * 2:
                            fetch(o + RG)
                ks_ = [V(lambda e, t=t: e.bn_stats(st6[:, t, :], X[:, t, :]), t_c2[place[t, 1]], chain=False) for t in g]
                for t, k in zip(g, ks_):
                    kk = V(lambda e, t=t: e.bn_aggr(mv[:, t, :], st6[:, t, :]), k, chain=False)
                k = A(lambda e: e.activation(rs[:, a:b], mv[:, a:b, 1], ACT.Sqrt, bias=epsc[:, 0:1]), kk)
                V(lambda e: e.reciprocal(rs[:, a:b], rs[:, a:b]), k)
                V(lambda e: e.tensor_tensor(rs[:, a:b], rs[:, a:b], dinv[:, a:b], ALU.mult), sorted_tok["dinv"])
                kx = ln_shift(a, b)
                for t in g:
                    kk = ln_apply(t, XB[:, t, :], t_sc, kx)
                    t_yh[t] = A(lambda e, t=t: e.activation(yhl[:, t, 0:256], XB[:, t, :], ACT.Identity, scale=YS), kk, tD[NS - 1])

            def low_halves(gi):
                for t in groups[gi]:
                    t_yl[t] = V(lambda e, t=t: e.scalar_tensor_tensor(yhl[:, t, 256:512], XB[:, t, :], YS, yhl[:, t, 0:256],
                                                                      ALU.mult, ALU.subtract), t_yh[t], chain=False)

            def rows(j):
                z = PS[3 + j % 2]
                src_ = [o for o in range(2) if 0 <= j - o < NT]
                for o in src_:
                    t_yz[j] = P(lambda e, o=o: e.matmul(z[:, :], sel[:, 2 * j + o, :], yhl[:, j - o, :], start=(o == src_[0]),
                                                        stop=(o == src_[-1])), t_sel[j], t_yl[j - o], t_yv.get(j - 2),
                                tyb[NS - 1], sig=(o == src_[-1]))
                t_yv[j] = A(lambda e: e.activation(yv[:, j, :], z[:, :], ACT.Identity), t_yz[j], tD[NS - 1])

            v_of = [[j for j in range(NV) if min(j, NT - 1) in g] for g in groups]

            for gi in range(len(groups) + 1):
                if gi < len(groups):
                    combine(gi)
                if gi == len(groups) - 3:
                    scatter(E0)
                if gi:
                    low_halves(gi - 1)
                    for j in v_of[gi - 1]:
                        rows(j)

            def load_a(t):
                t_ab[t] = dma("sp", s_ab[t % NAB], lambda e: e.dma_start(
                    ab[:, t % NAB, :], a_d[t * 128 * VW:(t + 1) * 128 * VW].rearrange("(p c) -> p c", c=VW)),
                    *t_A, t_c2[NT * 2 - 1], t_ap.get(t - NAB))

            def apply(t):
                z = PS[5 + t % 2][:, 0:256]
                for j in range(NV):
                    lhs = ab[:, t % NAB, j * 128:(j + 1) * 128]
                    for i in range(2):
                        last_ = j == NV - 1 and i == 1
                        t_ap[t] = P(lambda e, lhs=lhs, z=z, i=i, j=j, last_=last_: e.matmul(
                            z, lhs, yv[:, j, i * 256:(i + 1) * 256], start=(i + j == 0), stop=last_), t_ab[t], t_yv[j],
                            t_ev.get(t - 2), sig=last_)
                t_ev[t] = V(lambda e: e.scalar_tensor_tensor(XB[:, t, :], z, 1.0 / YS, XB[:, t, :], ALU.mult, ALU.add), t_ap[t],
                            t_yl[t])
                if t + NAB < NT:
                    load_a(t + NAB)

            for t in range(NAB):
                load_a(t)

            ca = Cut(2048)
            XT3 = ca([2, 2, 512])
            HT3 = ca([8, 512])
            xg = ca([NR, D])
            ohr = ca([4, 128, 8], BF16)
            assert ca.at <= 13696
            ca = Cut(14514)
            x3g = ca([NR, D])
            yz = ca([2, D])
            tab = ca([8, 15], I32)
            cmp3 = ca([15, NT], BF16)
            cand = ca([15], I32)
            cnt3 = ca([15])
            hit = ca([15])
            thr = ca([1], I32)
            one = ca([8])
            vv = ca([NT])
            two = ca([2 * NT])
            inc3 = ca([2, NT])
            pos3 = ca([2, NT])
            keepm = ca([NT])
            posi = ca([NT], I32)
            rlo = ca([32], BF16)
            rhi = ca([NT], I32)
            pl = ca([NT], I32)
            hi1 = ca([NT, NR], BF16)
            rid = ca([NT, 2 * NR], BF16)
            ids = ca([NR])
            gid = ca([NR], U32)
            sid = ca([NR], U32)
            late = ca([NR])
            wg = ca([NR])
            wsum = cw([NT])
            wm = cw([NT])
            jk = cw([D])
            cz = cw([2, D])
            t_s3, t_ctm, t_x3, t_xt, t_hm, t_h3, t_ob, t_y = ({} for _ in range(8))
            t_c1, t_om3, t_k3, last01 = {}, {}, {}, {}

            s_d3 = sem("s_d3")
            groups3 = [list(range(a, min(a + 4, NR))) for a in range(0, NR, 4)]

            def conv(gi):
                g, s = groups[gi], gi % 2
                for t in g:
                    k = A(lambda e, t=t: e.activation(XB[:, t, :], XB[:, t, :], ACT.Identity, scale=dinv[:, t:t + 1]), t_ev[t])
                n = 128 * len(g)
                for c in range(2):
                    for j, t in enumerate(g):
                        kk = P(lambda e, c=c, j=j, t=t: e.transpose(PS[c][:, j * 128:(j + 1) * 128],
                                                                    XB[:, t, c * 128:(c + 1) * 128], ident[:, :]),
                               k, last01.get(c), sig=(j == len(g) - 1))
                    last01[c] = t_c1[(gi, c)] = A(lambda e, c=c: e.activation(CT2[:, s, c, 0:n], PS[c][:, 0:n], ACT.Identity), kk,
                                      t_ctm.get(gi - 2))
                for j, t in enumerate(g):
                    z = PS[2 + 5 * (t % 2)][:, 0:256]
                    for c in range(2):
                        kk = P(lambda e, c=c, j=j, z=z: e.matmul(z, CT2[:, s, c, j * 128:(j + 1) * 128], cWT[:, c, :],
                                                                 start=(c == 0), stop=(c == 1)), t_c1[(gi, c)], t_cw,
                               t_x3.get(t - 2), sig=(c == 1))
                    kb = V(lambda e, t=t, z=z: e.tensor_tensor(cz[:, t % 2, :], z, cbr[:, :], ALU.add), kk)
                    t_x3[t] = V(lambda e, t=t: e.scalar_tensor_tensor(X[:, t, :], cz[:, t % 2, :], 0.0, X[:, t, :], ALU.max, ALU.add))
                    ks_ = ln_stats(t)
                t_ctm[gi] = kk
                ks_ = ln_scale(g[0], g[-1] + 1, ks_)
                for t in g:
                    kh = ln_apply(t, XB[:, t, :], t_c1[(gi, 1)], ks_)
                    V(lambda e, t=t: e.tensor_tensor_reduce(out=jk, in0=XB[:, t, :], in1=wrr[:, :], scale=1.0, scalar=0.0,
                                                            op0=ALU.mult, op1=ALU.add, accum_out=wsum[:, t:t + 1]), kh)
                    k = V(lambda e, t=t: e.tensor_tensor(X[:, t, :], X[:, t, :], XB[:, t, :], ALU.add))
                full = [t for t in g if t < NT - 1]
                for (d_, m) in ((xh_d, XB), (x3_d, X)):
                    t_d3 = dma("sp", s_d3, lambda e, d_=d_, m=m: e.dma_start(
                        d_[g[0] * 128:(g[-1] + 1) * 128, :].rearrange("(t p) d -> p t d", p=128), m[:, g[0]:g[-1] + 1, :]), k)
                if full:
                    t_out = dma("sp", s_out, lambda e: e.dma_start(
                        out[full[0] * 128:(full[-1] + 1) * 128, :].rearrange("(t p) d -> p t d", p=128),
                        X[:, full[0]:full[-1] + 1, :]), k)
                if NT - 1 in g:
                    t_out = dma("sp", s_out, lambda e: e.dma_start(
                        out[(NT - 1) * 128:N, :], X[0:N - (NT - 1) * 128, NT - 1, :]), k)
                return t_d3, t_out

            def turn3(gi):
                g, s = groups3[gi], gi % 2
                n = 128 * len(g)
                for c in range(2):
                    for j, r in enumerate(g):
                        kk = P(lambda e, c=c, j=j, r=r: e.transpose(PS[c][:, j * 128:(j + 1) * 128],
                                                                    xg[:, r, c * 128:(c + 1) * 128], ident[:, :]),
                               t_xg[r], last01.get(c), sig=(j == len(g) - 1))
                    last01[c] = t_xt[(gi, c)] = A(lambda e, c=c: e.activation(XT3[:, s, c, 0:n], PS[c][:, 0:n], ACT.Identity), kk,
                                                  t_hm.get(gi - 2), t_ap[NT - 1])

            def widen(gi):
                g, s = groups3[gi], gi % 2
                n = 128 * len(g)
                for c in range(8):
                    z = PS[3 + c % 2]
                    for i in range(2):
                        k = P(lambda e, c=c, i=i, z=z: e.matmul(z[:, 0:n], f1[:, i, c * 128:(c + 1) * 128], XT3[:, s, i, 0:n],
                                                                start=(i == 0), stop=(i == 1)), t_xt[(gi, i)],
                              t_h3.get((gi, c - 2)) if c >= 2 else t_h3.get((gi - 1, 7)), sig=(i == 1))
                    t_h3[(gi, c)] = A(lambda e, c=c, z=z: e.activation(HT3[:, c, 0:n], z[:, 0:n], ACT.Gelu_apprx_tanh,
                                                                       bias=fb1c[:, c:c + 1]), k, t_om3.get(gi - 1))
                t_hm[gi] = k

            def narrow(gi):
                g = groups3[gi]
                for j, r in enumerate(g):
                    z = PS[(5, 6, 2, 7)[r % 4]][:, 0:256]
                    for c in range(8):
                        k = P(lambda e, c=c, j=j, z=z: e.matmul(z, HT3[:, c, j * 128:(j + 1) * 128], f2[:, c, :],
                                                                start=(c == 0), stop=(c == 7)), t_h3[(gi, c)],
                              t_y.get(r - 4), t_x3[NT - 1], t_x3[NT - 2], t_pick, sig=(c == 7))
                    t_y[r] = V(lambda e, r=r, z=z: e.tensor_tensor(yz[:, r % 2, :], z, fb2r[:, :], ALU.add), k)
                    kk = V(lambda e, r=r: e.scalar_tensor_tensor(x3g[:, r, :], yz[:, r % 2, :], wg[:, r:r + 1], x3g[:, r, :],
                                                                 ALU.mult, ALU.add), t_xw[r], t_x3g[r])
                    dma("pool", s_fin, lambda e, r=r: e.indirect_dma_start(
                        out, bass.IndirectOffsetOnAxis(ap=sid[:, r:r + 1], axis=0), x3g[:, r, :], None,
                        bounds_check=N - 1, oob_is_err=False), kk, t_out)
                t_om3[gi] = k

            SHIFTS = (27, 23, 19, 15, 11, 7, 3, 0)
            t_tab = G(lambda e: e.iota(tab[:, 7, :], pattern=[[1, 15]], base=1, channel_multiplier=0), t_yv[NV - 1])
            t_late = G(lambda e: e.iota(late, pattern=[[128, NR]], base=0, channel_multiplier=1,
                                        allow_small_or_imprecise_dtypes=True), t_yv[NV - 1])

            for gi in range(len(groups)):
                for t in groups[gi]:
                    apply(t)
                if gi:
                    conv(gi - 1)
            t_d3, t_out = conv(len(groups) - 1)

            V(lambda e: e.tensor_scalar(wsum, wsum, brr[:, 0:1], None, ALU.add))
            V(lambda e: e.tensor_copy(wm, wsum))
            V(lambda e: e.tensor_scalar(jk[:, 0:1], padc[:, :], -1.0, 1.0, ALU.mult, ALU.add))
            V(lambda e: e.tensor_scalar(jk[:, 1:2], padc[:, :], -3.0e38, None, ALU.mult))

            def pads_last(ap):
                return V(lambda e: e.scalar_tensor_tensor(ap[:, NT - 1:NT], ap[:, NT - 1:NT], jk[:, 0:1], jk[:, 1:2],
                                                          ALU.mult, ALU.add))

            pads_last(wm)
            for r in range(7):
                V(lambda e, r=r: e.tensor_scalar(tab[:, r, :], tab[:, 7, :], SHIFTS[r], None, ALU.logical_shift_left), t_tab)

            def total(n, k):
                return P(lambda e: e.matmul(PS[5][:, 0:n], ones[:, :], cnt3[:, 0:n], start=True, stop=True), k, t_ev[NT - 1])

            k = V(lambda e: e.tensor_scalar(vv, wm, 0.0, 0.0, ALU.is_ge, ALU.add, accum_out=cnt3[:, 0:1]))
            k = total(1, k)
            V(lambda e: e.tensor_scalar(one[:, 2:3], PS[5][:, 0:1], float(KEEP), None, ALU.is_lt), k)
            V(lambda e: e.tensor_scalar(one[:, 0:1], one[:, 2:3], -2.0, 1.0, ALU.mult, ALU.add))
            V(lambda e: e.tensor_scalar(one[:, 1:2], one[:, 2:3], float(N - 2 * KEEP + 1), float(KEEP), ALU.mult, ALU.add))
            V(lambda e: e.tensor_scalar(vv, wsum, one[:, 0:1], None, ALU.mult))
            pads_last(vv)
            V(lambda e: e.memset(thr, 0))
            for r, sh in enumerate(SHIFTS):
                n = 15 if r < 7 else 7
                V(lambda e, r=r, n=n: e.tensor_tensor(cand[:, 0:n], thr.broadcast_to([128, n]), tab[:, r, 0:n], ALU.bitwise_or),
                  t_tab)
                V(lambda e, n=n: e.tensor_tensor(cmp3[:, 0:n, :], bc(vv, 1, n), bc(cand.bitcast(F32)[:, 0:n], 2, NT), ALU.is_ge))
                k = V(lambda e, n=n: e.tensor_reduce(cnt3[:, 0:n], cmp3[:, 0:n, :], AX.X, ALU.add))
                k = total(n, k)
                V(lambda e, n=n: e.tensor_scalar(hit[:, 0:n], PS[5][:, 0:n], one[:, 1:2], 0.0, ALU.is_ge, ALU.add,
                                                 accum_out=one[:, 3:4]), k)
                V(lambda e: e.tensor_copy(cand[:, 0:1], one[:, 3:4]))
                V(lambda e, sh=sh: e.tensor_scalar(cand[:, 0:1], cand[:, 0:1], sh, None, ALU.logical_shift_left))
                V(lambda e: e.tensor_tensor(thr, thr, cand[:, 0:1], ALU.bitwise_or))
            V(lambda e: e.tensor_tensor(one[:, 4:5], thr.bitcast(F32), one[:, 0:1], ALU.mult))
            V(lambda e: e.tensor_scalar(two[:, 0:NT], wm, one[:, 4:5], None, ALU.is_gt))
            k = V(lambda e: e.tensor_scalar(two[:, NT:2 * NT], wm, one[:, 4:5], None, ALU.is_equal))
            P(lambda e: e.matmul(PS[5][:, 0:2 * NT], tri[:, :], two, start=True, stop=True), k)
            k = P(lambda e: e.matmul(PS[6][:, 0:2 * NT], ones[:, :], two, start=True, stop=True))
            for i in range(2):
                V(lambda e, i=i: e.tensor_tensor_scan(inc3[:, i, :], ones[:, 0:NT], PS[6][:, i * NT:(i + 1) * NT], 0.0,
                                                      ALU.mult, ALU.add), k)
            p3 = pos3.rearrange("p a b -> p (a b)")
            V(lambda e: e.tensor_tensor(p3, inc3.rearrange("p a b -> p (a b)"), PS[6][:, 0:2 * NT], ALU.subtract))
            V(lambda e: e.tensor_tensor(p3, p3, PS[5][:, 0:2 * NT], ALU.add))
            V(lambda e: e.tensor_scalar(one[:, 5:6], inc3[:, 0, NT - 1:NT], -1.0, float(KEEP), ALU.mult, ALU.add))
            V(lambda e: e.scalar_tensor_tensor(keepm, pos3[:, 1, :], one[:, 5:6], two[:, NT:2 * NT], ALU.is_lt, ALU.mult))
            V(lambda e: e.tensor_tensor(keepm, keepm, two[:, 0:NT], ALU.add))
            V(lambda e: e.scalar_tensor_tensor(vv, pos3[:, 1, :], one[:, 5:6], pos3[:, 0, :], ALU.min, ALU.add))
            V(lambda e: e.scalar_tensor_tensor(vv, keepm, -4096.0, vv, ALU.mult, ALU.add))
            V(lambda e: e.tensor_scalar(posi, vv, 4096.0, None, ALU.add))
            V(lambda e: e.memset(rlo, 0.0))
            V(lambda e: e.tensor_scalar(pl, posi, 127, None, ALU.bitwise_and))
            V(lambda e: e.tensor_copy(rlo[:, 0:NT], pl))
            V(lambda e: e.tensor_scalar(rhi, posi, 7, None, ALU.logical_shift_right))
            for c in range(4):
                V(lambda e, c=c: e.tensor_tensor(ohr[:, c, :, :], iob8[:, :, :], bc(rlo[:, 8 * c:8 * c + 8], 1, 128), ALU.is_equal),
                  chain=(c == 0))
            V(lambda e: e.tensor_tensor(hi1, bc(rhi, 2, NR), bc(io16[:, 0:NR], 1, NT), ALU.is_equal))
            V(lambda e: e.tensor_scalar(rid[:, :, 0:NR], hi1, iop[:, 0:1], None, ALU.mult))
            k = V(lambda e: e.tensor_tensor(rid[:, :, NR:2 * NR], hi1, bc(iob25[:, :], 2, NR), ALU.mult))
            for t in range(NT):
                kp = P(lambda e, t=t: e.matmul(PS[2][:, 0:2 * NR], ohr[:, t // 8, :, t % 8], rid[:, t, :], start=(t == 0),
                                               stop=(t == NT - 1)), k, t_x3[NT - 1], t_x3[NT - 2], sig=(t == NT - 1))
            V(lambda e: e.tensor_copy(ids, PS[2][:, 0:NR]), kp)
            V(lambda e: e.scalar_tensor_tensor(ids, PS[2][:, NR:2 * NR], 128.0, ids, ALU.mult, ALU.add))
            t_gid = V(lambda e: e.tensor_copy(gid, ids))
            V(lambda e: e.tensor_scalar(late, late, float(KEEP), 100000.0, ALU.is_ge, ALU.mult), t_late)
            t_pick = V(lambda e: e.tensor_tensor(sid, ids, late, ALU.add))

            t_xg, t_x3g, t_xw = {}, {}, {}
            s_xg = [sem(f"s_xg{r}") for r in range(NR)]
            s_x3g = [sem(f"s_x3g{r}") for r in range(NR)]
            s_fin = sem("s_fin")

            def pull(r, into, frm, s_):
                return dma("pool", s_[r], lambda e: e.indirect_dma_start(
                    into[:, r, :], None, frm, bass.IndirectOffsetOnAxis(ap=gid[:, r:r + 1], axis=0)), t_gid, t_d3, t_ap[NT - 1])

            for r in range(NR):
                t_xg[r] = pull(r, xg, xh_d, s_xg)
            for r in range(NR):
                t_x3g[r] = pull(r, x3g, x3_d, s_x3g)
            for r in range(NR):
                V(lambda e, r=r: e.tensor_tensor_reduce(out=jk, in0=xg[:, r, :], in1=wrr[:, :], scale=1.0, scalar=0.0,
                                                        op0=ALU.mult, op1=ALU.add, accum_out=wg[:, r:r + 1]), t_xg[r])
                t_xw[r] = V(lambda e, r=r: e.tensor_scalar(wg[:, r:r + 1], wg[:, r:r + 1], brr[:, 0:1], None, ALU.add))
            turn3(0)
            for gi in range(len(groups3)):
                widen(gi)
                if gi + 1 < len(groups3):
                    turn3(gi + 1)
                narrow(gi)

        io64f = sb("io64f", [128, NS])
        stages_after()

        block = ctx.enter_context(nc.Block())

        @block.sync
        def _(e):
            q.run("sp", e)
            for t in q.landed():
                e.wait_ge(t.sem, t.val)

        @block.gpsimd
        def _(e):
            q.run("pool", e)

        @block.scalar
        def _(e):
            q.run("act", e)

        @block.vector
        def _(e):
            q.run("dve", e)

        @block.tensor
        def _(e):
            q.run("pe", e)


_INS = ["x", "src", "dst", "edge_attr_64", "L0_gnn_W1", "L0_gnn_b1", "L0_gnn_W2", "L0_gnn_b2", "L0_ffn_gate_w",
        "L0_ffn_gate_b", "L0_ffn_w1", "L0_ffn_w2", "L0_ffn_w3", "L1_gnn_W", "L1_gnn_b", "L1_ffn_attention_mask",
        "L1_ffn_wr", "L1_ffn_br", "L1_ffn_w1", "L1_ffn_b1", "L1_ffn_w2", "L1_ffn_b2"]
_OUTS = [((3125, 256), "float32")]


def kernel(**inputs):
    import numpy as _np
    import concourse.bacc as _bacc
    from concourse import mybir as _mybir
    from concourse.bass_utils import run_bass_kernel_spmd as _run

    nc = _bacc.Bacc("TRN2", target_bir_lowering=False, num_devices=1)
    arrays, args = {}, []
    for name in _INS:
        a = _np.ascontiguousarray(inputs[name])
        arrays[f"in_{name}_dram"] = a
        args.append(nc.dram_tensor(f"in_{name}_dram", a.shape, _mybir.dt.from_np(a.dtype), kind="ExternalInput").ap())
    for i, (shape, dtype) in enumerate(_OUTS):
        args.append(nc.dram_tensor(f"out_{i}_dram", shape, _mybir.dt.from_np(_np.dtype(dtype)), kind="ExternalOutput").ap())
    program(nc, *args)
    r = _run(nc, [arrays], core_ids=[0])
    return r.results[0]["out_0_dram"]
```
